# Optimizing a Trainium2 kernel written in Bass

```python
import numpy as np
import jax
import jax.numpy as jnp

def _softmax(x, axis=-1):
    return jax.nn.softmax(x, axis=axis)

def _gelu(x):
    return jax.nn.gelu(x, approximate=True)

def _silu(x):
    return jax.nn.silu(x)

def _sigmoid(x):
    return jax.nn.sigmoid(x)

def _layernorm(x, axis=-1, eps=1e-05):
    m = jnp.mean(x, axis=axis, keepdims=True)
    v = jnp.var(x, axis=axis, keepdims=True)
    return (x - m) / jnp.sqrt(v + eps)

def _scatter_add(tgt, idx, src, axis=0):
    return tgt.at[idx].add(src)

def _segment_sum(src, seg, n):
    return jax.ops.segment_sum(src, seg, n)
kernel_name = 'mk_audio_tower_d1_tok_audfeat1024_r4_a3ce44'

def setup_inputs(seed: int=0):
    np.random.seed(seed)
    _w = jnp.asarray

    def _rec_inputs():
        import jax
        import jax.numpy as jnp
        _rk = jax.random.key(seed)
        x = -0.000520686 + 1.00062 * jax.random.normal(jax.random.fold_in(_rk, 1), (64, 2, 4096), jnp.float32)
        return x
    x = _rec_inputs()

    def _L0_tok_setup():
        import jax, jax.numpy as jnp
        import numpy as np
        DS_RATE = 16
        key = jax.random.key(seed)
        ks = jax.random.split(key, 5)
        B, Cin, L = (64, 2, 4096)
        C_mid = 32
        embed_dim = 128
        X = jax.random.normal(ks[0], (B, Cin, L), dtype=jnp.float32)
        W_embed = jax.random.normal(ks[1], (C_mid, Cin, 7), dtype=jnp.float32) * 0.1
        b_embed = jax.random.normal(ks[2], (C_mid,), dtype=jnp.float32) * 0.1
        W_proj = jax.random.normal(ks[3], (embed_dim, C_mid * DS_RATE, 1), dtype=jnp.float32) * 0.05
        b_proj = jax.random.normal(ks[4], (embed_dim,), dtype=jnp.float32) * 0.05
        return {'X': X, 'W_embed': W_embed, 'b_embed': b_embed, 'W_proj': W_proj, 'b_proj': b_proj}
    _L0_tok_all = _L0_tok_setup()
    _L0_tok_in = {k: v for k, v in _L0_tok_all.items() if k in ('W_embed', 'b_embed', 'W_proj', 'b_proj')}
    del _L0_tok_all

    def _L0_attn_setup():
        import jax, jax.numpy as jnp
        import numpy as np
        BATCH, SEQ = (2, 512)
        D_MODEL, D_STATE, D_CONV, EXPAND = (256, 16, 4, 2)
        D_INNER = EXPAND * D_MODEL

        def _selective_scan(xc, delta, A, Bm, Cm):
            dA = jnp.exp(delta[..., None] * A)
            dBx = delta[..., None] * Bm[:, :, None, :] * xc[..., None]
            h0 = jnp.zeros((xc.shape[0], xc.shape[2], A.shape[1]), xc.dtype)

            def step(h, inp):
                dA_t, dBx_t, c_t = inp
                h = dA_t * h + dBx_t
                y = jnp.einsum('bdn,bn->bd', h, c_t)
                return (h, y)
            _, ys = jax.lax.scan(step, h0, (dA.swapaxes(0, 1), dBx.swapaxes(0, 1), Cm.swapaxes(0, 1)))
            return ys.swapaxes(0, 1)

        def _forward(x, W_in, conv_w, conv_b, W_xproj, w_dt, b_dt, A_log, D_param, W_out):
            xz = x @ W_in
            x_inner, z = jnp.split(xz, 2, axis=-1)
            xc = jax.lax.conv_general_dilated(x_inner.swapaxes(1, 2), conv_w, window_strides=(1,), padding=[(D_CONV - 1, 0)], dimension_numbers=('NCH', 'OIH', 'NCH'), feature_group_count=D_INNER) + conv_b[None, :, None]
            xc = jax.nn.silu(xc.swapaxes(1, 2))
            x_ssm = xc @ W_xproj
            delta_raw = x_ssm[..., :1]
            Bm = x_ssm[..., 1:1 + D_STATE]
            Cm = x_ssm[..., 1 + D_STATE:]
            delta = jax.nn.softplus(delta_raw * w_dt + b_dt)
            A = -jnp.exp(A_log)
            y = _selective_scan(xc, delta, A, Bm, Cm)
            y = y + xc * D_param
            y = y * jax.nn.silu(z)
            return y @ W_out
        key = jax.random.key(seed)
        ks = jax.random.split(key, 8)
        x = jax.random.normal(ks[0], (BATCH, SEQ, D_MODEL), jnp.float32)
        W_in = jax.random.normal(ks[1], (D_MODEL, 2 * D_INNER), jnp.float32) * D_MODEL ** (-0.5)
        conv_w = jax.random.normal(ks[2], (D_INNER, 1, D_CONV), jnp.float32) * D_CONV ** (-0.5)
        conv_b = jnp.zeros((D_INNER,), jnp.float32)
        W_xproj = jax.random.normal(ks[3], (D_INNER, 2 * D_STATE + 1), jnp.float32) * D_INNER ** (-0.5)
        w_dt = jax.random.normal(ks[4], (D_INNER,), jnp.float32)
        b_dt = jnp.zeros((D_INNER,), jnp.float32)
        A_log = jnp.log(jnp.tile(jnp.arange(1, D_STATE + 1, dtype=jnp.float32), (D_INNER, 1)))
        D_param = jnp.ones((D_INNER,), jnp.float32)
        W_out = jax.random.normal(ks[5], (D_INNER, D_MODEL), jnp.float32) * D_INNER ** (-0.5)
        return dict(x=x, W_in=W_in, conv_w=conv_w, conv_b=conv_b, W_xproj=W_xproj, w_dt=w_dt, b_dt=b_dt, A_log=A_log, D_param=D_param, W_out=W_out)
    _L0_attn_all = _L0_attn_setup()
    _L0_attn_in = {k: v for k, v in _L0_attn_all.items() if k in ('W_in', 'conv_w', 'conv_b', 'W_xproj', 'w_dt', 'b_dt', 'A_log', 'D_param', 'W_out')}
    del _L0_attn_all

    def _L0_ffn_setup():
        import jax, jax.numpy as jnp
        import numpy as np
        N_EXPERTS = 8
        TOP_K = 2
        key = jax.random.key(seed)
        ks = jax.random.split(key, 5)
        B, T, C, H, E = (4, 512, 256, 512, N_EXPERTS)
        scale = 0.02
        return {'x': jax.random.normal(ks[0], (B, T, C), dtype=jnp.float32), 'w_gate': jax.random.normal(ks[1], (C, E), dtype=jnp.float32) * scale, 'wi': jax.random.normal(ks[2], (E, C, H), dtype=jnp.float32) * scale, 'wg': jax.random.normal(ks[3], (E, C, H), dtype=jnp.float32) * scale, 'wo': jax.random.normal(ks[4], (E, H, C), dtype=jnp.float32) * scale}
    _L0_ffn_all = _L0_ffn_setup()
    _L0_ffn_in = {k: v for k, v in _L0_ffn_all.items() if k in ('w_gate', 'wi', 'wg', 'wo')}
    del _L0_ffn_all
    return {'x': x, 'L0_tok_W_embed': _L0_tok_in['W_embed'], 'L0_tok_b_embed': _L0_tok_in['b_embed'], 'L0_tok_W_proj': _L0_tok_in['W_proj'], 'L0_tok_b_proj': _L0_tok_in['b_proj'], 'L0_attn_W_in': _L0_attn_in['W_in'], 'L0_attn_conv_w': _L0_attn_in['conv_w'], 'L0_attn_conv_b': _L0_attn_in['conv_b'], 'L0_attn_W_xproj': _L0_attn_in['W_xproj'], 'L0_attn_w_dt': _L0_attn_in['w_dt'], 'L0_attn_b_dt': _L0_attn_in['b_dt'], 'L0_attn_A_log': _L0_attn_in['A_log'], 'L0_attn_D_param': _L0_attn_in['D_param'], 'L0_attn_W_out': _L0_attn_in['W_out'], 'L0_ffn_w_gate': _L0_ffn_in['w_gate'], 'L0_ffn_wi': _L0_ffn_in['wi'], 'L0_ffn_wg': _L0_ffn_in['wg'], 'L0_ffn_wo': _L0_ffn_in['wo']}

def reference(x, L0_tok_W_embed, L0_tok_b_embed, L0_tok_W_proj, L0_tok_b_proj, L0_attn_W_in, L0_attn_conv_w, L0_attn_conv_b, L0_attn_W_xproj, L0_attn_w_dt, L0_attn_b_dt, L0_attn_A_log, L0_attn_D_param, L0_attn_W_out, L0_ffn_w_gate, L0_ffn_wi, L0_ffn_wg, L0_ffn_wo):
    import jax
    import jax.numpy as jnp

    def _L0_tok_ref(X, W_embed, b_embed, W_proj, b_proj):
        import jax, jax.numpy as jnp
        import numpy as np
        DS_RATE = 16
        ds = DS_RATE
        h = jax.lax.conv_general_dilated(X, W_embed, window_strides=(1,), padding=((3, 3),), dimension_numbers=('NCH', 'OIH', 'NCH'))
        h = h + b_embed[None, :, None]
        B, C, L = h.shape
        Ld = L // ds
        h = h.reshape(B, C, Ld, ds).transpose(0, 3, 1, 2).reshape(B, ds * C, Ld)
        out = jnp.einsum('oc,bcl->bol', W_proj[:, :, 0], h) + b_proj[None, :, None]
        return out

    def _L0_attn_ref(x, W_in, conv_w, conv_b, W_xproj, w_dt, b_dt, A_log, D_param, W_out):
        import jax, jax.numpy as jnp
        import numpy as np
        BATCH, SEQ = (2, 512)
        D_MODEL, D_STATE, D_CONV, EXPAND = (256, 16, 4, 2)
        D_INNER = EXPAND * D_MODEL

        def _selective_scan(xc, delta, A, Bm, Cm):
            dA = jnp.exp(delta[..., None] * A)
            dBx = delta[..., None] * Bm[:, :, None, :] * xc[..., None]
            h0 = jnp.zeros((xc.shape[0], xc.shape[2], A.shape[1]), xc.dtype)

            def step(h, inp):
                dA_t, dBx_t, c_t = inp
                h = dA_t * h + dBx_t
                y = jnp.einsum('bdn,bn->bd', h, c_t)
                return (h, y)
            _, ys = jax.lax.scan(step, h0, (dA.swapaxes(0, 1), dBx.swapaxes(0, 1), Cm.swapaxes(0, 1)))
            return ys.swapaxes(0, 1)

        def _forward(x, W_in, conv_w, conv_b, W_xproj, w_dt, b_dt, A_log, D_param, W_out):
            xz = x @ W_in
            x_inner, z = jnp.split(xz, 2, axis=-1)
            xc = jax.lax.conv_general_dilated(x_inner.swapaxes(1, 2), conv_w, window_strides=(1,), padding=[(D_CONV - 1, 0)], dimension_numbers=('NCH', 'OIH', 'NCH'), feature_group_count=D_INNER) + conv_b[None, :, None]
            xc = jax.nn.silu(xc.swapaxes(1, 2))
            x_ssm = xc @ W_xproj
            delta_raw = x_ssm[..., :1]
            Bm = x_ssm[..., 1:1 + D_STATE]
            Cm = x_ssm[..., 1 + D_STATE:]
            delta = jax.nn.softplus(delta_raw * w_dt + b_dt)
            A = -jnp.exp(A_log)
            y = _selective_scan(xc, delta, A, Bm, Cm)
            y = y + xc * D_param
            y = y * jax.nn.silu(z)
            return y @ W_out
        return _forward(x, W_in, conv_w, conv_b, W_xproj, w_dt, b_dt, A_log, D_param, W_out)

    def _L0_ffn_ref(x, w_gate, wi, wg, wo):
        import jax, jax.numpy as jnp
        import numpy as np
        N_EXPERTS = 8
        TOP_K = 2
        B, T, C = x.shape
        E = w_gate.shape[-1]
        logits = jnp.einsum('btc,ce->bte', x, w_gate)
        gates = jax.nn.softmax(logits, axis=-1)
        topk_vals, topk_idx = jax.lax.top_k(gates, TOP_K)
        onehot = jax.nn.one_hot(topk_idx, E, dtype=x.dtype)
        combine = jnp.einsum('btk,btke->bte', topk_vals, onehot)
        x_flat = x.reshape(B * T, C)
        combine_flat = combine.reshape(B * T, E)
        out = jnp.zeros_like(x_flat)
        for e in range(E):
            up = x_flat @ wi[e]
            gate = x_flat @ wg[e]
            y = jax.nn.silu(gate) * up @ wo[e]
            out = out + combine_flat[:, e:e + 1] * y
        return out.reshape(B, T, C)
    h = _L0_tok_ref(x, L0_tok_W_embed, L0_tok_b_embed, L0_tok_W_proj, L0_tok_b_proj)
    h = h + _L0_attn_ref(_layernorm(h, axis=-1), L0_attn_W_in, L0_attn_conv_w, L0_attn_conv_b, L0_attn_W_xproj, L0_attn_w_dt, L0_attn_b_dt, L0_attn_A_log, L0_attn_D_param, L0_attn_W_out)
    h = h + _L0_ffn_ref(_layernorm(h, axis=-1), L0_ffn_w_gate, L0_ffn_wi, L0_ffn_wg, L0_ffn_wo)
    return h

_drawn_inputs = setup_inputs


def setup_inputs(seed=0):
    import zlib

    import numpy as np

    out = dict(_drawn_inputs(seed))
    spreads = {'L0_attn_conv_b': (0.0, 0.1), 'L0_attn_b_dt': (0.0, 0.1), 'L0_attn_D_param': (1.0, 0.2)}
    factors = {'L0_ffn_w_gate': 8.0,
     'L0_ffn_wi': 7.259,
     'L0_ffn_wg': 7.345,
     'L0_ffn_wo': 7.248,
     'L0_tok_b_embed': 4.922,
     'L0_tok_b_proj': 8.0}
    for name, (base, spread) in spreads.items():
        noise = np.random.default_rng([zlib.crc32(name.encode()), seed]).standard_normal(out[name].shape)
        drawn = base * np.exp(spread * noise) if base else spread * noise
        out[name] = jnp.asarray(drawn.astype(out[name].dtype))
    for name, factor in factors.items():
        out[name] = (out[name] * factor).astype(out[name].dtype)
    return out
```

```python
from contextlib import ExitStack

import concourse.bass as bass
from concourse import mybir

ALU = mybir.AluOpType
ACT = mybir.ActivationFunctionType
AX_X = mybir.AxisListType.X
F32 = mybir.dt.float32
BF16 = mybir.dt.bfloat16
I32 = mybir.dt.int32
U32 = mybir.dt.uint32

P = 128


def audio_tower(nc, x, W_embed, b_embed, W_proj, b_proj, W_in, conv_w, conv_b, W_xproj, w_dt, b_dt, A_log,
                D_param, W_out, w_gate, wi, wg, wo, out):
    B, CI, L = x.shape
    CM, _, KW = W_embed.shape
    PAD = KW // 2
    T = W_proj.shape[0]
    DS = W_proj.shape[1] // CM
    C = L // DS
    WIN = DS + KW - 1
    KX = CI * WIN + 1
    DI = W_out.shape[0]
    NCH = DI // P
    NK = C // P
    S = A_log.shape[1]
    TAPS = conv_w.shape[2]
    R = 2 * S + 1
    E = w_gate.shape[1]
    H = wi.shape[2]
    NH = H // P
    GB = 4
    GT = GB * T
    G = B // GB
    NJ = DS * CM // P
    SPC = P // CM
    EPS = 1e-5
    ROW = C + 2
    TOKENS = B * T
    REG = TOKENS + P
    NT = -(-(2 * TOKENS // P + E - 1) // 4) * 4
    MW = 2 * NK * H + NH * C
    assert T == P and GT == 512 and C == 256 and NCH == 4 and G % 2 == 0 and S == 16 and H == 512

    rows_dram = nc.dram_tensor("expert_rows", [E * REG + P, ROW], F32).ap()

    with ExitStack() as ctx:
        def sb(name, shape, dt=F32):
            return ctx.enter_context(nc.sbuf_tensor(name, shape, dt))

        def sem(name):
            return ctx.enter_context(nc.semaphore(name))

        ident = sb("ident", [P, P])
        w_in_sb = sb("w_in_sb", [P, NK, 2 * DI])
        w_out_sb = sb("w_out_sb", [P, NCH, C])
        w_x3 = sb("w_x3", [P, NCH, 3 * R])
        w_gate_sb = sb("w_gate_sb", [P, NK, E])
        diag_d = sb("diag_d", [P, NCH, P])
        select = sb("select", [3 * R, R, P], BF16)
        w_eff = sb("w_eff", [KX, T])
        a_neg = sb("a_neg", [P, NCH, S])
        cw = sb("cw", [P, NCH, TAPS])
        cb = sb("cb", [P, NCH])
        wdt = sb("wdt", [P, NCH])
        bdt = sb("bdt", [P, NCH])
        dpar = sb("dpar", [P, NCH])
        below = sb("below", [P, P], BF16)
        ones_bf = sb("ones_bf", [P, P], BF16)
        key_w = sb("key_w", [P, GB, E])
        half = sb("half", [P, GB])
        ones_c = sb("ones_c", [P, 1])
        counts = sb("counts", [P, E])
        tokf = sb("tokf", [P, GB])
        SCN = NCH * GT
        arena = sb("arena", [P, E * MW])
        parts = {}
        at = 0
        for name, n in (("dA0", SCN), ("dA1", SCN), ("dBx0", SCN), ("dBx1", SCN), ("hc0", SCN), ("hc1", SCN),
                        ("state", SCN), ("delta0", SCN), ("delta1", SCN), ("u0", SCN), ("u1", SCN), ("xc", SCN)):
            parts[name] = arena[:, at:at + n].rearrange("p (c t) -> p c t", c=NCH)
            at += n
        assert at == E * MW
        dA = [parts["dA0"], parts["dA1"]]
        dBx = [parts["dBx0"], parts["dBx1"]]
        hc = [parts["hc0"], parts["hc1"]]
        state, xc = parts["state"], parts["xc"]
        delta = [parts["delta0"], parts["delta1"]]
        u = [parts["u0"], parts["u1"]]
        w_moe = arena[:, :].rearrange("p (e m) -> p e m", e=E)

        def flat(ap):
            return ap.rearrange("p c t -> p (c t)")

        z = [sb(f"z{i}", [P, NCH, GT]) for i in range(2)]
        hres = [sb(f"hres{i}", [P, GB, C]) for i in range(2)]
        bc3 = [sb(f"bc3_{i}", [3 * R, GT], BF16) for i in range(2)]
        b_rep = [sb(f"b_rep{i}", [P, GT]) for i in range(2)]
        xw = [sb(f"xw{i}", [P, GB, NK, KX]) for i in range(2)]
        xn = sb("xn", [P, GB, C])
        xnt = sb("xnt", [P, NK, GT])
        xt = xnt[0:KX, :, :].rearrange("p k t -> p (k t)")
        tap = [[sb(f"tap{i}_{k}", [P, GB, T]) for k in range(TAPS)] for i in range(2)]
        soft = sb("soft", [P, NCH, GT])
        split = sb("split", [2 * R, GT])
        yz = soft
        h2 = sb("h2", [P, GB, C])
        row = [sb(f"row{i}", [P, GB, ROW]) for i in range(2)]
        xn2t = xn[:, :, :].rearrange("p (k b) c -> p k (b c)", k=NK)
        stat = sb("stat", [P, 2, GB, 6])
        mv = sb("mv", [P, 2, GB, 2])
        rstd = sb("rstd", [P, 2, GB])
        lmax = sb("lmax", [P, GB])
        ex = sb("ex", [P, GB, E])
        esum = sb("esum", [P, GB])
        einv = sb("einv", [P, GB])
        gates = sb("gates", [P, GB, E])
        g2 = sb("g2", [P, GB, E])
        m1 = sb("m1", [P, 2, GB])
        eq = sb("eq", [P, GB, E])
        key = sb("key", [P, GB, E])
        kmax = sb("kmax", [P, GB])
        oh = [sb(f"oh{i}", [P, GB, E]) for i in range(2)]
        mask = sb("mask", [P, GB, E], BF16)
        pos = sb("pos", [P, GB, E])
        slot_f = sb("slot_f", [P, 2, GB])
        slot = sb("slot", [P, 2, GB], U32)
        band = z[0][:, 0, 0:NJ * KX].rearrange("p (j k) -> p j k", j=NJ)
        wp_sb = z[1][:, 0, :]
        wpt = z[1][:, 1, :].rearrange("p (j t) -> p j t", j=NJ)
        e_last = z[0][0:1, 1, 0:KX]
        bp_row = z[0][0:1, 2, 0:T]

        ne = sb("ne", [1, E])
        ebase = sb("ebase", [P, E])
        jlim = sb("jlim", [1, TOKENS // P])
        tile_no = sb("tile_no", [1, NT])
        cmp1 = z[0][0:1, 0, 0:E * (TOKENS // P)].rearrange("p (e j) -> p e j", e=E)
        cmp2 = z[0][0:1, :, :].rearrange("p c t -> p (c t)")[:, 0:NT * E].rearrange("p (i e) -> p i e", e=E)
        cmp3 = z[1][0:1, :, :].rearrange("p c t -> p (c t)")[:, 0:NT * E].rearrange("p (i e) -> p i e", e=E)
        nt = sb("nt", [1, E])
        ones_e = sb("ones_e", [1, E])
        tend = sb("tend", [1, E])
        e_of, t_of, r_of, b_of = (hres[1][0:1, i, 0:NT] for i in range(4))
        tab = sb("tab", [1, 2, NT + 4], I32)
        pad_idx_f = sb("pad_idx_f", [P, E])
        pad_idx = sb("pad_idx", [P, E], U32)
        pad_row = sb("pad_row", [P, ROW])
        iota_p = sb("iota_p", [P, 1])
        XB = 4
        xg = [tap[i % 2][i // 2 * 2][:, :, :].rearrange("p b t -> p (b t)")[:, 0:ROW] for i in range(XB)]
        xgt = [xnt[:, i, 0:C] for i in range(2)]
        sg = [xn2t[:, i, :] for i in range(2)]
        act = [z[1][:, 2 + i, :] for i in range(2)]
        actt = [z[1][:, i, :] for i in range(2)]
        yt = [hres[0][:, i, :] for i in range(2)]
        tok_id = [sb(f"tok_id{i}", [P, 1], U32) for i in range(XB)]
        tok_w = [sb(f"tok_w{i}", [P, 1]) for i in range(XB)]

        psum = ctx.enter_context(nc.psum_tensor("psum", [P, 8, 512], F32))
        yacc = psum[:, 0:NCH, :]
        b_ps, c_ps = psum[:, 4, :], psum[:, 5, :]
        bank_a, bank_b = psum[:, 6, :], psum[:, 7, :]
        pg = [psum[:, 0, :], psum[:, 1, :]]
        pu = [psum[:, 2, :], psum[:, 3, :]]
        py = [psum[:, 4, 0:C], psum[:, 5, 0:C]]
        px, pt = psum[:, 6, :], psum[:, 7, :]

        s_par = sem("s_par")
        s_wts = sem("s_wts")
        s_band0 = sem("s_band0")
        s_const = sem("s_const")
        s_ctmp = sem("s_ctmp")
        s_zero = sem("s_zero")
        s_set = sem("s_set")
        s_aexp = sem("s_aexp")
        s_wpt = sem("s_wpt")
        s_wptc = sem("s_wptc")
        s_weff = sem("s_weff")
        s_weffc = sem("s_weffc")
        x_loaded = [sem(f"x_loaded{i}") for i in range(2)]
        a_full = sem("a_full")
        a_free = sem("a_free")
        stat_step = [sem(f"stat_step{i}") for i in range(2)]
        stat1 = sem("stat1")
        pow1 = sem("pow1")
        xn_ready = sem("xn_ready")
        conv_part = sem("conv_part")
        conv_ready = sem("conv_ready")
        xc_ready = sem("xc_ready")
        z_ready = sem("z_ready")
        hi_ready = sem("hi_ready")
        rest_ready = sem("rest_ready")
        mid_ready = sem("mid_ready")
        bc_ready = sem("bc_ready")
        sexp_ready = sem("sexp_ready")
        ln_ready = sem("ln_ready")
        delta_ready = sem("delta_ready")
        u_ready = sem("u_ready")
        b_full = sem("b_full")
        b_copied = sem("b_copied")
        c_full = sem("c_full")
        dA_ready = sem("dA_ready")
        dbx_dve = sem("dbx_dve")
        dbx_pool = sem("dbx_pool")
        scan_done = sem("scan_done")
        hc_ready = sem("hc_ready")
        skip_done = sem("skip_done")
        sum_done = sem("sum_done")
        yz_ready = sem("yz_ready")
        o_full = sem("o_full")
        h2_ready = sem("h2_ready")
        h2_stored = sem("h2_stored")
        stat2 = sem("stat2")
        pow2 = sem("pow2")
        row_ready = sem("row_ready")
        t_full = sem("t_full")
        xn2t_ready = sem("xn2t_ready")
        l_full = sem("l_full")
        lsub_ready = sem("lsub_ready")
        lexp_ready = sem("lexp_ready")
        mask_ready = sem("mask_ready")
        n_full = sem("n_full")
        slot_ready = sem("slot_ready")
        scattered = sem("scattered")
        rows_left = sem("rows_left")
        dv = sem("dv")
        w_loaded = sem("w_loaded")
        tab_ready = sem("tab_ready")
        pad_ready = sem("pad_ready")
        padded = sem("padded")
        tile_loaded = [sem(f"tile_loaded{i}") for i in range(XB)]
        xg_turned = sem("xg_turned")
        xgt_ready = sem("xgt_ready")
        meta_ready = sem("meta_ready")
        gate_full = sem("gate_full")
        up_full = sem("up_full")
        silu_ready = sem("silu_ready")
        act_ready = sem("act_ready")
        at_full = sem("at_full")
        actt_ready = sem("actt_ready")
        y_full = sem("y_full")
        y_ready = sem("y_ready")
        added = sem("added")

        N_PAR = 2 + DS + SPC + 6
        N_WTS = 6
        X_PER = 16 * 4 * GB
        ROUTER = 26
        UA = 16
        FA = UA - 1
        HS = S // 2

        def gn(g, n):
            return (g + 1, n - S) if n >= S else (g, n)

        def ahead(eng, s, value):
            if not (isinstance(value, int) and value <= 0):
                eng.wait_ge(s, value)

        passed = {name: sem(f"passed_{name}") for name in ("pe", "dve", "pool")}

        def apart(eng, name):
            eng.sem_inc(passed[name], 1)

        block = ctx.enter_context(nc.Block())

        @block.sync
        def _(sp):
            sp.sem_inc(h2_stored, 16)
            sp.sem_inc(rows_left, 1)
            sp.dma_start(wp_sb, W_proj.rearrange("o c a -> o (c a)")).then_inc(s_par, 16)
            sp.dma_start(bp_row, b_proj.rearrange("(a o) -> a o", a=1)).then_inc(s_par, 16)
            sp.wait_ge(s_band0, 2)
            for s in range(DS):
                j, q = s // SPC, s % SPC
                dst = band[q * CM:(q + 1) * CM, j, 0:CI * WIN].rearrange("p (c w) -> p c w", c=CI)[:, :, s:s + KW]
                sp.dma_start(dst, W_embed).then_inc(s_par, 16)
            for q in range(SPC):
                sp.dma_start(band[q * CM:(q + 1) * CM, :, KX - 1:KX],
                             b_embed.rearrange("(c a b) -> c a b", a=1, b=1).broadcast_to([CM, NJ, 1]),
                             allow_slow_non_contiguous=True)\
                    .then_inc(s_par, 16)

            def load_x(g, par):
                ahead(sp, a_full, UA * (g - 2) + 2)

                for b in range(GB):
                    def win(first_row, rows_, cut, width):
                        at0 = first_row * DS - PAD + cut
                        src = x[bass.ds(g * GB + b, 1), :, at0:at0 + width]
                        return bass.AP(tensor=src.tensor, offset=src.offset,
                                       ap=[[DS, rows_], [L, CI], [1, width]])

                    def cell(k, p0, p1, cut, width):
                        return xw[par][p0:p1, b, k, 0:CI * WIN].rearrange("p (c w) -> p c w", c=CI)[:, :, cut:cut + width]

                    sp.dma_start(cell(0, 1, P, 0, WIN), win(1, P - 1, 0, WIN)).then_inc(x_loaded[par], 16)
                    sp.dma_start(cell(0, 0, 1, PAD, WIN - PAD), win(0, 1, PAD, WIN - PAD)).then_inc(x_loaded[par], 16)
                    sp.dma_start(cell(1, 0, P - 1, 0, WIN), win(P, P - 1, 0, WIN)).then_inc(x_loaded[par], 16)
                    sp.dma_start(cell(1, P - 1, P, 0, WIN - PAD), win(2 * P - 1, 1, 0, WIN - PAD))\
                        .then_inc(x_loaded[par], 16)

            def store_h2(g):
                sp.wait_ge(h2_ready, 2 * g + 2)
                sp.dma_start(out[bass.ds(g * GB, GB), :, :].rearrange("b o l -> o b l"), h2[:, :, :])\
                    .then_inc(h2_stored, 16)

            sp.wait_ge(s_zero, 1)
            load_x(0, 0)
            sp.dma_start(w_in_sb[:, :, :], W_in.rearrange("(k p) n -> p k n", p=P)).then_inc(s_wts, 16)
            load_x(1, 1)

            def step(g, par, first, last):
                if not last:
                    load_x(g + 2, par)
                if not first:
                    store_h2(g - 1)

            step(0, 0, True, False)
            with sp.Fori(1, G - 3, 2) as g:
                step(g, 1, False, False)
                step(g + 1, 0, False, False)
            step(G - 3, 1, False, False)
            step(G - 2, 0, False, True)
            step(G - 1, 1, False, True)

            sp.wait_ge(sum_done, S * G)
            for e in range(E):
                gate_w = w_moe[:, e, 0:NK * H].rearrange("p (k h) -> p k h", k=NK)
                up_w = w_moe[:, e, NK * H:2 * NK * H].rearrange("p (k h) -> p k h", k=NK)
                down_w = w_moe[:, e, 2 * NK * H:].rearrange("p (k c) -> p k c", k=NH)
                sp.dma_start(gate_w, wg[e].rearrange("(k p) h -> p k h", p=P)).then_inc(w_loaded, 16)
                sp.dma_start(up_w, wi[e].rearrange("(k p) h -> p k h", p=P)).then_inc(w_loaded, 16)
                sp.dma_start(down_w, wo[e].rearrange("(k p) c -> p k c", p=P)).then_inc(w_loaded, 16)
            store_h2(G - 1)

            sp.wait_ge(tab_ready, 1)
            sp.wait_ge(padded, 16 * (E + 1))
            sp.wait_ge(scattered, 16 * 2 * GB * G)

            def load_tile(i, k, first):
                if not first:
                    sp.wait_ge(xg_turned, i - XB + 1)
                    sp.wait_ge(meta_ready, i - XB + 1)
                r = sp.value_load(tab[0:1, 1, bass.ds(i, 1)], min_val=0, max_val=E * REG)
                sp.dma_start(xg[k], rows_dram[bass.ds(r, P), :]).then_inc(tile_loaded[k], 16)

            for k in range(XB):
                load_tile(k, k, True)
            with sp.Fori(XB, NT, XB) as i:
                for k in range(XB):
                    load_tile(i + k, k, False)
            sp.wait_ge(h2_stored, 16 * (G + 1))
            sp.wait_ge(added, 16 * NT)

        @block.gpsimd
        def _(pool):
            pool.memset(ident[:, :], 0.0).then_inc(s_ctmp, 1)
            pool.memset(select[:, :, :], 0.0).then_inc(s_ctmp, 1)
            pool.memset(below[:, :], 1.0).then_inc(s_ctmp, 1)
            pool.wait_ge(s_ctmp, 3)
            pool.affine_select(out=ident[:, :], in_=ident[:, :], compare_op=ALU.not_equal, fill=1.0, base=0,
                               pattern=[[-1, P]], channel_multiplier=1).then_inc(s_const, 1)
            pool.affine_select(out=below[:, :], in_=below[:, :], compare_op=ALU.is_gt, fill=0.0, base=0,
                               pattern=[[1, P]], channel_multiplier=-1).then_inc(s_const, 1)
            for q in range(3):
                pool.affine_select(out=select[:, :, :], in_=select[:, :, :], compare_op=ALU.not_equal, fill=1.0,
                                   base=-q * R, pattern=[[-1, R], [0, P]], channel_multiplier=1).then_inc(s_ctmp, 1)
                pool.wait_ge(s_ctmp, 4 + q)
            pool.iota(key_w[:, :, :], pattern=[[0, GB], [-1, E]], base=E, channel_multiplier=0,
                      allow_small_or_imprecise_dtypes=True).then_inc(s_const, 1)
            pool.iota(ebase[:, :], pattern=[[REG, E]], base=0, channel_multiplier=0,
                      allow_small_or_imprecise_dtypes=True).then_inc(s_const, 1)
            pool.iota(jlim[:, :], pattern=[[P, TOKENS // P]], base=0, channel_multiplier=0,
                      allow_small_or_imprecise_dtypes=True).then_inc(s_const, 1)
            pool.iota(tile_no[:, :], pattern=[[1, NT]], base=0, channel_multiplier=0,
                      allow_small_or_imprecise_dtypes=True).then_inc(s_const, 1)
            pool.iota(iota_p[:, :], pattern=[[0, 1]], base=0, channel_multiplier=1,
                      allow_small_or_imprecise_dtypes=True).then_inc(s_const, 1)
            pool.iota(tokf[:, :], pattern=[[P, GB]], base=0, channel_multiplier=1,
                      allow_small_or_imprecise_dtypes=True).then_inc(s_const, 1)
            pool.memset(half[:, :], -0.5).then_inc(s_const, 1)
            pool.memset(ones_bf[:, :], 1.0).then_inc(s_const, 1)

            def rsqrt(g, which, ready, done):
                pool.wait_ge(ready, g + 1)
                pool.tensor_tensor(rstd[:, which, :], mv[:, which, :, 1], half[:, :], ALU.pow).then_inc(done, 1)

            def conv(g, c):
                t = tap[c % 2]
                if c == 0:
                    ahead(pool, skip_done, g)
                    ahead(pool, u_ready, g)
                pool.wait_ge(a_free, FA * g + 6 + c + 1)
                dst = xc[:, c, :].rearrange("p (b t) -> p b t", b=GB)
                pool.tensor_tensor(dst, t[3][:, :, :], t[2][:, :, :], ALU.add).then_inc(conv_part, 1)
                pool.wait_ge(conv_part, 2 * (NCH * g + c) + 1)
                pool.tensor_tensor(dst, dst, t[1][:, :, :], ALU.add).then_inc(conv_part, 1)
                pool.wait_ge(conv_part, 2 * (NCH * g + c) + 2)
                pool.tensor_tensor(dst, dst, t[0][:, :, :], ALU.add).then_inc(conv_ready, 1)

            def make_u(g, par):
                pool.wait_ge(ln_ready, g + 1)
                pool.tensor_tensor(delta[par], delta[par], soft[:, :, :], ALU.add).then_inc(delta_ready, 1)
                pool.wait_ge(delta_ready, g + 1)
                pool.wait_ge(xc_ready, g + 1)
                ahead(pool, scan_done, S * (g - 1))
                pool.tensor_tensor(u[par], delta[par], xc, ALU.mult).then_inc(u_ready, 1)

            def make_dbx(g, n, par):
                pool.wait_ge(b_copied, HS * g + n // 2 + 1)
                if n == 1:
                    pool.wait_ge(u_ready, g + 1)
                ahead(pool, scan_done, S * g + n - 1)
                rep = b_rep[n // 2 % 2][:, :].rearrange("p (a t) -> p a t", a=1)
                pool.tensor_tensor(dBx[n % 2], u[par], rep.broadcast_to([P, NCH, GT]), ALU.mult).then_inc(dbx_pool, 1)

            def scatter(g):
                pool.wait_ge(slot_ready, g + 1)
                apart(pool, "pool")
                for k in range(2):
                    for b in range(GB):
                        pool.indirect_dma_start(
                            out=rows_dram[:, :], out_offset=bass.IndirectOffsetOnAxis(ap=slot[:, k, b:b + 1], axis=0),
                            in_=row[k][:, b, :], in_offset=None).then_inc(scattered, 16)
                pool.wait_ge(scattered, 16 * 2 * GB * (g + 1))
                pool.sem_inc(rows_left, 1)

            def front(g, par):
                rsqrt(g, 0, stat1, pow1)
                for c in range(NCH):
                    conv(g, c)
                make_u(g, par)

            def step(g, par, first, last):
                for n in range(S):
                    if n % 2 == 0:
                        make_dbx(g, n + 1, par)
                    if n == 4 and not last:
                        rsqrt(g + 1, 0, stat1, pow1)
                    if n == 5 and not first:
                        rsqrt(g - 1, 1, stat2, pow2)
                    if n in (6, 7, 8, 9) and not last:
                        conv(g + 1, n - 6)
                    if n == 13 and not last:
                        make_u(g + 1, 1 - par)
                    if n == 15 and not first:
                        scatter(g - 1)

            front(0, 0)
            step(0, 0, True, False)
            with pool.Fori(1, G - 1, 2) as g:
                step(g, 1, False, False)
                step(g + 1, 0, False, False)
            step(G - 1, 1, False, True)
            rsqrt(G - 1, 1, stat2, pow2)
            scatter(G - 1)

            pool.wait_ge(pad_ready, 1)
            pool.dma_start(rows_dram[E * REG:E * REG + P, :], pad_row[:, :]).then_inc(padded, 16)
            for e in range(E):
                pool.indirect_dma_start(
                    out=rows_dram[:, :], out_offset=bass.IndirectOffsetOnAxis(ap=pad_idx[:, e:e + 1], axis=0),
                    in_=pad_row[:, :], in_offset=None).then_inc(padded, 16)

            pool.wait_ge(h2_stored, 16 * (G + 1))

            def add_tile(i, k, first):
                pool.wait_ge(y_ready, i + 1)
                if not first:
                    pool.wait_ge(added, 16 * i)
                apart(pool, "pool")
                pool.indirect_dma_start(
                    out=out.rearrange("b o l -> (b o) l"),
                    out_offset=bass.IndirectOffsetOnAxis(ap=tok_id[k][:, 0:1], axis=0), in_=yt[k % 2],
                    in_offset=None, bounds_check=TOKENS - 1, oob_is_err=False, compute_op=ALU.add).then_inc(added, 16)

            for k in range(XB):
                add_tile(k, k, k == 0)
            with pool.Fori(XB, NT, XB) as i:
                for k in range(XB):
                    add_tile(i + k, k, False)

        @block.scalar
        def _(actq):
            actq.dma_start(a_neg[:, :, :], A_log.rearrange("(c p) s -> p c s", p=P)).then_inc(s_par, 16)
            for dst, src in ((cb, conv_b), (wdt, w_dt), (bdt, b_dt), (dpar, D_param)):
                actq.dma_start(dst[:, :], src.rearrange("(c p) -> p c", p=P), allow_slow_non_contiguous=True)\
                    .then_inc(s_par, 16)
            actq.dma_start(cw[:, :, :], conv_w.rearrange("(c p) a k -> p c (a k)", p=P)).then_inc(s_par, 16)
            for q in range(3):
                actq.dma_start(w_x3[:, :, q * R:(q + 1) * R], W_xproj.rearrange("(c p) r -> p c r", p=P))\
                    .then_inc(s_wts, 16)
            actq.dma_start(w_out_sb[:, :, :], W_out.rearrange("(c p) n -> p c n", p=P)).then_inc(s_wts, 16)
            actq.dma_start(w_gate_sb[:, :, :], w_gate.rearrange("(k p) n -> p k n", p=P)).then_inc(s_wts, 16)
            actq.wait_ge(s_par, 16 * N_PAR)
            actq.activation(a_neg[:, :, :], a_neg[:, :, :], ACT.Exp).then_inc(s_aexp, 1)
            actq.wait_ge(s_wpt, 1)
            actq.activation(wpt.rearrange("p j t -> p (j t)"), bank_a, ACT.Copy).then_inc(s_wptc, 1)
            actq.wait_ge(s_weff, 1)
            actq.activation(w_eff[:, :], bank_b[0:KX, 0:T], ACT.Copy).then_inc(s_weffc, 1)

            def use(g, k):
                actq.wait_ge(a_full, UA * g + k + 1)

            def evac_xt(g, m):
                use(g, m)
                nc.scalar.activation(xt[:, m * GT:(m + 1) * GT], bank_a[0:KX, :], ACT.Copy).then_inc(a_free, 1)

            def evac_h(g, par, m):
                use(g, 2 + m)
                ahead(actq, h2_ready, 2 * (g - 1))
                dst = hres[par][:, 2 * m:2 * m + 2, :].rearrange("p b c -> p (b c)")
                nc.scalar.activation(dst, bank_a, ACT.Copy).then_inc(a_free, 1)

            def evac_xnt(g, k):
                use(g, 4 + k)
                nc.scalar.activation(xnt[:, k, :], bank_a, ACT.Copy).then_inc(a_free, 1)

            def taps(g, c):
                use(g, 6 + c)
                ahead(actq, conv_ready, NCH * g + c - 1)
                src = bank_a.rearrange("p (b t) -> p b t", b=GB)
                for k in range(TAPS):
                    d = TAPS - 1 - k
                    if d == 0:
                        nc.scalar.activation(tap[c % 2][k][:, :, :], src, ACT.Identity, scale=cw[:, c, k:k + 1],
                                             bias=cb[:, c:c + 1]).then_inc(a_free, 1)
                    else:
                        nc.scalar.activation(tap[c % 2][k][:, :, d:T], src[:, :, 0:T - d], ACT.Copy,
                                             scale=cw[:, c, k:k + 1])

            def evac_z(g, par, c):
                use(g, 10 + c)
                if c == 0:
                    ahead(actq, yz_ready, g - 1)
                nc.scalar.activation(z[par][:, c, :], bank_a, ACT.Copy).then_inc(a_free, 1)

            def silus(g, par):
                actq.wait_ge(conv_ready, NCH * (g + 1))
                nc.scalar.activation(xc, xc, ACT.Silu).then_inc(xc_ready, 1)
                actq.wait_ge(a_free, FA * g + 14)
                nc.scalar.activation(z[par][:, :, :], z[par][:, :, :], ACT.Silu).then_inc(z_ready, 1)

            def split_hi(g, par):
                use(g, 14)
                ahead(actq, c_full, S * (g - 1))
                nc.scalar.activation(bc3[par][:, :], bank_a[0:3 * R, :], ACT.Copy).then_inc(hi_ready, 1)

            def split_mid(g, par):
                actq.wait_ge(rest_ready, g + 1)
                nc.scalar.activation(bc3[par][0:2 * R, :], split[:, :], ACT.Copy).then_inc(mid_ready, 1)

            def softplus_in(g, par):
                use(g, 15)
                ahead(actq, o_full, 2 * (g - 1))
                ahead(actq, delta_ready, g)
                for c in range(NCH):
                    nc.scalar.activation(soft[:, c, :], bank_a, ACT.Abs, scale=wdt[:, c:c + 1], bias=bdt[:, c:c + 1])
                    last = nc.scalar.activation(delta[par][:, c, :], bank_a, ACT.Relu, scale=wdt[:, c:c + 1],
                                                bias=bdt[:, c:c + 1])
                last.then_inc(a_free, 1)

            def softplus_out(g):
                actq.wait_ge(a_free, FA * (g + 1))
                nc.scalar.activation(soft[:, :, :], soft[:, :, :], ACT.Exp, scale=-1.0).then_inc(sexp_ready, 1)
                actq.wait_ge(sexp_ready, g + 1)
                nc.scalar.activation(soft[:, :, :], soft[:, :, :], ACT.Ln, bias=1.0).then_inc(ln_ready, 1)

            def copy_b(g, n):
                actq.wait_ge(b_full, S * g + n + 1)
                ahead(actq, dbx_pool, HS * g + n // 2 - 1)
                nc.scalar.activation(b_rep[n // 2 % 2][:, :], b_ps, ACT.Copy).then_inc(b_copied, 1)

            def exps(g, n, par):
                if n == 0:
                    actq.wait_ge(delta_ready, g + 1)
                ahead(actq, scan_done, S * g + n - 1)
                for c in range(NCH):
                    o = dA[n % 2][:, c, :].rearrange("p (b t) -> p b t", b=GB)[:, :, 1:T]
                    i = delta[par][:, c, :].rearrange("p (b t) -> p b t", b=GB)[:, :, 1:T]
                    last = nc.scalar.activation(o, i, ACT.Exp, scale=a_neg[:, c, n:n + 1])
                last.then_inc(dA_ready, 1)

            def evac_xn2t(g, k):
                actq.wait_ge(t_full, NK * g + k + 1)
                nc.scalar.activation(xn2t[:, k, :], bank_b, ACT.Copy).then_inc(xn2t_ready, 1)

            def router_exp(g):
                actq.wait_ge(lsub_ready, g + 1)
                nc.scalar.activation(ex[:, :, :], ex[:, :, :], ACT.Exp).then_inc(lexp_ready, 1)

            def front(g, par):
                for m in range(2):
                    evac_xt(g, m)
                for m in range(2):
                    evac_h(g, par, m)
                for k in range(NK):
                    evac_xnt(g, k)
                for c in range(NCH):
                    taps(g, c)
                for c in range(NCH):
                    evac_z(g, par, c)
                silus(g, par)
                split_hi(g, par)
                split_mid(g, par)
                softplus_in(g, par)
                softplus_out(g)

            def step(g, par, first, last):
                for n in range(S):
                    g1, n1 = gn(g, n + 1)
                    if n1 % 2 == 1:
                        copy_b(g1, n1)
                    if not (last and n1 == 0):
                        exps(g1, n1, par if n1 else 1 - par)
                    if not first and n == 7:
                        evac_xn2t(g - 1, 0)
                        evac_xn2t(g - 1, 1)
                    if not last:
                        if n == 0:
                            evac_xt(g + 1, 0)
                            evac_xt(g + 1, 1)
                        if n == 3:
                            evac_h(g + 1, 1 - par, 0)
                            evac_h(g + 1, 1 - par, 1)
                        if n == 5:
                            evac_xnt(g + 1, 0)
                            evac_xnt(g + 1, 1)
                        if n in (6, 7):
                            taps(g + 1, 2 * (n - 6))
                            taps(g + 1, 2 * (n - 6) + 1)
                        if n in (8, 9):
                            evac_z(g + 1, 1 - par, 2 * (n - 8))
                            evac_z(g + 1, 1 - par, 2 * (n - 8) + 1)
                        if n == 10:
                            silus(g + 1, 1 - par)
                        if n == 11:
                            split_hi(g + 1, 1 - par)
                        if n == 12:
                            split_mid(g + 1, 1 - par)
                        if n == 13:
                            softplus_in(g + 1, 1 - par)
                            softplus_out(g + 1)
                    if not first and n == 11:
                        router_exp(g - 1)

            actq.wait_ge(s_zero, 2)
            actq.wait_ge(s_set, 6 + NCH + 1)
            front(0, 0)
            exps(0, 0, 0)
            step(0, 0, True, False)
            with actq.Fori(1, G - 1, 2) as g:
                step(g, 1, False, False)
                step(g + 1, 0, False, False)
            step(G - 1, 1, False, True)
            evac_xn2t(G - 1, 0)
            evac_xn2t(G - 1, 1)
            router_exp(G - 1)

            def evac_x(i, k):
                actq.wait_ge(xg_turned, i + 1)
                if not (isinstance(i, int) and i < 2):
                    actq.wait_ge(up_full, i - 1)
                nc.scalar.activation(xgt[k % 2], px[:, 0:C], ACT.Copy).then_inc(xgt_ready, 1)

            def silu(i, k):
                actq.wait_ge(gate_full, i + 1)
                if not (isinstance(i, int) and i < 2):
                    actq.wait_ge(act_ready, i - 1)
                nc.scalar.activation(sg[k % 2], pg[k % 2], ACT.Silu).then_inc(silu_ready, 1)

            def weigh(i, k):
                actq.wait_ge(y_full, i + 1)
                actq.wait_ge(meta_ready, i + 1)
                if not (isinstance(i, int) and i < 2):
                    actq.wait_ge(added, 16 * (i - 1))
                nc.scalar.activation(yt[k % 2], py[k % 2], ACT.Copy, scale=tok_w[k][:, 0:1]).then_inc(y_ready, 1)

            def tiles(i, first, last):
                for k in range(XB):
                    if not (last and k == XB - 1):
                        evac_x(i + k + 1, (k + 1) % XB)
                    silu(i + k, k)
                    if not (first and k == 0):
                        weigh(i + k - 1, (k - 1) % XB)

            evac_x(0, 0)
            tiles(0, True, False)
            with actq.Fori(XB, NT - XB, XB) as i:
                tiles(i, False, False)
            tiles(NT - XB, False, True)
            weigh(NT - 1, XB - 1)

        @block.vector
        def _(dve):
            dve.memset(band, 0.0).then_inc(s_band0, 1)
            dve.memset(z[0][0:1, 1, 0:KX], 0.0).then_inc(s_band0, 1)
            dve.wait_ge(s_band0, 2)
            dve.memset(e_last[:, KX - 1:KX], 1.0).then_inc(s_set, 1)
            for i in range(2):
                dve.memset(xw[i][:, :, :, :], 0.0).then_inc(s_set, 1)
            dve.wait_ge(s_set, 3)
            dve.memset(xw[0][:, :, :, KX - 1:KX], 1.0)
            dve.memset(xw[1][:, :, :, KX - 1:KX], 1.0).then_inc(s_zero, 1)
            for i in range(2):
                for k in range(TAPS - 1):
                    dve.memset(tap[i][k][:, :, 0:TAPS - 1 - k], 0.0)
                for c in range(NCH):
                    last = dve.memset(dA[i][:, c, :].rearrange("p (b t) -> p b t", b=GB)[:, :, 0:1], 0.0)
            last.then_inc(s_zero, 1)
            dve.memset(pad_row[:, :], 0.0).then_inc(s_set, 1)
            dve.memset(ones_e[:, :], 1.0)
            dve.wait_ge(s_set, 4)
            dve.memset(pad_row[:, C:C + 1].bitcast(I32), TOKENS).then_inc(s_set, 1)
            dve.wait_ge(s_par, 16 * N_PAR)
            dve.wait_ge(s_aexp, 1)
            dve.tensor_scalar(a_neg[:, :, :], a_neg[:, :, :], -1.0, None, ALU.mult).then_inc(s_set, 1)
            dve.wait_ge(s_const, 10)
            for c in range(NCH):
                dve.tensor_scalar(diag_d[:, c, :], ident[:, :], dpar[:, c:c + 1], None, ALU.mult).then_inc(s_set, 1)
            dve.tensor_copy(counts[:, :], ebase[:, :]).then_inc(s_set, 1)
            dve.wait_ge(s_set, 6 + NCH + 1)

            def stats(g, which, src, ready):
                for b in range(GB):
                    ins = nc.vector.bn_stats(stat[:, which, b, :], src[:, b, :])
                ins.then_inc(stat_step[which], 1)
                dve.wait_ge(stat_step[which], 2 * g + 1)
                apart(dve, "dve")
                for b in range(GB):
                    ins = nc.vector.bn_aggr(mv[:, which, b, :], stat[:, which, b, :])
                ins.then_inc(stat_step[which], 1)
                dve.wait_ge(stat_step[which], 2 * g + 2)
                nc.vector.tensor_scalar(mv[:, which, :, 1], mv[:, which, :, 1], EPS, None, ALU.add).then_inc(ready, 1)

            def norm1_stats(g, par):
                dve.wait_ge(a_free, FA * g + 4)
                stats(g, 0, hres[par], stat1)

            def norm1(g, par):
                dve.wait_ge(pow1, g + 1)
                ahead(dve, a_full, UA * (g - 1) + 6)
                for b in range(GB):
                    last = nc.vector.tensor_scalar(xn[:, b, :], hres[par][:, b, :], mv[:, 0, b, 0:1],
                                                   rstd[:, 0, b:b + 1], ALU.subtract, ALU.mult)
                last.then_inc(xn_ready, 1)

            def split_rest(g, par):
                dve.wait_ge(hi_ready, g + 1)
                nc.vector.tensor_tensor(split[:, :], bank_a[0:2 * R, :], bc3[par][0:2 * R, :], ALU.subtract)\
                    .then_inc(rest_ready, 1)

            def split_lo(g, par):
                dve.wait_ge(mid_ready, g + 1)
                nc.vector.tensor_tensor(bc3[par][0:R, :], split[0:R, :], bc3[par][0:R, :], ALU.subtract)\
                    .then_inc(bc_ready, 1)

            def make_dbx(g, n, par):
                dve.wait_ge(b_full, S * g + n + 1)
                if n == 0:
                    dve.wait_ge(u_ready, g + 1)
                ahead(dve, scan_done, S * g + n - 1)
                rep = b_ps.rearrange("p (a t) -> p a t", a=1)
                nc.vector.tensor_tensor(dBx[n % 2], u[par], rep.broadcast_to([P, NCH, GT]), ALU.mult)\
                    .then_inc(dbx_dve, 1)

            def scan(g, n):
                dve.wait_ge(dA_ready, S * g + n + 1)
                if n % 2:
                    dve.wait_ge(dbx_pool, HS * g + n // 2 + 1)
                else:
                    dve.wait_ge(dbx_dve, HS * g + n // 2 + 1)
                ahead(dve, hc_ready, S * g + n)
                nc.vector.tensor_tensor_scan(flat(state), flat(dA[n % 2]), flat(dBx[n % 2]), 0.0,
                                             ALU.mult, ALU.add).then_inc(scan_done, 1)

            def times_c(g, n):
                dve.wait_ge(scan_done, S * g + n + 1)
                dve.wait_ge(c_full, S * g + n + 1)
                ahead(dve, sum_done, S * g + n - 1)
                rep = c_ps.rearrange("p (a t) -> p a t", a=1)
                nc.vector.tensor_tensor(hc[n % 2], state, rep.broadcast_to([P, NCH, GT]), ALU.mult)\
                    .then_inc(hc_ready, 1)

            def gate_y(g, par):
                dve.wait_ge(sum_done, S * (g + 1))
                dve.wait_ge(z_ready, g + 1)
                dve.wait_ge(delta_ready, min(g + 2, G) if isinstance(g, int) else g + 2)
                nc.vector.tensor_tensor(yz[:, :, :], yacc, z[par][:, :, :], ALU.mult).then_inc(yz_ready, 1)

            def residual(g, par, m):
                dve.wait_ge(o_full, 2 * g + m + 1)
                if m == 0:
                    dve.wait_ge(h2_stored, 16 * (g + 1))
                dst = h2[:, 2 * m:2 * m + 2, :].rearrange("p b c -> p (b c)")
                src = hres[par][:, 2 * m:2 * m + 2, :].rearrange("p b c -> p (b c)")
                nc.vector.tensor_tensor(dst, bank_b, src, ALU.add).then_inc(h2_ready, 1)

            def norm2_stats(g):
                dve.wait_ge(h2_ready, 2 * g + 2)
                stats(g, 1, h2, stat2)

            def norm2(g):
                dve.wait_ge(pow2, g + 1)
                dve.wait_ge(rows_left, g + 1)
                for k in range(2):
                    for b in range(GB):
                        last = nc.vector.tensor_scalar(row[k][:, b, 0:C], h2[:, b, :], mv[:, 1, b, 0:1],
                                                       rstd[:, 1, b:b + 1], ALU.subtract, ALU.mult)
                last.then_inc(row_ready, 1)

            def after(g, k):
                dve.wait_ge(dv, ROUTER * g + k)

            def bc(ap):
                return ap.rearrange("p (b a) -> p b a", a=1).broadcast_to([P, GB, E])

            def router_a(g):
                dve.wait_ge(l_full, g + 1)
                logits = bank_b[:, 0:GB * E].rearrange("p (b e) -> p b e", b=GB)
                nc.vector.tensor_reduce(lmax[:, :], logits, AX_X, ALU.max).then_inc(dv, 1)
                after(g, 1)
                nc.vector.tensor_tensor(ex[:, :, :], logits, bc(lmax[:, :]), ALU.subtract).then_inc(lsub_ready, 1)

            def router_b(g):
                dve.wait_ge(lexp_ready, g + 1)
                nc.vector.tensor_reduce(esum[:, :], ex[:, :, :], AX_X, ALU.add).then_inc(dv, 1)
                after(g, 2)
                nc.vector.reciprocal(einv[:, :], esum[:, :]).then_inc(dv, 1)
                after(g, 3)
                nc.vector.tensor_tensor(gates[:, :, :], ex[:, :, :], bc(einv[:, :]), ALU.mult).then_inc(dv, 1)
                n = 4
                for k, src in ((0, gates), (1, g2)):
                    after(g, n)
                    nc.vector.tensor_reduce(m1[:, k, :], src[:, :, :], AX_X, ALU.max).then_inc(dv, 1)
                    after(g, n + 1)
                    nc.vector.tensor_tensor(eq[:, :, :], src[:, :, :], bc(m1[:, k, :]), ALU.is_equal).then_inc(dv, 1)
                    after(g, n + 2)
                    nc.vector.tensor_tensor(key[:, :, :], eq[:, :, :], key_w[:, :, :], ALU.mult).then_inc(dv, 1)
                    after(g, n + 3)
                    nc.vector.tensor_reduce(kmax[:, :], key[:, :, :], AX_X, ALU.max).then_inc(dv, 1)
                    after(g, n + 4)
                    nc.vector.tensor_tensor(oh[k][:, :, :], key[:, :, :], bc(kmax[:, :]), ALU.is_equal).then_inc(dv, 1)
                    n += 5
                    if k == 0:
                        after(g, n)
                        nc.vector.scalar_tensor_tensor(out=g2[:, :, :], in0=oh[0][:, :, :], scalar=-2.0,
                                                       in1=gates[:, :, :], op0=ALU.mult, op1=ALU.add).then_inc(dv, 1)
                        n += 1
                after(g, n)
                nc.vector.tensor_tensor(mask[:, :, :], oh[0][:, :, :], oh[1][:, :, :], ALU.add).then_inc(mask_ready, 1)
                for k in range(2):
                    nc.vector.tensor_copy(row[k][:, :, C:C + 1].bitcast(I32),
                                          tokf[:, :].rearrange("p (b a) -> p b a", a=1)).then_inc(dv, 1)
                    nc.vector.tensor_copy(row[k][:, :, C + 1:C + 2],
                                          m1[:, k, :].rearrange("p (b a) -> p b a", a=1)).then_inc(dv, 1)
                n += 4
                after(g, n)
                nc.vector.tensor_scalar(tokf[:, :], tokf[:, :], float(GT), None, ALU.add).then_inc(dv, 1)
                assert n + 1 == 20

            def router_c(g):
                dve.wait_ge(n_full, g + 1)
                earlier = bank_b[:, 0:GB * E].rearrange("p (b e) -> p b e", b=GB)
                cb_ = counts[:, :].rearrange("p (a e) -> p a e", a=1).broadcast_to([P, GB, E])
                nc.vector.tensor_tensor(pos[:, :, :], earlier, cb_, ALU.add).then_inc(dv, 1)
                after(g, 21)
                nc.vector.tensor_tensor(counts[:, :], counts[:, :], bank_b[:, GB * E:(GB + 1) * E], ALU.add)\
                    .then_inc(dv, 1)
                n = 22
                for k in range(2):
                    nc.vector.tensor_tensor(eq[:, :, :], oh[k][:, :, :], pos[:, :, :], ALU.mult).then_inc(dv, 1)
                    after(g, n + 1)
                    nc.vector.tensor_reduce(slot_f[:, k, :], eq[:, :, :], AX_X, ALU.add).then_inc(dv, 1)
                    n += 2
                    after(g, n)
                nc.vector.tensor_copy(slot[:, :, :], slot_f[:, :, :]).then_inc(slot_ready, 1)

            def front(g, par):
                norm1_stats(g, par)
                norm1(g, par)
                split_rest(g, par)
                split_lo(g, par)

            def step(g, par, first, last):
                for n in range(S):
                    if n == 0 and not first:
                        gate_y(g - 1, 1 - par)
                    if n == 4 and not last:
                        norm1_stats(g + 1, 1 - par)
                    g1, n1 = gn(g, n + 1)
                    scan(g, n)
                    if n1 % 2 == 0 and n1:
                        make_dbx(g1, n1, par)
                    times_c(g, n)
                    if n1 == 0 and not last:
                        make_dbx(g1, 0, 1 - par)
                    if not first:
                        if n == 1:
                            residual(g - 1, 1 - par, 0)
                        if n == 2:
                            residual(g - 1, 1 - par, 1)
                        if n == 5:
                            norm2_stats(g - 1)
                        if n == 6:
                            norm2(g - 1)
                        if n == 10:
                            router_a(g - 1)
                        if n == 12:
                            router_b(g - 1)
                        if n == 14:
                            router_c(g - 1)
                    if not last:
                        if n == 4:
                            norm1(g + 1, 1 - par)
                        if n == 11:
                            split_rest(g + 1, 1 - par)
                        if n == 12:
                            split_lo(g + 1, 1 - par)

            front(0, 0)
            make_dbx(0, 0, 0)
            step(0, 0, True, False)
            with dve.Fori(1, G - 1, 2) as g:
                step(g, 1, False, False)
                step(g + 1, 0, False, False)
            step(G - 1, 1, False, True)
            gate_y(G - 1, 1)
            residual(G - 1, 1, 0)
            residual(G - 1, 1, 1)
            norm2_stats(G - 1)
            norm2(G - 1)
            router_a(G - 1)
            router_b(G - 1)
            router_c(G - 1)

            base = ROUTER * G
            dve.wait_ge(slot_ready, G)
            nc.vector.tensor_scalar(pad_idx_f[:, :], counts[:, :], iota_p[:, 0:1], None, ALU.add).then_inc(dv, 1)
            dve.wait_ge(dv, base + 1)
            nc.vector.tensor_copy(pad_idx[:, :], pad_idx_f[:, :]).then_inc(pad_ready, 1)
            nc.vector.tensor_tensor(ne[:, :], counts[0:1, :], ebase[0:1, :], ALU.subtract).then_inc(dv, 1)
            dve.wait_ge(dv, base + 2)
            J = TOKENS // P
            ne_b = ne[:, :].rearrange("p (e a) -> p e a", a=1).broadcast_to([1, E, J])
            jl_b = jlim[:, :].rearrange("p (a j) -> p a j", a=1).broadcast_to([1, E, J])
            nc.vector.tensor_tensor(cmp1, ne_b, jl_b, ALU.is_gt).then_inc(dv, 1)
            dve.wait_ge(dv, base + 3)
            nc.vector.tensor_reduce(nt[:, :], cmp1, AX_X, ALU.add).then_inc(dv, 1)
            dve.wait_ge(dv, base + 4)
            nc.vector.tensor_tensor_scan(tend[:, :], ones_e[:, :], nt[:, :], 0.0, ALU.mult, ALU.add).then_inc(dv, 1)
            dve.wait_ge(dv, base + 5)
            te_b = tend[:, :].rearrange("p (a e) -> p a e", a=1).broadcast_to([1, NT, E])
            nt_b = nt[:, :].rearrange("p (a e) -> p a e", a=1).broadcast_to([1, NT, E])
            no_b = tile_no[:, :].rearrange("p (i a) -> p i a", a=1).broadcast_to([1, NT, E])
            nc.vector.tensor_tensor(cmp2, te_b, no_b, ALU.is_le).then_inc(dv, 1)
            dve.wait_ge(dv, base + 6)
            nc.vector.tensor_reduce(e_of, cmp2, AX_X, ALU.add).then_inc(dv, 1)
            nc.vector.tensor_tensor(cmp3, cmp2, nt_b, ALU.mult).then_inc(dv, 1)
            dve.wait_ge(dv, base + 8)
            nc.vector.tensor_reduce(t_of, cmp3, AX_X, ALU.add).then_inc(dv, 1)
            dve.wait_ge(dv, base + 9)
            nc.vector.tensor_tensor(r_of, tile_no[:, :], t_of, ALU.subtract).then_inc(dv, 1)
            nc.vector.tensor_scalar(b_of, e_of, float(REG), None, ALU.mult).then_inc(dv, 1)
            dve.wait_ge(dv, base + 11)
            nc.vector.scalar_tensor_tensor(out=r_of, in0=r_of, scalar=float(P), in1=b_of,
                                           op0=ALU.mult, op1=ALU.add).then_inc(dv, 1)
            dve.wait_ge(dv, base + 12)
            nc.vector.tensor_scalar(tab[:, 1, 0:NT], r_of, float(E * REG), None, ALU.min).then_inc(dv, 1)
            nc.vector.tensor_scalar(tab[:, 0, 0:NT], e_of, float(E - 1), None, ALU.min).then_inc(dv, 1)
            dve.wait_ge(dv, base + 14)
            dve.sem_inc(tab_ready, 1)

            def meta(i, k):
                dve.wait_ge(tile_loaded[k], (16 * (i // XB + 1)) if isinstance(i, int) else (i - k) * (16 // XB) + 16)
                if not (isinstance(i, int) and i < XB):
                    dve.wait_ge(added, 16 * (i - XB + 1))
                nc.vector.tensor_copy(tok_id[k][:, :], xg[k][:, C:C + 1].bitcast(U32))
                nc.vector.tensor_copy(tok_w[k][:, :], xg[k][:, C + 1:C + 2]).then_inc(meta_ready, 1)

            def gated(i, k):
                dve.wait_ge(silu_ready, i + 1)
                dve.wait_ge(up_full, i + 1)
                if not (isinstance(i, int) and i < 2):
                    dve.wait_ge(at_full, i - 1)
                nc.vector.tensor_tensor(act[k % 2], pu[k % 2], sg[k % 2], ALU.mult).then_inc(act_ready, 1)

            def evac_at(i, k):
                dve.wait_ge(at_full, i + 1)
                if not (isinstance(i, int) and i < 2):
                    dve.wait_ge(y_full, i - 1)
                nc.vector.tensor_copy(actt[k % 2], pt).then_inc(actt_ready, 1)

            def tiles(i, first, last):
                for k in range(XB):
                    if not (first and k == 0):
                        evac_at(i + k - 1, (k - 1) % XB)
                    meta(i + k, k)
                    gated(i + k, k)

            tiles(0, True, False)
            with dve.Fori(XB, NT - XB, XB) as i:
                tiles(i, False, False)
            tiles(NT - XB, False, True)
            evac_at(NT - 1, XB - 1)

        @block.tensor
        def _(pe):
            pe.wait_ge(s_par, 16 * N_PAR)
            pe.wait_ge(s_const, 10)
            pe.wait_ge(s_set, 6 + NCH + 1)
            for j in range(NJ):
                last = nc.tensor.transpose(bank_a[:, j * T:(j + 1) * T], wp_sb[:, j * P:(j + 1) * P], ident[:, :])
            last.then_inc(s_wpt, 1)
            pe.wait_ge(s_wptc, 1)
            for j in range(NJ):
                nc.tensor.matmul(bank_b[0:KX, 0:T], band[:, j, :], wpt[:, j, :], start=(j == 0), stop=False)
            nc.tensor.matmul(bank_b[0:KX, 0:T], e_last, bp_row, start=False, stop=True).then_inc(s_weff, 1)
            pe.wait_ge(s_weffc, 1)
            pe.wait_ge(s_wts, 16 * N_WTS)

            def take_a(g, k):
                ahead(pe, a_free, FA * g + k)

            def turn_x(g, par, m):
                take_a(g, m)
                if m == 0:
                    pe.wait_ge(x_loaded[par], (g - par) * (X_PER // 2) + X_PER)
                apart(pe, "pe")
                for q in range(4):
                    b, k = 2 * m + q // 2, q % 2
                    last = nc.tensor.transpose(bank_a[0:KX, q * P:(q + 1) * P], xw[par][:, b, k, :], ident[:, :])
                last.then_inc(a_full, 1)

            def embed(g, m):
                take_a(g, 2 + m)
                nc.tensor.matmul(bank_a, w_eff[:, :], xt[:, m * GT:(m + 1) * GT], start=True, stop=True)\
                    .then_inc(a_full, 1)

            def turn_xn(g, k):
                take_a(g, 4 + k)
                pe.wait_ge(xn_ready, g + 1)
                for b in range(GB):
                    last = nc.tensor.transpose(bank_a[:, b * T:(b + 1) * T], xn[:, b, k * P:(k + 1) * P], ident[:, :])
                last.then_inc(a_full, 1)

            def project(g, c):
                take_a(g, 6 + c)
                for k in range(NK):
                    last = nc.tensor.matmul(bank_a, w_in_sb[:, k, c * P:(c + 1) * P], xnt[:, k, :],
                                            start=(k == 0), stop=(k == NK - 1))
                last.then_inc(a_full, 1)

            def x_ssm(g):
                take_a(g, 14)
                pe.wait_ge(xc_ready, g + 1)
                for c in range(NCH):
                    last = nc.tensor.matmul(bank_a[0:3 * R, :], w_x3[:, c, :], xc[:, c, :],
                                            start=(c == 0), stop=(c == NCH - 1))
                last.then_inc(a_full, 1)

            def replicate(dst, par, r):
                return nc.tensor.matmul(dst, select[:, r, :], bc3[par][:, :], start=True, stop=True)

            def delta_raw(g, par):
                pe.wait_ge(bc_ready, g + 1)
                replicate(bank_a, par, 0).then_inc(a_full, 1)

            def b_all(g, n, par):
                g0, n0 = (g, n - 1) if n else (g - 1, S - 1)
                if n0 % 2:
                    ahead(pe, b_copied, HS * g0 + n0 // 2 + 1)
                else:
                    ahead(pe, dbx_dve, HS * g0 + n0 // 2 + 1)
                replicate(b_ps, par, 1 + n).then_inc(b_full, 1)

            def c_all(g, n, par):
                ahead(pe, hc_ready, S * g + n)
                replicate(c_ps, par, 1 + S + n).then_inc(c_full, 1)

            def skip(g):
                ahead(pe, yz_ready, g)
                for c in range(NCH):
                    last = nc.tensor.matmul(yacc[:, c, :], diag_d[:, c, :], xc[:, c, :], start=True, stop=False)
                last.then_inc(skip_done, 1)

            def add_state(g, n):
                pe.wait_ge(hc_ready, S * g + n + 1)
                for c in range(NCH):
                    last = nc.tensor.matmul(yacc[:, c, :], ident[:, :], hc[n % 2][:, c, :], start=False,
                                            stop=(n == S - 1))
                last.then_inc(sum_done, 1)

            def project_out(g, m):
                if m == 0:
                    pe.wait_ge(yz_ready, g + 1)
                else:
                    pe.wait_ge(h2_ready, 2 * g + 1)
                for b in range(2):
                    for c in range(NCH):
                        t0 = (2 * m + b) * T
                        last = nc.tensor.matmul(bank_b[:, b * C:(b + 1) * C], yz[:, c, t0:t0 + T], w_out_sb[:, c, :],
                                                start=(c == 0), stop=(c == NCH - 1))
                last.then_inc(o_full, 1)

            def turn_row(g, k):
                if k == 0:
                    pe.wait_ge(row_ready, g + 1)
                else:
                    pe.wait_ge(xn2t_ready, NK * g + k)
                for b in range(GB):
                    last = nc.tensor.transpose(bank_b[:, b * T:(b + 1) * T], row[0][:, b, k * P:(k + 1) * P],
                                               ident[:, :])
                last.then_inc(t_full, 1)

            def router(g):
                pe.wait_ge(xn2t_ready, NK * (g + 1))
                for b in range(GB):
                    for k in range(NK):
                        last = nc.tensor.matmul(bank_b[:, b * E:(b + 1) * E], xn2t[:, k, b * T:(b + 1) * T],
                                                w_gate_sb[:, k, :], start=(k == 0), stop=(k == NK - 1))
                last.then_inc(l_full, 1)

            def count(g):
                pe.wait_ge(mask_ready, g + 1)
                for b in range(GB + 1):
                    dst = bank_b[:, b * E:(b + 1) * E]
                    if b < GB:
                        last = nc.tensor.matmul(dst, below[:, :], mask[:, b, :], start=True, stop=(b == 0))
                    for b0 in range(b):
                        last = nc.tensor.matmul(dst, ones_bf[:, :], mask[:, b0, :], start=(b == GB and b0 == 0),
                                                stop=(b0 == b - 1))
                last.then_inc(n_full, 1)

            def front(g, par):
                for m in range(2):
                    turn_x(g, par, m)
                for m in range(2):
                    embed(g, m)
                for k in range(NK):
                    turn_xn(g, k)
                for c in range(2 * NCH):
                    project(g, c)
                x_ssm(g)
                delta_raw(g, par)

            def step(g, par, first, last):
                for n in range(S):
                    g2_, n2 = gn(g, n + 2)
                    if not first:
                        if n == 1:
                            project_out(g - 1, 0)
                        if n == 2:
                            project_out(g - 1, 1)
                        if n == 7:
                            turn_row(g - 1, 0)
                            turn_row(g - 1, 1)
                        if n == 9:
                            router(g - 1)
                        if n == 13:
                            count(g - 1)
                    if not last:
                        if n == 0:
                            turn_x(g + 1, 1 - par, 0)
                            turn_x(g + 1, 1 - par, 1)
                        if n == 3:
                            embed(g + 1, 0)
                            embed(g + 1, 1)
                        if n == 5:
                            turn_xn(g + 1, 0)
                            turn_xn(g + 1, 1)
                        if n in (6, 7, 8, 9):
                            project(g + 1, 2 * (n - 6))
                            project(g + 1, 2 * (n - 6) + 1)
                        if n == 11:
                            x_ssm(g + 1)
                        if n == 13:
                            delta_raw(g + 1, 1 - par)
                    if not (last and n2 < 2):
                        b_all(g2_, n2, par if n2 >= 2 else 1 - par)
                    g1, n1 = gn(g, n + 1)
                    if not (last and n1 == 0):
                        c_all(g1, n1, par if n1 else 1 - par)
                    if n == 0:
                        skip(g)
                    add_state(g, n)

            front(0, 0)
            b_all(0, 0, 0)
            b_all(0, 1, 0)
            c_all(0, 0, 0)
            step(0, 0, True, False)
            with pe.Fori(1, G - 1, 2) as g:
                step(g, 1, False, False)
                step(g + 1, 0, False, False)
            step(G - 1, 1, False, True)
            project_out(G - 1, 0)
            project_out(G - 1, 1)
            turn_row(G - 1, 0)
            turn_row(G - 1, 1)
            router(G - 1)
            count(G - 1)

            pe.wait_ge(tab_ready, 1)
            pe.wait_ge(w_loaded, 16 * 3 * E)

            def turn_tile(i, k):
                pe.wait_ge(tile_loaded[k], (16 * (i // XB + 1)) if isinstance(i, int) else (i - k) * (16 // XB) + 16)
                if not (isinstance(i, int) and i < 1):
                    pe.wait_ge(xgt_ready, i)
                for q in range(NK):
                    last = nc.tensor.transpose(px[:, q * P:(q + 1) * P], xg[k][:, q * P:(q + 1) * P], ident[:, :])
                last.then_inc(xg_turned, 1)

            def hidden(i, k, e, base, dst, done):
                for q in range(NK):
                    w = w_moe[:, bass.ds(e, 1), base + q * H:base + (q + 1) * H].rearrange("p a h -> p (a h)")
                    last = nc.tensor.matmul(dst[k % 2], xgt[k % 2][:, q * P:(q + 1) * P], w,
                                            start=(q == 0), stop=(q == NK - 1))
                last.then_inc(done, 1)

            def turn_act(i, k):
                pe.wait_ge(act_ready, i + 1)
                if not (isinstance(i, int) and i < 1):
                    pe.wait_ge(actt_ready, i)
                for q in range(NH):
                    last = nc.tensor.transpose(pt[:, q * P:(q + 1) * P], act[k % 2][:, q * P:(q + 1) * P], ident[:, :])
                last.then_inc(at_full, 1)

            def down(i, k, e):
                pe.wait_ge(actt_ready, i + 1)
                if not (isinstance(i, int) and i < 2):
                    pe.wait_ge(y_ready, i - 1)
                for q in range(NH):
                    w = w_moe[:, bass.ds(e, 1), 2 * NK * H + q * C:2 * NK * H + (q + 1) * C]\
                        .rearrange("p a h -> p (a h)")
                    last = nc.tensor.matmul(py[k % 2], actt[k % 2][:, q * P:(q + 1) * P], w,
                                            start=(q == 0), stop=(q == NH - 1))
                last.then_inc(y_full, 1)

            def expert(i):
                return pe.value_load(tab[0:1, 0, bass.ds(i, 1)], min_val=0, max_val=E - 1)

            def tiles(i, first, last):
                e = None
                for k in range(XB):
                    t = i + k
                    e_before = expert(t - 1) if k == 0 and not first else e if k else None
                    e = expert(t)
                    if not (last and k == XB - 1):
                        turn_tile(t + 1, (k + 1) % XB)
                    pe.wait_ge(xgt_ready, t + 1)
                    if not (isinstance(t, int) and t < 2):
                        pe.wait_ge(silu_ready, t - 1)
                    hidden(t, k, e, 0, pg, gate_full)
                    if not (first and k == 0):
                        turn_act(t - 1, (k - 1) % XB)
                    hidden(t, k, e, NK * H, pu, up_full)
                    if not (first and k == 0):
                        down(t - 1, (k - 1) % XB, e_before)

            turn_tile(0, 0)
            tiles(0, True, False)
            with pe.Fori(XB, NT - XB, XB) as i:
                tiles(i, False, False)
            tiles(NT - XB, False, True)
            turn_act(NT - 1, XB - 1)
            down(NT - 1, XB - 1, expert(NT - 1))
    return nc


_INS = ['x', 'L0_tok_W_embed', 'L0_tok_b_embed', 'L0_tok_W_proj', 'L0_tok_b_proj', 'L0_attn_W_in', 'L0_attn_conv_w',
        'L0_attn_conv_b', 'L0_attn_W_xproj', 'L0_attn_w_dt', 'L0_attn_b_dt', 'L0_attn_A_log', 'L0_attn_D_param',
        'L0_attn_W_out', 'L0_ffn_w_gate', 'L0_ffn_wi', 'L0_ffn_wg', 'L0_ffn_wo']
_OUT = (64, 128, 256)


def kernel(**inputs):
    import numpy as _np
    import concourse.bacc as _bacc
    from concourse import mybir as _mybir
    from concourse.bass_utils import run_bass_kernel_spmd as _run

    nc = _bacc.Bacc("TRN2", target_bir_lowering=False, num_devices=1)
    arrays, args = {}, []
    for name in _INS:
        a = _np.ascontiguousarray(inputs[name])
        arrays[f"in_{name}_dram"] = a
        args.append(nc.dram_tensor(f"in_{name}_dram", a.shape, _mybir.dt.from_np(a.dtype), kind="ExternalInput").ap())
    args.append(nc.dram_tensor("out_0_dram", _OUT, _mybir.dt.from_np(_np.dtype("float32")), kind="ExternalOutput").ap())
    audio_tower(nc, *args)
    r = _run(nc, [arrays], core_ids=[0])
    return r.results[0]["out_0_dram"]
```

```python
from contextlib import ExitStack

import concourse.bass as bass
from concourse import mybir

ALU = mybir.AluOpType
ACT = mybir.ActivationFunctionType
AX_X = mybir.AxisListType.X
F32 = mybir.dt.float32
BF16 = mybir.dt.bfloat16
I32 = mybir.dt.int32
U32 = mybir.dt.uint32

P = 128


def audio_tower(nc, x, W_embed, b_embed, W_proj, b_proj, W_in, conv_w, conv_b, W_xproj, w_dt, b_dt, A_log,
                D_param, W_out, w_gate, wi, wg, wo, out):
    B, CI, L = x.shape
    CM, _, KW = W_embed.shape
    PAD = KW // 2
    T = W_proj.shape[0]
    DS = W_proj.shape[1] // CM
    C = L // DS
    WIN = DS + KW - 1
    KX = CI * WIN + 1
    DI = W_out.shape[0]
    NCH = DI // P
    NK = C // P
    S = A_log.shape[1]
    TAPS = conv_w.shape[2]
    R = 2 * S + 1
    E = w_gate.shape[1]
    H = wi.shape[2]
    NH = H // P
    GB = 4
    GT = GB * T
    G = B // GB
    NJ = DS * CM // P
    SPC = P // CM
    EPS = 1e-5
    ROW = C + 2
    TOKENS = B * T
    REG = TOKENS + P
    NT = -(-(2 * TOKENS // P + E - 1) // 4) * 4
    MW = 2 * NK * H + NH * C
    assert T == P and GT == 512 and C == 256 and NCH == 4 and G % 2 == 0 and S == 16 and H == 512

    rows_dram = nc.dram_tensor("expert_rows", [E * REG + P, ROW], F32).ap()

    with ExitStack() as ctx:
        def sb(name, shape, dt=F32):
            return ctx.enter_context(nc.sbuf_tensor(name, shape, dt))

        def sem(name):
            return ctx.enter_context(nc.semaphore(name))

        ident = sb("ident", [P, P])
        w_in_sb = sb("w_in_sb", [P, NK, 2 * DI])
        w_out_sb = sb("w_out_sb", [P, NCH, C])
        w_x3 = sb("w_x3", [P, NCH, 3 * R])
        w_gate_sb = sb("w_gate_sb", [P, NK, E])
        diag_d = sb("diag_d", [P, NCH, P])
        select = sb("select", [3 * R, R, P], BF16)
        w_eff = sb("w_eff", [KX, T])
        a_neg = sb("a_neg", [P, NCH, S])
        cw = sb("cw", [P, NCH, TAPS])
        cb = sb("cb", [P, NCH])
        wdt = sb("wdt", [P, NCH])
        bdt = sb("bdt", [P, NCH])
        dpar = sb("dpar", [P, NCH])
        below = sb("below", [P, P], BF16)
        ones_bf = sb("ones_bf", [P, P], BF16)
        key_w = sb("key_w", [P, GB, E])
        half = sb("half", [P, GB])
        ones_c = sb("ones_c", [P, 1])
        counts = sb("counts", [P, E])
        tokf = sb("tokf", [P, GB])
        SCN = NCH * GT
        arena = sb("arena", [P, E * MW])
        parts = {}
        at = 0
        for name, n in (("dA0", SCN), ("dA1", SCN), ("dBx0", SCN), ("dBx1", SCN), ("hc0", SCN), ("hc1", SCN),
                        ("state", SCN), ("delta0", SCN), ("delta1", SCN), ("u0", SCN), ("u1", SCN), ("xc", SCN)):
            parts[name] = arena[:, at:at + n].rearrange("p (c t) -> p c t", c=NCH)
            at += n
        assert at == E * MW
        dA = [parts["dA0"], parts["dA1"]]
        dBx = [parts["dBx0"], parts["dBx1"]]
        hc = [parts["hc0"], parts["hc1"]]
        state, xc = parts["state"], parts["xc"]
        delta = [parts["delta0"], parts["delta1"]]
        u = [parts["u0"], parts["u1"]]
        w_moe = arena[:, :].rearrange("p (e m) -> p e m", e=E)

        def flat(ap):
            return ap.rearrange("p c t -> p (c t)")

        z = sb("z", [P, NCH, GT])
        hnew = sb("hnew", [P, GB, C])
        hres = [sb(f"hres{i}", [P, GB, C]) for i in range(2)]
        bc3 = [sb(f"bc3_{i}", [3 * R, GT], BF16) for i in range(2)]
        b_rep = [sb(f"b_rep{i}", [P, GT]) for i in range(2)]
        xw = [sb(f"xw{i}", [P, GB, NK, KX]) for i in range(2)]
        xn = sb("xn", [P, GB, C])
        xnt = [sb(f"xnt{i}", [P, NK, GT]) for i in range(2)]
        tap = [[sb(f"tap{i}_{k}", [P, GB, T]) for k in range(TAPS)] for i in range(2)]
        xt = [tap[i][TAPS - 1][0:KX, :, :].rearrange("p b t -> p (b t)") for i in range(2)]
        soft = sb("soft", [P, NCH, GT])
        split = sb("split", [2 * R, GT])
        yz = soft
        h2 = sb("h2", [P, GB, C])
        row = [sb(f"row{i}", [P, GB, ROW]) for i in range(2)]
        xn2t = xn[:, :, :].rearrange("p (k b) c -> p k (b c)", k=NK)
        stat = sb("stat", [P, 2, GB, 6])
        mv = sb("mv", [P, 2, GB, 2])
        rstd = sb("rstd", [P, 2, GB])
        lmax = sb("lmax", [P, GB])
        ex = sb("ex", [P, GB, E])
        esum = sb("esum", [P, GB])
        einv = sb("einv", [P, GB])
        gates = sb("gates", [P, GB, E])
        g2 = sb("g2", [P, GB, E])
        m1 = sb("m1", [P, 2, GB])
        eq = sb("eq", [P, GB, E])
        key = sb("key", [P, GB, E])
        kmax = sb("kmax", [P, GB])
        oh = [sb(f"oh{i}", [P, GB, E]) for i in range(2)]
        mask = sb("mask", [P, GB, E], BF16)
        pos = sb("pos", [P, GB, E])
        slot_f = sb("slot_f", [P, 2, GB])
        slot = sb("slot", [P, 2, GB], U32)
        band = z[:, 0, 0:NJ * KX].rearrange("p (j k) -> p j k", j=NJ)
        e_last = z[0:1, 1, 0:KX]
        bp_row = z[0:1, 2, 0:T]
        wp_sb = z[:, 3, :]
        wpt = soft[:, 0, :].rearrange("p (j t) -> p j t", j=NJ)

        ne = sb("ne", [1, E])
        ebase = sb("ebase", [P, E])
        jlim = sb("jlim", [1, TOKENS // P])
        tile_no = sb("tile_no", [1, NT])
        cmp1 = z[0:1, 0, 0:E * (TOKENS // P)].rearrange("p (e j) -> p e j", e=E)
        cmp2 = z[0:1, :, :].rearrange("p c t -> p (c t)")[:, 0:NT * E].rearrange("p (i e) -> p i e", e=E)
        cmp3 = soft[0:1, :, :].rearrange("p c t -> p (c t)")[:, 0:NT * E].rearrange("p (i e) -> p i e", e=E)
        nt = sb("nt", [1, E])
        ones_e = sb("ones_e", [1, E])
        tend = sb("tend", [1, E])
        e_of, t_of, r_of, b_of = (hres[1][0:1, i, 0:NT] for i in range(4))
        tab = sb("tab", [1, 2, NT + 4], I32)
        pad_idx_f = sb("pad_idx_f", [P, E])
        pad_idx = sb("pad_idx", [P, E], U32)
        pad_row = sb("pad_row", [P, ROW])
        iota_p = sb("iota_p", [P, 1])
        XB = 4
        xg = [tap[i % 2][i // 2 * 2][:, :, :].rearrange("p b t -> p (b t)")[:, 0:ROW] for i in range(XB)]
        xgt = [xnt[0][:, i, 0:C] for i in range(2)]
        sg = [xn2t[:, i, :] for i in range(2)]
        act = [z[:, 2 + i, :] for i in range(2)]
        actt = [z[:, i, :] for i in range(2)]
        yt = [hres[0][:, i, :] for i in range(2)]
        tok_id = [sb(f"tok_id{i}", [P, 1], U32) for i in range(XB)]
        tok_w = [sb(f"tok_w{i}", [P, 1]) for i in range(XB)]

        psum = ctx.enter_context(nc.psum_tensor("psum", [P, 8, 512], F32))
        yacc = psum[:, 0:NCH, :]
        b_ps, c_ps = psum[:, 4, :], psum[:, 5, :]
        bank_a, bank_b = psum[:, 6, :], psum[:, 7, :]
        bank = [bank_a, bank_b]
        pg = [psum[:, 0, :], psum[:, 1, :]]
        pu = [psum[:, 2, :], psum[:, 3, :]]
        py = [psum[:, 4, 0:C], psum[:, 5, 0:C]]
        px, pt = psum[:, 6, :], psum[:, 7, :]

        s_par = sem("s_par")
        s_wts = sem("s_wts")
        s_band0 = sem("s_band0")
        s_const = sem("s_const")
        s_ctmp = sem("s_ctmp")
        s_zero = sem("s_zero")
        s_set = sem("s_set")
        s_aexp = sem("s_aexp")
        s_wpt = sem("s_wpt")
        s_wptc = sem("s_wptc")
        s_weff = sem("s_weff")
        s_weffc = sem("s_weffc")
        x_loaded = [sem(f"x_loaded{i}") for i in range(2)]
        tx_full = sem("tx_full")
        tx_free = sem("tx_free")
        emb_full = sem("emb_full")
        emb_free = sem("emb_free")
        h_moved = sem("h_moved")
        xnt_full = sem("xnt_full")
        xnt_free = sem("xnt_free")
        xi_full = sem("xi_full")
        xi_free = sem("xi_free")
        z_full = sem("z_full")
        z_free = sem("z_free")
        ssm_full = sem("ssm_full")
        draw_full = sem("draw_full")
        draw_free = sem("draw_free")
        stat_step = [sem(f"stat_step{i}") for i in range(2)]
        stat1 = sem("stat1")
        pow1 = sem("pow1")
        xn_ready = sem("xn_ready")
        conv_part = sem("conv_part")
        conv_ready = sem("conv_ready")
        xc_ready = sem("xc_ready")
        z_ready = sem("z_ready")
        hi_ready = sem("hi_ready")
        rest_ready = sem("rest_ready")
        mid_ready = sem("mid_ready")
        bc_ready = sem("bc_ready")
        sexp_ready = sem("sexp_ready")
        ln_ready = sem("ln_ready")
        delta_ready = sem("delta_ready")
        u_ready = sem("u_ready")
        b_full = sem("b_full")
        b_copied = sem("b_copied")
        c_full = sem("c_full")
        dA_ready = sem("dA_ready")
        dbx_dve = sem("dbx_dve")
        dbx_pool = sem("dbx_pool")
        scan_done = sem("scan_done")
        hc_ready = sem("hc_ready")
        skip_done = sem("skip_done")
        sum_done = sem("sum_done")
        yz_ready = sem("yz_ready")
        o_full = sem("o_full")
        h2_ready = sem("h2_ready")
        h2_stored = sem("h2_stored")
        stat2 = sem("stat2")
        pow2 = sem("pow2")
        row_ready = sem("row_ready")
        t_full = sem("t_full")
        xn2t_ready = sem("xn2t_ready")
        l_full = sem("l_full")
        lsub_ready = sem("lsub_ready")
        lexp_ready = sem("lexp_ready")
        mask_ready = sem("mask_ready")
        n_full = sem("n_full")
        slot_ready = sem("slot_ready")
        scattered = sem("scattered")
        rows_left = sem("rows_left")
        dv = sem("dv")
        w_loaded = sem("w_loaded")
        tab_ready = sem("tab_ready")
        pad_ready = sem("pad_ready")
        padded = sem("padded")
        tile_loaded = [sem(f"tile_loaded{i}") for i in range(XB)]
        xg_turned = sem("xg_turned")
        xgt_ready = sem("xgt_ready")
        meta_ready = sem("meta_ready")
        gate_full = sem("gate_full")
        up_full = sem("up_full")
        silu_ready = sem("silu_ready")
        act_ready = sem("act_ready")
        at_full = sem("at_full")
        actt_ready = sem("actt_ready")
        y_full = sem("y_full")
        y_ready = sem("y_ready")
        added = sem("added")

        N_PAR = 2 + DS + SPC + 6
        N_WTS = 6
        X_PER = 16 * 4 * GB
        ROUTER = 26
        ON_POOL = [1, 3, 5, 7, 9, 11, 13, 15]
        ON_DVE = [n for n in range(S) if n not in ON_POOL]
        NP_, ND_ = len(ON_POOL), len(ON_DVE)

        def gn(g, n):
            return (g + 1, n - S) if n >= S else (g, n)

        def ahead(eng, s, value):
            if not (isinstance(value, int) and value <= 0):
                eng.wait_ge(s, value)

        passed = {name: sem(f"passed_{name}") for name in ("pe", "dve", "pool", "sp")}

        def apart(eng, name):
            eng.sem_inc(passed[name], 1)

        block = ctx.enter_context(nc.Block())

        @block.sync
        def _(sp):
            sp.sem_inc(h2_stored, 16)
            sp.sem_inc(rows_left, 1)
            sp.dma_start(wp_sb, W_proj.rearrange("o c a -> o (c a)")).then_inc(s_par, 16)
            sp.dma_start(bp_row, b_proj.rearrange("(a o) -> a o", a=1)).then_inc(s_par, 16)
            sp.wait_ge(s_band0, 2)
            for s in range(DS):
                j, q = s // SPC, s % SPC
                dst = band[q * CM:(q + 1) * CM, j, 0:CI * WIN].rearrange("p (c w) -> p c w", c=CI)[:, :, s:s + KW]
                sp.dma_start(dst, W_embed).then_inc(s_par, 16)
            for q in range(SPC):
                sp.dma_start(band[q * CM:(q + 1) * CM, :, KX - 1:KX],
                             b_embed.rearrange("(c a b) -> c a b", a=1, b=1).broadcast_to([CM, NJ, 1]),
                             allow_slow_non_contiguous=True)\
                    .then_inc(s_par, 16)

            def load_x(g, par):
                ahead(sp, tx_full, 2 * (g - 1))
                apart(sp, "sp")

                for b in range(GB):
                    def win(first_row, rows_, cut, width):
                        at0 = first_row * DS - PAD + cut
                        src = x[bass.ds(g * GB + b, 1), :, at0:at0 + width]
                        return bass.AP(tensor=src.tensor, offset=src.offset,
                                       ap=[[DS, rows_], [L, CI], [1, width]])

                    def cell(k, p0, p1, cut, width):
                        return xw[par][p0:p1, b, k, 0:CI * WIN].rearrange("p (c w) -> p c w", c=CI)[:, :, cut:cut + width]

                    sp.dma_start(cell(0, 1, P, 0, WIN), win(1, P - 1, 0, WIN)).then_inc(x_loaded[par], 16)
                    sp.dma_start(cell(0, 0, 1, PAD, WIN - PAD), win(0, 1, PAD, WIN - PAD)).then_inc(x_loaded[par], 16)
                    sp.dma_start(cell(1, 0, P - 1, 0, WIN), win(P, P - 1, 0, WIN)).then_inc(x_loaded[par], 16)
                    sp.dma_start(cell(1, P - 1, P, 0, WIN - PAD), win(2 * P - 1, 1, 0, WIN - PAD))\
                        .then_inc(x_loaded[par], 16)

            def move_h(g, par):
                sp.wait_ge(emb_free, 2 * (g + 1))
                apart(sp, "sp")
                ahead(sp, h2_ready, 2 * (g - 1))
                sp.dma_start(hres[par][:, :, :], hnew[:, :, :]).then_inc(h_moved, 16)

            def store_h2(g):
                sp.wait_ge(h2_ready, 2 * g + 2)
                sp.dma_start(out[bass.ds(g * GB, GB), :, :].rearrange("b o l -> o b l"), h2[:, :, :])\
                    .then_inc(h2_stored, 16)

            sp.wait_ge(s_zero, 1)
            load_x(0, 0)
            sp.dma_start(w_in_sb[:, :, :], W_in.rearrange("(k p) n -> p k n", p=P)).then_inc(s_wts, 16)
            load_x(1, 1)

            def step(g, par, first, load, last):
                if load:
                    load_x(g + 2, par)
                if not last:
                    move_h(g + 1, 1 - par)
                if not first:
                    store_h2(g - 1)

            move_h(0, 0)
            step(0, 0, True, True, False)
            with sp.Fori(1, G - 3, 2) as g:
                step(g, 1, False, True, False)
                step(g + 1, 0, False, True, False)
            step(G - 3, 1, False, True, False)
            step(G - 2, 0, False, False, False)
            step(G - 1, 1, False, False, True)

            sp.wait_ge(sum_done, S * G)
            for e in range(E):
                gate_w = w_moe[:, e, 0:NK * H].rearrange("p (k h) -> p k h", k=NK)
                up_w = w_moe[:, e, NK * H:2 * NK * H].rearrange("p (k h) -> p k h", k=NK)
                down_w = w_moe[:, e, 2 * NK * H:].rearrange("p (k c) -> p k c", k=NH)
                sp.dma_start(gate_w, wg[e].rearrange("(k p) h -> p k h", p=P)).then_inc(w_loaded, 16)
                sp.dma_start(up_w, wi[e].rearrange("(k p) h -> p k h", p=P)).then_inc(w_loaded, 16)
                sp.dma_start(down_w, wo[e].rearrange("(k p) c -> p k c", p=P)).then_inc(w_loaded, 16)
            store_h2(G - 1)

            sp.wait_ge(tab_ready, 1)
            sp.wait_ge(padded, 16 * (E + 1))
            sp.wait_ge(scattered, 16 * 2 * GB * G)

            def load_tile(i, k, first):
                if not first:
                    sp.wait_ge(xg_turned, i - XB + 1)
                    sp.wait_ge(meta_ready, i - XB + 1)
                r = sp.value_load(tab[0:1, 1, bass.ds(i, 1)], min_val=0, max_val=E * REG)
                sp.dma_start(xg[k], rows_dram[bass.ds(r, P), :]).then_inc(tile_loaded[k], 16)

            for k in range(XB):
                load_tile(k, k, True)
            with sp.Fori(XB, NT, XB) as i:
                for k in range(XB):
                    load_tile(i + k, k, False)
            sp.wait_ge(h2_stored, 16 * (G + 1))
            sp.wait_ge(added, 16 * NT)

        @block.gpsimd
        def _(pool):
            pool.memset(ident[:, :], 0.0).then_inc(s_ctmp, 1)
            pool.memset(select[:, :, :], 0.0).then_inc(s_ctmp, 1)
            pool.memset(below[:, :], 1.0).then_inc(s_ctmp, 1)
            pool.wait_ge(s_ctmp, 3)
            pool.affine_select(out=ident[:, :], in_=ident[:, :], compare_op=ALU.not_equal, fill=1.0, base=0,
                               pattern=[[-1, P]], channel_multiplier=1).then_inc(s_const, 1)
            pool.affine_select(out=below[:, :], in_=below[:, :], compare_op=ALU.is_gt, fill=0.0, base=0,
                               pattern=[[1, P]], channel_multiplier=-1).then_inc(s_const, 1)
            for q in range(3):
                pool.affine_select(out=select[:, :, :], in_=select[:, :, :], compare_op=ALU.not_equal, fill=1.0,
                                   base=-q * R, pattern=[[-1, R], [0, P]], channel_multiplier=1).then_inc(s_ctmp, 1)
                pool.wait_ge(s_ctmp, 4 + q)
            pool.iota(key_w[:, :, :], pattern=[[0, GB], [-1, E]], base=E, channel_multiplier=0,
                      allow_small_or_imprecise_dtypes=True).then_inc(s_const, 1)
            pool.iota(ebase[:, :], pattern=[[REG, E]], base=0, channel_multiplier=0,
                      allow_small_or_imprecise_dtypes=True).then_inc(s_const, 1)
            pool.iota(jlim[:, :], pattern=[[P, TOKENS // P]], base=0, channel_multiplier=0,
                      allow_small_or_imprecise_dtypes=True).then_inc(s_const, 1)
            pool.iota(tile_no[:, :], pattern=[[1, NT]], base=0, channel_multiplier=0,
                      allow_small_or_imprecise_dtypes=True).then_inc(s_const, 1)
            pool.iota(iota_p[:, :], pattern=[[0, 1]], base=0, channel_multiplier=1,
                      allow_small_or_imprecise_dtypes=True).then_inc(s_const, 1)
            pool.iota(tokf[:, :], pattern=[[P, GB]], base=0, channel_multiplier=1,
                      allow_small_or_imprecise_dtypes=True).then_inc(s_const, 1)
            pool.memset(half[:, :], -0.5).then_inc(s_const, 1)
            pool.memset(ones_bf[:, :], 1.0).then_inc(s_const, 1)

            def rsqrt(g, which, ready, done):
                pool.wait_ge(ready, g + 1)
                pool.tensor_tensor(rstd[:, which, :], mv[:, which, :, 1], half[:, :], ALU.pow).then_inc(done, 1)

            def conv(g, c):
                t = tap[c % 2]
                if c == 0:
                    ahead(pool, skip_done, g)
                    ahead(pool, u_ready, g)
                pool.wait_ge(xi_free, NCH * g + c + 1)
                dst = xc[:, c, :].rearrange("p (b t) -> p b t", b=GB)
                pool.tensor_tensor(dst, t[3][:, :, :], t[2][:, :, :], ALU.add).then_inc(conv_part, 1)
                pool.wait_ge(conv_part, 2 * (NCH * g + c) + 1)
                pool.tensor_tensor(dst, dst, t[1][:, :, :], ALU.add).then_inc(conv_part, 1)
                pool.wait_ge(conv_part, 2 * (NCH * g + c) + 2)
                pool.tensor_tensor(dst, dst, t[0][:, :, :], ALU.add).then_inc(conv_ready, 1)

            def add_delta(g, par):
                pool.wait_ge(ln_ready, g + 1)
                pool.tensor_tensor(delta[par], delta[par], soft[:, :, :], ALU.add).then_inc(delta_ready, 1)

            def make_dbx(g, n, par):
                k = ON_POOL.index(n)
                if k == 0:
                    pool.wait_ge(u_ready, g + 1)
                ahead(pool, scan_done, S * g + n - 1)
                pool.wait_ge(b_copied, NP_ * g + k + 1)
                rep = b_rep[(NP_ * par + k) % 2][:, :].rearrange("p (a t) -> p a t", a=1)
                pool.tensor_tensor(dBx[n % 2], u[par], rep.broadcast_to([P, NCH, GT]), ALU.mult).then_inc(dbx_pool, 1)

            def scatter(g):
                pool.wait_ge(slot_ready, g + 1)
                apart(pool, "pool")
                for k in range(2):
                    for b in range(GB):
                        pool.indirect_dma_start(
                            out=rows_dram[:, :], out_offset=bass.IndirectOffsetOnAxis(ap=slot[:, k, b:b + 1], axis=0),
                            in_=row[k][:, b, :], in_offset=None).then_inc(scattered, 16)
                pool.wait_ge(scattered, 16 * 2 * GB * (g + 1))
                pool.sem_inc(rows_left, 1)

            def front(g, par):
                rsqrt(g, 0, stat1, pow1)
                for c in range(NCH):
                    conv(g, c)
                add_delta(g, par)

            def step(g, par, first, last):
                for n in range(S):
                    if n == 4 and not first:
                        rsqrt(g - 1, 1, stat2, pow2)
                    if n + 1 in ON_POOL:
                        make_dbx(g, n + 1, par)
                    if n == 1 and not last:
                        rsqrt(g + 1, 0, stat1, pow1)
                    if n in (5, 6, 7, 8) and not last:
                        conv(g + 1, n - 5)
                    if n == 13 and not last:
                        add_delta(g + 1, 1 - par)
                    if n == 15 and not first:
                        scatter(g - 1)

            front(0, 0)
            step(0, 0, True, False)
            with pool.Fori(1, G - 1, 2) as g:
                step(g, 1, False, False)
                step(g + 1, 0, False, False)
            step(G - 1, 1, False, True)
            rsqrt(G - 1, 1, stat2, pow2)
            scatter(G - 1)

            pool.wait_ge(pad_ready, 1)
            pool.dma_start(rows_dram[E * REG:E * REG + P, :], pad_row[:, :]).then_inc(padded, 16)
            for e in range(E):
                pool.indirect_dma_start(
                    out=rows_dram[:, :], out_offset=bass.IndirectOffsetOnAxis(ap=pad_idx[:, e:e + 1], axis=0),
                    in_=pad_row[:, :], in_offset=None).then_inc(padded, 16)

            pool.wait_ge(h2_stored, 16 * (G + 1))

            def add_tile(i, k, first):
                pool.wait_ge(y_ready, i + 1)
                if not first:
                    pool.wait_ge(added, 16 * i)
                apart(pool, "pool")
                pool.indirect_dma_start(
                    out=out.rearrange("b o l -> (b o) l"),
                    out_offset=bass.IndirectOffsetOnAxis(ap=tok_id[k][:, 0:1], axis=0), in_=yt[k % 2],
                    in_offset=None, bounds_check=TOKENS - 1, oob_is_err=False, compute_op=ALU.add).then_inc(added, 16)

            for k in range(XB):
                add_tile(k, k, k == 0)
            with pool.Fori(XB, NT, XB) as i:
                for k in range(XB):
                    add_tile(i + k, k, False)

        @block.scalar
        def _(actq):
            actq.dma_start(a_neg[:, :, :], A_log.rearrange("(c p) s -> p c s", p=P)).then_inc(s_par, 16)
            for dst, src in ((cb, conv_b), (wdt, w_dt), (bdt, b_dt), (dpar, D_param)):
                actq.dma_start(dst[:, :], src.rearrange("(c p) -> p c", p=P), allow_slow_non_contiguous=True)\
                    .then_inc(s_par, 16)
            actq.dma_start(cw[:, :, :], conv_w.rearrange("(c p) a k -> p c (a k)", p=P)).then_inc(s_par, 16)
            for q in range(3):
                actq.dma_start(w_x3[:, :, q * R:(q + 1) * R], W_xproj.rearrange("(c p) r -> p c r", p=P))\
                    .then_inc(s_wts, 16)
            actq.dma_start(w_out_sb[:, :, :], W_out.rearrange("(c p) n -> p c n", p=P)).then_inc(s_wts, 16)
            actq.dma_start(w_gate_sb[:, :, :], w_gate.rearrange("(k p) n -> p k n", p=P)).then_inc(s_wts, 16)
            actq.wait_ge(s_par, 16 * N_PAR)
            actq.activation(a_neg[:, :, :], a_neg[:, :, :], ACT.Exp).then_inc(s_aexp, 1)
            actq.wait_ge(s_wpt, 1)
            actq.activation(wpt.rearrange("p j t -> p (j t)"), bank_a, ACT.Copy).then_inc(s_wptc, 1)
            actq.wait_ge(s_weff, 1)
            actq.activation(w_eff[:, :], bank_b[0:KX, 0:T], ACT.Copy).then_inc(s_weffc, 1)

            def evac_xt(g, m):
                actq.wait_ge(tx_full, 2 * g + m + 1)
                ahead(actq, conv_ready, NCH * g)
                nc.scalar.activation(xt[m], bank[m][0:KX, :], ACT.Copy).then_inc(tx_free, 1)

            def evac_h(g, m):
                actq.wait_ge(emb_full, 2 * g + m + 1)
                if m == 0:
                    ahead(actq, h_moved, 16 * g)
                    ahead(actq, xn_ready, g)
                dst = hnew[:, 2 * m:2 * m + 2, :].rearrange("p b c -> p (b c)")
                nc.scalar.activation(dst, bank[m], ACT.Copy).then_inc(emb_free, 1)

            def evac_xnt(g, par, k):
                actq.wait_ge(xnt_full, NK * g + k + 1)
                nc.scalar.activation(xnt[par][:, k, :], bank[k], ACT.Copy).then_inc(xnt_free, 1)

            def taps(g, c):
                actq.wait_ge(xi_full, NCH * g + c + 1)
                ahead(actq, conv_ready, NCH * g + c - 1)
                src = bank_a.rearrange("p (b t) -> p b t", b=GB)
                for k in range(TAPS):
                    d = TAPS - 1 - k
                    if d == 0:
                        nc.scalar.activation(tap[c % 2][k][:, :, :], src, ACT.Identity, scale=cw[:, c, k:k + 1],
                                             bias=cb[:, c:c + 1]).then_inc(xi_free, 1)
                    else:
                        nc.scalar.activation(tap[c % 2][k][:, :, d:T], src[:, :, 0:T - d], ACT.Copy,
                                             scale=cw[:, c, k:k + 1])

            def evac_z(g, c):
                actq.wait_ge(z_full, NCH * g + c + 1)
                if c == 0:
                    ahead(actq, yz_ready, g)
                nc.scalar.activation(z[:, c, :], bank[c // 2], ACT.Copy).then_inc(z_free, 1)

            def silu_x(g):
                actq.wait_ge(conv_ready, NCH * (g + 1))
                nc.scalar.activation(xc, xc, ACT.Silu).then_inc(xc_ready, 1)

            def silu_z(g):
                actq.wait_ge(z_free, NCH * (g + 1))
                nc.scalar.activation(z[:, :, :], z[:, :, :], ACT.Silu).then_inc(z_ready, 1)

            def split_hi(g, par):
                actq.wait_ge(ssm_full, g + 1)
                ahead(actq, c_full, S * (g - 1))
                nc.scalar.activation(bc3[par][:, :], bank_a[0:3 * R, :], ACT.Copy).then_inc(hi_ready, 1)

            def split_mid(g, par):
                actq.wait_ge(rest_ready, g + 1)
                nc.scalar.activation(bc3[par][0:2 * R, :], split[:, :], ACT.Copy).then_inc(mid_ready, 1)

            def softplus_in(g, par):
                actq.wait_ge(draw_full, g + 1)
                ahead(actq, o_full, 2 * (g - 1))
                ahead(actq, delta_ready, g)
                for c in range(NCH):
                    nc.scalar.activation(soft[:, c, :], bank_a, ACT.Abs, scale=wdt[:, c:c + 1], bias=bdt[:, c:c + 1])
                    last = nc.scalar.activation(delta[par][:, c, :], bank_a, ACT.Relu, scale=wdt[:, c:c + 1],
                                                bias=bdt[:, c:c + 1])
                last.then_inc(draw_free, 1)

            def softplus_out(g):
                actq.wait_ge(draw_free, g + 1)
                nc.scalar.activation(soft[:, :, :], soft[:, :, :], ACT.Exp, scale=-1.0).then_inc(sexp_ready, 1)
                actq.wait_ge(sexp_ready, g + 1)
                nc.scalar.activation(soft[:, :, :], soft[:, :, :], ACT.Ln, bias=1.0).then_inc(ln_ready, 1)

            def copy_b(g, n, par):
                k = ON_POOL.index(n)
                actq.wait_ge(b_full, S * g + n + 1)
                ahead(actq, dbx_pool, NP_ * g + k - 1)
                nc.scalar.activation(b_rep[(NP_ * par + k) % 2][:, :], b_ps, ACT.Copy).then_inc(b_copied, 1)

            def exps(g, n, par):
                if n == 0:
                    actq.wait_ge(delta_ready, g + 1)
                ahead(actq, scan_done, S * g + n - 1)
                for c in range(NCH):
                    o = dA[n % 2][:, c, :].rearrange("p (b t) -> p b t", b=GB)[:, :, 1:T]
                    i = delta[par][:, c, :].rearrange("p (b t) -> p b t", b=GB)[:, :, 1:T]
                    last = nc.scalar.activation(o, i, ACT.Exp, scale=a_neg[:, c, n:n + 1])
                last.then_inc(dA_ready, 1)

            def evac_xn2t(g, k):
                actq.wait_ge(t_full, NK * g + k + 1)
                nc.scalar.activation(xn2t[:, k, :], bank_b, ACT.Copy).then_inc(xn2t_ready, 1)

            def router_exp(g):
                actq.wait_ge(lsub_ready, g + 1)
                nc.scalar.activation(ex[:, :, :], ex[:, :, :], ACT.Exp).then_inc(lexp_ready, 1)

            def front(g, par):
                for m in range(2):
                    evac_xt(g, m)
                for m in range(2):
                    evac_h(g, m)
                for k in range(NK):
                    evac_xnt(g, par, k)
                for c in range(NCH):
                    taps(g, c)
                silu_x(g)
                split_hi(g, par)
                split_mid(g, par)
                softplus_in(g, par)
                softplus_out(g)
                for m in range(2):
                    evac_xt(g + 1, m)

            def step(g, par, first, more, last):
                for n in range(S):
                    g2, n2 = gn(g, n + 2)
                    if not (last and n2 < 2):
                        exps(g2, n2, par if n2 >= 2 else 1 - par)
                        if n2 in ON_POOL:
                            copy_b(g2, n2, par if n2 >= 2 else 1 - par)
                    if not last:
                        if n == 0:
                            evac_h(g + 1, 0)
                            evac_h(g + 1, 1)
                        if n == 3:
                            evac_xnt(g + 1, 1 - par, 0)
                            evac_xnt(g + 1, 1 - par, 1)
                        if n in (4, 5, 6, 7):
                            taps(g + 1, n - 4)
                        if n == 8:
                            silu_x(g + 1)
                            silu_z(g)
                        if n == 9:
                            split_hi(g + 1, 1 - par)
                        if n == 10:
                            split_mid(g + 1, 1 - par)
                        if n == 12:
                            softplus_in(g + 1, 1 - par)
                            softplus_out(g + 1)
                    if n in (1, 2):
                        evac_z(g, n - 1)
                    if n in (4, 5):
                        evac_z(g, n - 2)
                    if last and n == 8:
                        silu_z(g)
                    if not first:
                        if n in (6, 7):
                            evac_xn2t(g - 1, n - 6)
                        if n == 9:
                            router_exp(g - 1)
                    if more and n == 14:
                        evac_xt(g + 2, 0)
                        evac_xt(g + 2, 1)

            actq.wait_ge(s_zero, 2)
            actq.wait_ge(s_set, 6 + NCH + 1)
            front(0, 0)
            exps(0, 0, 0)
            exps(0, 1, 0)
            copy_b(0, 1, 0)
            step(0, 0, True, True, False)
            with actq.Fori(1, G - 3, 2) as g:
                step(g, 1, False, True, False)
                step(g + 1, 0, False, True, False)
            step(G - 3, 1, False, True, False)
            step(G - 2, 0, False, False, False)
            step(G - 1, 1, False, False, True)
            evac_xn2t(G - 1, 0)
            evac_xn2t(G - 1, 1)
            router_exp(G - 1)

            def evac_x(i, k):
                actq.wait_ge(xg_turned, i + 1)
                if not (isinstance(i, int) and i < 2):
                    actq.wait_ge(up_full, i - 1)
                nc.scalar.activation(xgt[k % 2], px[:, 0:C], ACT.Copy).then_inc(xgt_ready, 1)

            def silu(i, k):
                actq.wait_ge(gate_full, i + 1)
                if not (isinstance(i, int) and i < 2):
                    actq.wait_ge(act_ready, i - 1)
                nc.scalar.activation(sg[k % 2], pg[k % 2], ACT.Silu).then_inc(silu_ready, 1)

            def weigh(i, k):
                actq.wait_ge(y_full, i + 1)
                actq.wait_ge(meta_ready, i + 1)
                if not (isinstance(i, int) and i < 2):
                    actq.wait_ge(added, 16 * (i - 1))
                nc.scalar.activation(yt[k % 2], py[k % 2], ACT.Copy, scale=tok_w[k][:, 0:1]).then_inc(y_ready, 1)

            def tiles(i, first, last):
                for k in range(XB):
                    if not (last and k == XB - 1):
                        evac_x(i + k + 1, (k + 1) % XB)
                    silu(i + k, k)
                    if not (first and k == 0):
                        weigh(i + k - 1, (k - 1) % XB)

            evac_x(0, 0)
            tiles(0, True, False)
            with actq.Fori(XB, NT - XB, XB) as i:
                tiles(i, False, False)
            tiles(NT - XB, False, True)
            weigh(NT - 1, XB - 1)

        @block.vector
        def _(dve):
            dve.memset(band, 0.0).then_inc(s_band0, 1)
            dve.memset(e_last, 0.0).then_inc(s_band0, 1)
            dve.wait_ge(s_band0, 2)
            dve.memset(e_last[:, KX - 1:KX], 1.0).then_inc(s_set, 1)
            for i in range(2):
                dve.memset(xw[i][:, :, :, :], 0.0).then_inc(s_set, 1)
            dve.wait_ge(s_set, 3)
            dve.memset(xw[0][:, :, :, KX - 1:KX], 1.0)
            dve.memset(xw[1][:, :, :, KX - 1:KX], 1.0).then_inc(s_zero, 1)
            for i in range(2):
                for k in range(TAPS - 1):
                    dve.memset(tap[i][k][:, :, 0:TAPS - 1 - k], 0.0)
                for c in range(NCH):
                    last = dve.memset(dA[i][:, c, :].rearrange("p (b t) -> p b t", b=GB)[:, :, 0:1], 0.0)
            last.then_inc(s_zero, 1)
            dve.memset(pad_row[:, :], 0.0).then_inc(s_set, 1)
            dve.memset(ones_e[:, :], 1.0)
            dve.wait_ge(s_set, 4)
            dve.memset(pad_row[:, C:C + 1].bitcast(I32), TOKENS).then_inc(s_set, 1)
            dve.wait_ge(s_par, 16 * N_PAR)
            dve.wait_ge(s_aexp, 1)
            dve.tensor_scalar(a_neg[:, :, :], a_neg[:, :, :], -1.0, None, ALU.mult).then_inc(s_set, 1)
            dve.wait_ge(s_const, 10)
            for c in range(NCH):
                dve.tensor_scalar(diag_d[:, c, :], ident[:, :], dpar[:, c:c + 1], None, ALU.mult).then_inc(s_set, 1)
            dve.tensor_copy(counts[:, :], ebase[:, :]).then_inc(s_set, 1)
            dve.wait_ge(s_set, 6 + NCH + 1)

            def stats(g, which, src, ready):
                for b in range(GB):
                    ins = nc.vector.bn_stats(stat[:, which, b, :], src[:, b, :])
                ins.then_inc(stat_step[which], 1)
                dve.wait_ge(stat_step[which], 2 * g + 1)
                apart(dve, "dve")
                for b in range(GB):
                    ins = nc.vector.bn_aggr(mv[:, which, b, :], stat[:, which, b, :])
                ins.then_inc(stat_step[which], 1)
                dve.wait_ge(stat_step[which], 2 * g + 2)
                nc.vector.tensor_scalar(mv[:, which, :, 1], mv[:, which, :, 1], EPS, None, ALU.add).then_inc(ready, 1)

            def norm1_stats(g):
                dve.wait_ge(emb_free, 2 * (g + 1))
                stats(g, 0, hnew, stat1)

            def norm1(g):
                dve.wait_ge(pow1, g + 1)
                ahead(dve, xnt_full, NK * g)
                for b in range(GB):
                    last = nc.vector.tensor_scalar(xn[:, b, :], hnew[:, b, :], mv[:, 0, b, 0:1],
                                                   rstd[:, 0, b:b + 1], ALU.subtract, ALU.mult)
                last.then_inc(xn_ready, 1)

            def split_rest(g, par):
                dve.wait_ge(hi_ready, g + 1)
                nc.vector.tensor_tensor(split[:, :], bank_a[0:2 * R, :], bc3[par][0:2 * R, :], ALU.subtract)\
                    .then_inc(rest_ready, 1)

            def split_lo(g, par):
                dve.wait_ge(mid_ready, g + 1)
                nc.vector.tensor_tensor(bc3[par][0:R, :], split[0:R, :], bc3[par][0:R, :], ALU.subtract)\
                    .then_inc(bc_ready, 1)

            def make_u(g, par):
                dve.wait_ge(delta_ready, g + 1)
                dve.wait_ge(xc_ready, g + 1)
                nc.vector.tensor_tensor(u[par], delta[par], xc, ALU.mult).then_inc(u_ready, 1)

            def make_dbx(g, n, par):
                k = ON_DVE.index(n)
                if k == 0:
                    dve.wait_ge(u_ready, g + 1)
                ahead(dve, scan_done, S * g + n - 1)
                dve.wait_ge(b_full, S * g + n + 1)
                rep = b_ps.rearrange("p (a t) -> p a t", a=1)
                nc.vector.tensor_tensor(dBx[n % 2], u[par], rep.broadcast_to([P, NCH, GT]), ALU.mult)\
                    .then_inc(dbx_dve, 1)

            def scan(g, n):
                dve.wait_ge(dA_ready, S * g + n + 1)
                if n in ON_POOL:
                    dve.wait_ge(dbx_pool, NP_ * g + ON_POOL.index(n) + 1)
                else:
                    dve.wait_ge(dbx_dve, ND_ * g + ON_DVE.index(n) + 1)
                ahead(dve, hc_ready, S * g + n)
                nc.vector.tensor_tensor_scan(flat(state), flat(dA[n % 2]), flat(dBx[n % 2]), 0.0,
                                             ALU.mult, ALU.add).then_inc(scan_done, 1)

            def times_c(g, n):
                dve.wait_ge(scan_done, S * g + n + 1)
                dve.wait_ge(c_full, S * g + n + 1)
                ahead(dve, sum_done, S * g + n - 1)
                rep = c_ps.rearrange("p (a t) -> p a t", a=1)
                nc.vector.tensor_tensor(hc[n % 2], state, rep.broadcast_to([P, NCH, GT]), ALU.mult)\
                    .then_inc(hc_ready, 1)

            def gate_y(g):
                dve.wait_ge(sum_done, S * (g + 1))
                dve.wait_ge(z_ready, g + 1)
                dve.wait_ge(delta_ready, min(g + 2, G) if isinstance(g, int) else g + 2)
                nc.vector.tensor_tensor(yz[:, :, :], yacc, z[:, :, :], ALU.mult).then_inc(yz_ready, 1)

            def residual(g, par, m):
                dve.wait_ge(o_full, 2 * g + m + 1)
                if m == 0:
                    dve.wait_ge(h_moved, 16 * (g + 1))
                    dve.wait_ge(h2_stored, 16 * (g + 1))
                dst = h2[:, 2 * m:2 * m + 2, :].rearrange("p b c -> p (b c)")
                src = hres[par][:, 2 * m:2 * m + 2, :].rearrange("p b c -> p (b c)")
                nc.vector.tensor_tensor(dst, bank_b, src, ALU.add).then_inc(h2_ready, 1)

            def norm2_stats(g):
                dve.wait_ge(h2_ready, 2 * g + 2)
                stats(g, 1, h2, stat2)

            def norm2(g):
                dve.wait_ge(pow2, g + 1)
                dve.wait_ge(rows_left, g + 1)
                for k in range(2):
                    for b in range(GB):
                        last = nc.vector.tensor_scalar(row[k][:, b, 0:C], h2[:, b, :], mv[:, 1, b, 0:1],
                                                       rstd[:, 1, b:b + 1], ALU.subtract, ALU.mult)
                last.then_inc(row_ready, 1)

            def after(g, k):
                dve.wait_ge(dv, ROUTER * g + k)

            def bc(ap):
                return ap.rearrange("p (b a) -> p b a", a=1).broadcast_to([P, GB, E])

            def router_a(g):
                dve.wait_ge(l_full, g + 1)
                logits = bank_b[:, 0:GB * E].rearrange("p (b e) -> p b e", b=GB)
                nc.vector.tensor_reduce(lmax[:, :], logits, AX_X, ALU.max).then_inc(dv, 1)
                after(g, 1)
                nc.vector.tensor_tensor(ex[:, :, :], logits, bc(lmax[:, :]), ALU.subtract).then_inc(lsub_ready, 1)

            def router_b(g):
                dve.wait_ge(lexp_ready, g + 1)
                nc.vector.tensor_reduce(esum[:, :], ex[:, :, :], AX_X, ALU.add).then_inc(dv, 1)
                after(g, 2)
                nc.vector.reciprocal(einv[:, :], esum[:, :]).then_inc(dv, 1)
                after(g, 3)
                nc.vector.tensor_tensor(gates[:, :, :], ex[:, :, :], bc(einv[:, :]), ALU.mult).then_inc(dv, 1)
                n = 4
                for k, src in ((0, gates), (1, g2)):
                    after(g, n)
                    nc.vector.tensor_reduce(m1[:, k, :], src[:, :, :], AX_X, ALU.max).then_inc(dv, 1)
                    after(g, n + 1)
                    nc.vector.tensor_tensor(eq[:, :, :], src[:, :, :], bc(m1[:, k, :]), ALU.is_equal).then_inc(dv, 1)
                    after(g, n + 2)
                    nc.vector.tensor_tensor(key[:, :, :], eq[:, :, :], key_w[:, :, :], ALU.mult).then_inc(dv, 1)
                    after(g, n + 3)
                    nc.vector.tensor_reduce(kmax[:, :], key[:, :, :], AX_X, ALU.max).then_inc(dv, 1)
                    after(g, n + 4)
                    nc.vector.tensor_tensor(oh[k][:, :, :], key[:, :, :], bc(kmax[:, :]), ALU.is_equal).then_inc(dv, 1)
                    n += 5
                    if k == 0:
                        after(g, n)
                        nc.vector.scalar_tensor_tensor(out=g2[:, :, :], in0=oh[0][:, :, :], scalar=-2.0,
                                                       in1=gates[:, :, :], op0=ALU.mult, op1=ALU.add).then_inc(dv, 1)
                        n += 1
                after(g, n)
                nc.vector.tensor_tensor(mask[:, :, :], oh[0][:, :, :], oh[1][:, :, :], ALU.add).then_inc(mask_ready, 1)
                for k in range(2):
                    nc.vector.tensor_copy(row[k][:, :, C:C + 1].bitcast(I32),
                                          tokf[:, :].rearrange("p (b a) -> p b a", a=1)).then_inc(dv, 1)
                    nc.vector.tensor_copy(row[k][:, :, C + 1:C + 2],
                                          m1[:, k, :].rearrange("p (b a) -> p b a", a=1)).then_inc(dv, 1)
                n += 4
                after(g, n)
                nc.vector.tensor_scalar(tokf[:, :], tokf[:, :], float(GT), None, ALU.add).then_inc(dv, 1)
                assert n + 1 == 20

            def router_c(g):
                dve.wait_ge(n_full, g + 1)
                earlier = bank_b[:, 0:GB * E].rearrange("p (b e) -> p b e", b=GB)
                cb_ = counts[:, :].rearrange("p (a e) -> p a e", a=1).broadcast_to([P, GB, E])
                nc.vector.tensor_tensor(pos[:, :, :], earlier, cb_, ALU.add).then_inc(dv, 1)
                after(g, 21)
                nc.vector.tensor_tensor(counts[:, :], counts[:, :], bank_b[:, GB * E:(GB + 1) * E], ALU.add)\
                    .then_inc(dv, 1)
                n = 22
                for k in range(2):
                    nc.vector.tensor_tensor(eq[:, :, :], oh[k][:, :, :], pos[:, :, :], ALU.mult).then_inc(dv, 1)
                    after(g, n + 1)
                    nc.vector.tensor_reduce(slot_f[:, k, :], eq[:, :, :], AX_X, ALU.add).then_inc(dv, 1)
                    n += 2
                    after(g, n)
                nc.vector.tensor_copy(slot[:, :, :], slot_f[:, :, :]).then_inc(slot_ready, 1)

            def front(g, par):
                norm1_stats(g)
                norm1(g)
                split_rest(g, par)
                split_lo(g, par)
                make_u(g, par)

            def step(g, par, first, last):
                for n in range(S):
                    if n == 0 and not first:
                        gate_y(g - 1)
                    scan(g, n)
                    if n + 1 in ON_DVE:
                        make_dbx(g, n + 1, par)
                    if not last:
                        if n == 1:
                            norm1_stats(g + 1)
                        if n == 2:
                            norm1(g + 1)
                        if n == 10:
                            split_rest(g + 1, 1 - par)
                        if n == 11:
                            split_lo(g + 1, 1 - par)
                        if n == 15:
                            make_u(g + 1, 1 - par)
                    if n == 5 and not first:
                        norm2(g - 1)
                    times_c(g, n)
                    if n == 15 and not last:
                        make_dbx(g + 1, 0, 1 - par)
                    if not first:
                        if n in (1, 2):
                            residual(g - 1, 1 - par, n - 1)
                        if n == 3:
                            norm2_stats(g - 1)
                        if n == 8:
                            router_a(g - 1)
                        if n == 10:
                            router_b(g - 1)
                        if n == 12:
                            router_c(g - 1)

            front(0, 0)
            make_dbx(0, 0, 0)
            step(0, 0, True, False)
            with dve.Fori(1, G - 1, 2) as g:
                step(g, 1, False, False)
                step(g + 1, 0, False, False)
            step(G - 1, 1, False, True)
            gate_y(G - 1)
            residual(G - 1, 1, 0)
            residual(G - 1, 1, 1)
            norm2_stats(G - 1)
            norm2(G - 1)
            router_a(G - 1)
            router_b(G - 1)
            router_c(G - 1)

            base = ROUTER * G
            dve.wait_ge(slot_ready, G)
            nc.vector.tensor_scalar(pad_idx_f[:, :], counts[:, :], iota_p[:, 0:1], None, ALU.add).then_inc(dv, 1)
            dve.wait_ge(dv, base + 1)
            nc.vector.tensor_copy(pad_idx[:, :], pad_idx_f[:, :]).then_inc(pad_ready, 1)
            nc.vector.tensor_tensor(ne[:, :], counts[0:1, :], ebase[0:1, :], ALU.subtract).then_inc(dv, 1)
            dve.wait_ge(dv, base + 2)
            J = TOKENS // P
            ne_b = ne[:, :].rearrange("p (e a) -> p e a", a=1).broadcast_to([1, E, J])
            jl_b = jlim[:, :].rearrange("p (a j) -> p a j", a=1).broadcast_to([1, E, J])
            nc.vector.tensor_tensor(cmp1, ne_b, jl_b, ALU.is_gt).then_inc(dv, 1)
            dve.wait_ge(dv, base + 3)
            nc.vector.tensor_reduce(nt[:, :], cmp1, AX_X, ALU.add).then_inc(dv, 1)
            dve.wait_ge(dv, base + 4)
            nc.vector.tensor_tensor_scan(tend[:, :], ones_e[:, :], nt[:, :], 0.0, ALU.mult, ALU.add).then_inc(dv, 1)
            dve.wait_ge(dv, base + 5)
            te_b = tend[:, :].rearrange("p (a e) -> p a e", a=1).broadcast_to([1, NT, E])
            nt_b = nt[:, :].rearrange("p (a e) -> p a e", a=1).broadcast_to([1, NT, E])
            no_b = tile_no[:, :].rearrange("p (i a) -> p i a", a=1).broadcast_to([1, NT, E])
            nc.vector.tensor_tensor(cmp2, te_b, no_b, ALU.is_le).then_inc(dv, 1)
            dve.wait_ge(dv, base + 6)
            nc.vector.tensor_reduce(e_of, cmp2, AX_X, ALU.add).then_inc(dv, 1)
            nc.vector.tensor_tensor(cmp3, cmp2, nt_b, ALU.mult).then_inc(dv, 1)
            dve.wait_ge(dv, base + 8)
            nc.vector.tensor_reduce(t_of, cmp3, AX_X, ALU.add).then_inc(dv, 1)
            dve.wait_ge(dv, base + 9)
            nc.vector.tensor_tensor(r_of, tile_no[:, :], t_of, ALU.subtract).then_inc(dv, 1)
            nc.vector.tensor_scalar(b_of, e_of, float(REG), None, ALU.mult).then_inc(dv, 1)
            dve.wait_ge(dv, base + 11)
            nc.vector.scalar_tensor_tensor(out=r_of, in0=r_of, scalar=float(P), in1=b_of,
                                           op0=ALU.mult, op1=ALU.add).then_inc(dv, 1)
            dve.wait_ge(dv, base + 12)
            nc.vector.tensor_scalar(tab[:, 1, 0:NT], r_of, float(E * REG), None, ALU.min).then_inc(dv, 1)
            nc.vector.tensor_scalar(tab[:, 0, 0:NT], e_of, float(E - 1), None, ALU.min).then_inc(dv, 1)
            dve.wait_ge(dv, base + 14)
            dve.sem_inc(tab_ready, 1)

            def meta(i, k):
                dve.wait_ge(tile_loaded[k], (16 * (i // XB + 1)) if isinstance(i, int) else (i - k) * (16 // XB) + 16)
                if not (isinstance(i, int) and i < XB):
                    dve.wait_ge(added, 16 * (i - XB + 1))
                nc.vector.tensor_copy(tok_id[k][:, :], xg[k][:, C:C + 1].bitcast(U32))
                nc.vector.tensor_copy(tok_w[k][:, :], xg[k][:, C + 1:C + 2]).then_inc(meta_ready, 1)

            def gated(i, k):
                dve.wait_ge(silu_ready, i + 1)
                dve.wait_ge(up_full, i + 1)
                if not (isinstance(i, int) and i < 2):
                    dve.wait_ge(at_full, i - 1)
                nc.vector.tensor_tensor(act[k % 2], pu[k % 2], sg[k % 2], ALU.mult).then_inc(act_ready, 1)

            def evac_at(i, k):
                dve.wait_ge(at_full, i + 1)
                if not (isinstance(i, int) and i < 2):
                    dve.wait_ge(y_full, i - 1)
                nc.vector.tensor_copy(actt[k % 2], pt).then_inc(actt_ready, 1)

            def tiles(i, first, last):
                for k in range(XB):
                    if not (first and k == 0):
                        evac_at(i + k - 1, (k - 1) % XB)
                    meta(i + k, k)
                    gated(i + k, k)

            tiles(0, True, False)
            with dve.Fori(XB, NT - XB, XB) as i:
                tiles(i, False, False)
            tiles(NT - XB, False, True)
            evac_at(NT - 1, XB - 1)

        @block.tensor
        def _(pe):
            pe.wait_ge(s_par, 16 * N_PAR)
            pe.wait_ge(s_const, 10)
            pe.wait_ge(s_set, 6 + NCH + 1)
            for j in range(NJ):
                last = nc.tensor.transpose(bank_a[:, j * T:(j + 1) * T], wp_sb[:, j * P:(j + 1) * P], ident[:, :])
            last.then_inc(s_wpt, 1)
            pe.wait_ge(s_wptc, 1)
            for j in range(NJ):
                nc.tensor.matmul(bank_b[0:KX, 0:T], band[:, j, :], wpt[:, j, :], start=(j == 0), stop=False)
            nc.tensor.matmul(bank_b[0:KX, 0:T], e_last, bp_row, start=False, stop=True).then_inc(s_weff, 1)
            pe.wait_ge(s_weffc, 1)
            pe.wait_ge(s_wts, 16 * N_WTS)

            def turn_x(g, par, m):
                pe.wait_ge(x_loaded[par], (g - par) * (X_PER // 2) + X_PER)
                apart(pe, "pe")
                for q in range(4):
                    b, k = 2 * m + q // 2, q % 2
                    last = nc.tensor.transpose(bank[m][0:KX, q * P:(q + 1) * P], xw[par][:, b, k, :], ident[:, :])
                last.then_inc(tx_full, 1)

            def embed(g, m):
                pe.wait_ge(tx_free, 2 * g + m + 1)
                nc.tensor.matmul(bank[m], w_eff[:, :], xt[m], start=True, stop=True).then_inc(emb_full, 1)

            def turn_xn(g, k):
                pe.wait_ge(xn_ready, g + 1)
                for b in range(GB):
                    last = nc.tensor.transpose(bank[k][:, b * T:(b + 1) * T], xn[:, b, k * P:(k + 1) * P], ident[:, :])
                last.then_inc(xnt_full, 1)

            def project(dst, par, c):
                for k in range(NK):
                    last = nc.tensor.matmul(dst, w_in_sb[:, k, c * P:(c + 1) * P], xnt[par][:, k, :],
                                            start=(k == 0), stop=(k == NK - 1))
                return last

            def project_x(g, par, c):
                if c == 0:
                    pe.wait_ge(xnt_free, NK * (g + 1))
                else:
                    pe.wait_ge(xi_free, NCH * g + c)
                project(bank_a, par, c).then_inc(xi_full, 1)

            def project_z(g, par, c):
                if c % 2:
                    pe.wait_ge(z_free, NCH * g + c)
                project(bank[c // 2], par, NCH + c).then_inc(z_full, 1)

            def x_ssm(g):
                pe.wait_ge(xc_ready, g + 1)
                for c in range(NCH):
                    last = nc.tensor.matmul(bank_a[0:3 * R, :], w_x3[:, c, :], xc[:, c, :],
                                            start=(c == 0), stop=(c == NCH - 1))
                last.then_inc(ssm_full, 1)

            def replicate(dst, par, r):
                return nc.tensor.matmul(dst, select[:, r, :], bc3[par][:, :], start=True, stop=True)

            def delta_raw(g, par):
                pe.wait_ge(bc_ready, g + 1)
                replicate(bank_a, par, 0).then_inc(draw_full, 1)

            def b_all(g, n, par):
                g0, n0 = (g, n - 1) if n else (g - 1, S - 1)
                if n0 in ON_POOL:
                    ahead(pe, b_copied, NP_ * g0 + ON_POOL.index(n0) + 1)
                else:
                    ahead(pe, dbx_dve, ND_ * g0 + ON_DVE.index(n0) + 1)
                replicate(b_ps, par, 1 + n).then_inc(b_full, 1)

            def c_all(g, n, par):
                ahead(pe, hc_ready, S * g + n)
                replicate(c_ps, par, 1 + S + n).then_inc(c_full, 1)

            def skip(g):
                ahead(pe, yz_ready, g)
                for c in range(NCH):
                    last = nc.tensor.matmul(yacc[:, c, :], diag_d[:, c, :], xc[:, c, :], start=True, stop=False)
                last.then_inc(skip_done, 1)

            def add_state(g, n):
                pe.wait_ge(hc_ready, S * g + n + 1)
                for c in range(NCH):
                    last = nc.tensor.matmul(yacc[:, c, :], ident[:, :], hc[n % 2][:, c, :], start=False,
                                            stop=(n == S - 1))
                last.then_inc(sum_done, 1)

            def project_out(g, m):
                if m == 0:
                    pe.wait_ge(yz_ready, g + 1)
                else:
                    pe.wait_ge(h2_ready, 2 * g + 1)
                for b in range(2):
                    for c in range(NCH):
                        t0 = (2 * m + b) * T
                        last = nc.tensor.matmul(bank_b[:, b * C:(b + 1) * C], yz[:, c, t0:t0 + T], w_out_sb[:, c, :],
                                                start=(c == 0), stop=(c == NCH - 1))
                last.then_inc(o_full, 1)

            def turn_row(g, k):
                if k == 0:
                    pe.wait_ge(row_ready, g + 1)
                else:
                    pe.wait_ge(xn2t_ready, NK * g + k)
                for b in range(GB):
                    last = nc.tensor.transpose(bank_b[:, b * T:(b + 1) * T], row[0][:, b, k * P:(k + 1) * P],
                                               ident[:, :])
                last.then_inc(t_full, 1)

            def router(g):
                pe.wait_ge(xn2t_ready, NK * (g + 1))
                for b in range(GB):
                    for k in range(NK):
                        last = nc.tensor.matmul(bank_b[:, b * E:(b + 1) * E], xn2t[:, k, b * T:(b + 1) * T],
                                                w_gate_sb[:, k, :], start=(k == 0), stop=(k == NK - 1))
                last.then_inc(l_full, 1)

            def count(g):
                pe.wait_ge(mask_ready, g + 1)
                for b in range(GB + 1):
                    dst = bank_b[:, b * E:(b + 1) * E]
                    if b < GB:
                        last = nc.tensor.matmul(dst, below[:, :], mask[:, b, :], start=True, stop=(b == 0))
                    for b0 in range(b):
                        last = nc.tensor.matmul(dst, ones_bf[:, :], mask[:, b0, :], start=(b == GB and b0 == 0),
                                                stop=(b0 == b - 1))
                last.then_inc(n_full, 1)

            def front(g, par):
                for m in range(2):
                    turn_x(g, par, m)
                for m in range(2):
                    embed(g, m)
                for k in range(NK):
                    turn_xn(g, k)
                for c in range(NCH):
                    project_x(g, par, c)
                x_ssm(g)
                delta_raw(g, par)
                pe.wait_ge(draw_free, g + 1)
                for m in range(2):
                    turn_x(g + 1, 1 - par, m)

            def step(g, par, first, more, last):
                for n in range(S):
                    g2_, n2 = gn(g, n + 2)
                    g1, n1 = gn(g, n + 1)
                    if n == 0 and not last:
                        embed(g + 1, 0)
                    if n == 1:
                        if last:
                            pe.wait_ge(draw_free, g + 1)
                        else:
                            pe.wait_ge(emb_free, 2 * g + 3)
                        project_z(g, par, 0)
                    if n == 2:
                        project_z(g, par, 1)
                    if n == 3 and not last:
                        pe.wait_ge(z_free, NCH * g + 2)
                        turn_xn(g + 1, 0)
                    if n in (4, 5, 6, 7) and not last:
                        project_x(g + 1, 1 - par, n - 4)
                    if n == 9 and not last:
                        x_ssm(g + 1)
                    if n == 12 and not last:
                        delta_raw(g + 1, 1 - par)
                    if n == 0 and not last:
                        embed(g + 1, 1)
                    if n == 1 and not first:
                        if not last:
                            pe.wait_ge(emb_free, 2 * g + 4)
                        project_out(g - 1, 0)
                    if n == 2 and not first:
                        project_out(g - 1, 1)
                    if n == 3 and not last:
                        if not first:
                            pe.wait_ge(h2_ready, 2 * g)
                        turn_xn(g + 1, 1)
                    if n == 4:
                        if last:
                            pe.wait_ge(h2_ready, 2 * g)
                        else:
                            pe.wait_ge(xnt_free, NK * (g + 2))
                        project_z(g, par, 2)
                    if n == 5:
                        project_z(g, par, 3)
                    if n == 6 and not first:
                        pe.wait_ge(z_free, NCH * (g + 1))
                        turn_row(g - 1, 0)
                    if n == 7 and not first:
                        turn_row(g - 1, 1)
                    if n == 8 and not first:
                        router(g - 1)
                    if n == 12 and not first:
                        count(g - 1)
                    if n == 14 and more:
                        pe.wait_ge(draw_free, g + 2)
                        turn_x(g + 2, par, 0)
                        if first:
                            pe.wait_ge(z_free, NCH)
                        else:
                            pe.wait_ge(slot_ready, g)
                        turn_x(g + 2, par, 1)
                    if not (last and n2 < 2):
                        b_all(g2_, n2, par if n2 >= 2 else 1 - par)
                    if not (last and n1 == 0):
                        c_all(g1, n1, par if n1 else 1 - par)
                    if n == 0:
                        skip(g)
                    add_state(g, n)

            front(0, 0)
            b_all(0, 0, 0)
            b_all(0, 1, 0)
            c_all(0, 0, 0)
            step(0, 0, True, True, False)
            with pe.Fori(1, G - 3, 2) as g:
                step(g, 1, False, True, False)
                step(g + 1, 0, False, True, False)
            step(G - 3, 1, False, True, False)
            step(G - 2, 0, False, False, False)
            step(G - 1, 1, False, False, True)
            project_out(G - 1, 0)
            project_out(G - 1, 1)
            turn_row(G - 1, 0)
            turn_row(G - 1, 1)
            router(G - 1)
            count(G - 1)

            pe.wait_ge(tab_ready, 1)
            pe.wait_ge(w_loaded, 16 * 3 * E)

            def turn_tile(i, k):
                pe.wait_ge(tile_loaded[k], (16 * (i // XB + 1)) if isinstance(i, int) else (i - k) * (16 // XB) + 16)
                if not (isinstance(i, int) and i < 1):
                    pe.wait_ge(xgt_ready, i)
                for q in range(NK):
                    last = nc.tensor.transpose(px[:, q * P:(q + 1) * P], xg[k][:, q * P:(q + 1) * P], ident[:, :])
                last.then_inc(xg_turned, 1)

            def hidden(i, k, e, base, dst, done):
                for q in range(NK):
                    w = w_moe[:, bass.ds(e, 1), base + q * H:base + (q + 1) * H].rearrange("p a h -> p (a h)")
                    last = nc.tensor.matmul(dst[k % 2], xgt[k % 2][:, q * P:(q + 1) * P], w,
                                            start=(q == 0), stop=(q == NK - 1))
                last.then_inc(done, 1)

            def turn_act(i, k):
                pe.wait_ge(act_ready, i + 1)
                if not (isinstance(i, int) and i < 1):
                    pe.wait_ge(actt_ready, i)
                for q in range(NH):
                    last = nc.tensor.transpose(pt[:, q * P:(q + 1) * P], act[k % 2][:, q * P:(q + 1) * P], ident[:, :])
                last.then_inc(at_full, 1)

            def down(i, k, e):
                pe.wait_ge(actt_ready, i + 1)
                if not (isinstance(i, int) and i < 2):
                    pe.wait_ge(y_ready, i - 1)
                for q in range(NH):
                    w = w_moe[:, bass.ds(e, 1), 2 * NK * H + q * C:2 * NK * H + (q + 1) * C]\
                        .rearrange("p a h -> p (a h)")
                    last = nc.tensor.matmul(py[k % 2], actt[k % 2][:, q * P:(q + 1) * P], w,
                                            start=(q == 0), stop=(q == NH - 1))
                last.then_inc(y_full, 1)

            def expert(i):
                return pe.value_load(tab[0:1, 0, bass.ds(i, 1)], min_val=0, max_val=E - 1)

            def tiles(i, first, last):
                e = None
                for k in range(XB):
                    t = i + k
                    e_before = expert(t - 1) if k == 0 and not first else e if k else None
                    e = expert(t)
                    if not (last and k == XB - 1):
                        turn_tile(t + 1, (k + 1) % XB)
                    pe.wait_ge(xgt_ready, t + 1)
                    if not (isinstance(t, int) and t < 2):
                        pe.wait_ge(silu_ready, t - 1)
                    hidden(t, k, e, 0, pg, gate_full)
                    if not (first and k == 0):
                        turn_act(t - 1, (k - 1) % XB)
                    hidden(t, k, e, NK * H, pu, up_full)
                    if not (first and k == 0):
                        down(t - 1, (k - 1) % XB, e_before)

            turn_tile(0, 0)
            tiles(0, True, False)
            with pe.Fori(XB, NT - XB, XB) as i:
                tiles(i, False, False)
            tiles(NT - XB, False, True)
            turn_act(NT - 1, XB - 1)
            down(NT - 1, XB - 1, expert(NT - 1))
    return nc


_INS = ['x', 'L0_tok_W_embed', 'L0_tok_b_embed', 'L0_tok_W_proj', 'L0_tok_b_proj', 'L0_attn_W_in', 'L0_attn_conv_w',
        'L0_attn_conv_b', 'L0_attn_W_xproj', 'L0_attn_w_dt', 'L0_attn_b_dt', 'L0_attn_A_log', 'L0_attn_D_param',
        'L0_attn_W_out', 'L0_ffn_w_gate', 'L0_ffn_wi', 'L0_ffn_wg', 'L0_ffn_wo']
_OUT = (64, 128, 256)


def kernel(**inputs):
    import numpy as _np
    import concourse.bacc as _bacc
    from concourse import mybir as _mybir
    from concourse.bass_utils import run_bass_kernel_spmd as _run

    nc = _bacc.Bacc("TRN2", target_bir_lowering=False, num_devices=1)
    arrays, args = {}, []
    for name in _INS:
        a = _np.ascontiguousarray(inputs[name])
        arrays[f"in_{name}_dram"] = a
        args.append(nc.dram_tensor(f"in_{name}_dram", a.shape, _mybir.dt.from_np(a.dtype), kind="ExternalInput").ap())
    args.append(nc.dram_tensor("out_0_dram", _OUT, _mybir.dt.from_np(_np.dtype("float32")), kind="ExternalOutput").ap())
    audio_tower(nc, *args)
    r = _run(nc, [arrays], core_ids=[0])
    return r.results[0]["out_0_dram"]
```

```python
from contextlib import ExitStack

import concourse.bass as bass
from concourse import mybir

ALU = mybir.AluOpType
ACT = mybir.ActivationFunctionType
AX_X = mybir.AxisListType.X
F32 = mybir.dt.float32
BF16 = mybir.dt.bfloat16
I32 = mybir.dt.int32
U32 = mybir.dt.uint32

P = 128


def audio_tower(nc, x, W_embed, b_embed, W_proj, b_proj, W_in, conv_w, conv_b, W_xproj, w_dt, b_dt, A_log,
                D_param, W_out, w_gate, wi, wg, wo, out):
    B, CI, L = x.shape
    CM, _, KW = W_embed.shape
    PAD = KW // 2
    T = W_proj.shape[0]
    DS = W_proj.shape[1] // CM
    C = L // DS
    WIN = DS + KW - 1
    KX = CI * WIN + 1
    DI = W_out.shape[0]
    NCH = DI // P
    NK = C // P
    S = A_log.shape[1]
    TAPS = conv_w.shape[2]
    R = 2 * S + 1
    E = w_gate.shape[1]
    H = wi.shape[2]
    NH = H // P
    GB = 4
    GT = GB * T
    G = B // GB
    NJ = DS * CM // P
    SPC = P // CM
    EPS = 1e-5
    ROW = C + 2
    TOKENS = B * T
    REG = TOKENS + P
    NT = -(-(2 * TOKENS // P + E - 1) // 4) * 4
    MW = 2 * NK * H + NH * C
    assert T == P and GT == 512 and C == 256 and NCH == 4 and G % 2 == 0 and S == 16 and H == 512

    rows_dram = nc.dram_tensor("expert_rows", [E * REG + P, ROW], F32).ap()

    with ExitStack() as ctx:
        def sb(name, shape, dt=F32):
            return ctx.enter_context(nc.sbuf_tensor(name, shape, dt))

        def sem(name):
            return ctx.enter_context(nc.semaphore(name))

        ident = sb("ident", [P, P])
        w_in_sb = sb("w_in_sb", [P, NK, 2 * DI])
        w_out_sb = sb("w_out_sb", [P, NCH, C])
        w_x3 = sb("w_x3", [P, NCH, 3 * R])
        w_gate_sb = sb("w_gate_sb", [P, NK, E])
        diag_d = sb("diag_d", [P, NCH, P])
        select = sb("select", [3 * R, R, P], BF16)
        w_eff = sb("w_eff", [KX, T])
        a_neg = sb("a_neg", [P, NCH, S])
        cw = sb("cw", [P, NCH, TAPS])
        cb = sb("cb", [P, NCH])
        wdt = sb("wdt", [P, NCH])
        bdt = sb("bdt", [P, NCH])
        dpar = sb("dpar", [P, NCH])
        below = sb("below", [P, P], BF16)
        ones_bf = sb("ones_bf", [P, P], BF16)
        key_w = sb("key_w", [P, GB, E])
        half = sb("half", [P, GB])
        counts = sb("counts", [P, E])
        tokf = sb("tokf", [P, GB])
        SCN = NCH * GT
        arena = sb("arena", [P, E * MW])
        parts = {}
        at = 0
        for name, n in (("xc", SCN), ("delta0", SCN), ("u0", SCN), ("delta1", SCN), ("u1", SCN), ("dA0", SCN),
                        ("dA1", SCN), ("dBx0", SCN), ("dBx1", SCN), ("state", SCN), ("hc0", SCN), ("hc1", SCN)):
            parts[name] = arena[:, at:at + n].rearrange("p (c t) -> p c t", c=NCH)
            at += n
        assert at == E * MW
        dA = [parts["dA0"], parts["dA1"]]
        dBx = [parts["dBx0"], parts["dBx1"]]
        hc = [parts["hc0"], parts["hc1"]]
        state, xc = parts["state"], parts["xc"]
        delta = [parts["delta0"], parts["delta1"]]
        u = [parts["u0"], parts["u1"]]
        w_moe = arena[:, :].rearrange("p (e m) -> p e m", e=E)

        def flat(ap):
            return ap.rearrange("p c t -> p (c t)")

        z = sb("z", [P, NCH, GT])
        hnew = sb("hnew", [P, GB, C])
        hres = [sb(f"hres{i}", [P, GB, C]) for i in range(2)]
        bc3 = [sb(f"bc3_{i}", [3 * R, GT], BF16) for i in range(2)]
        b_rep = [sb(f"b_rep{i}", [P, GT]) for i in range(2)]
        xw = [sb(f"xw{i}", [P, GB, NK, KX]) for i in range(2)]
        xn = sb("xn", [P, GB, C])
        xnt = [sb(f"xnt{i}", [P, NK, GT]) for i in range(2)]
        tap = [[sb(f"tap{i}_{k}", [P, GB, T]) for k in range(TAPS)] for i in range(2)]
        xt = [tap[i][TAPS - 1][0:KX, :, :].rearrange("p b t -> p (b t)") for i in range(2)]
        soft = sb("soft", [P, NCH, GT])
        split = sb("split", [2 * R, GT])
        yz = soft
        h2 = sb("h2", [P, GB, C])
        row = [sb(f"row{i}", [P, GB, ROW]) for i in range(2)]
        xn2t = xn[:, :, :].rearrange("p (k b) c -> p k (b c)", k=NK)
        stat = sb("stat", [P, 2, GB, 6])
        mv = sb("mv", [P, 2, GB, 2])
        rstd = sb("rstd", [P, 2, GB])
        lmax = sb("lmax", [P, GB])
        ex = sb("ex", [P, GB, E])
        esum = sb("esum", [P, GB])
        einv = sb("einv", [P, GB])
        gates = sb("gates", [P, GB, E])
        g2 = sb("g2", [P, GB, E])
        m1 = sb("m1", [P, 2, GB])
        eq = sb("eq", [P, GB, E])
        key = sb("key", [P, GB, E])
        kmax = sb("kmax", [P, GB])
        oh = [sb(f"oh{i}", [P, GB, E]) for i in range(2)]
        mask = sb("mask", [P, GB, E], BF16)
        pos = sb("pos", [P, GB, E])
        slot_f = sb("slot_f", [P, 2, GB])
        slot = sb("slot", [P, 2, GB], U32)
        band = z[:, 0, 0:NJ * KX].rearrange("p (j k) -> p j k", j=NJ)
        e_last = z[0:1, 1, 0:KX]
        bp_row = z[0:1, 2, 0:T]
        wp_sb = z[:, 3, :]
        wpt = soft[:, 0, :].rearrange("p (j t) -> p j t", j=NJ)

        ne = sb("ne", [1, E])
        ebase = sb("ebase", [P, E])
        jlim = sb("jlim", [1, TOKENS // P])
        tile_no = sb("tile_no", [1, NT])
        cmp1 = z[0:1, 0, 0:E * (TOKENS // P)].rearrange("p (e j) -> p e j", e=E)
        cmp2 = z[0:1, :, :].rearrange("p c t -> p (c t)")[:, 0:NT * E].rearrange("p (i e) -> p i e", e=E)
        cmp3 = soft[0:1, :, :].rearrange("p c t -> p (c t)")[:, 0:NT * E].rearrange("p (i e) -> p i e", e=E)
        nt = sb("nt", [1, E])
        ones_e = sb("ones_e", [1, E])
        tend = sb("tend", [1, E])
        e_of, t_of, r_of, b_of = (hres[1][0:1, i, 0:NT] for i in range(4))
        tab = sb("tab", [1, 2, NT + 4], I32)
        pad_at = sb("pad_at", [1, E], I32)
        pad_row = sb("pad_row", [P, ROW])
        iota_p = sb("iota_p", [P, 1])
        XB = 4
        xg = [tap[i % 2][i // 2 * 2][:, :, :].rearrange("p b t -> p (b t)")[:, 0:ROW] for i in range(XB)]
        xgt = [xnt[0][:, i, 0:C] for i in range(2)]
        sg = [xn2t[:, i, :] for i in range(2)]
        act = [z[:, 2 + i, :] for i in range(2)]
        actt = [z[:, i, :] for i in range(2)]
        yt = [hres[0][:, i, :] for i in range(2)]
        tok_id = [sb(f"tok_id{i}", [P, 1], U32) for i in range(XB)]
        tok_w = [sb(f"tok_w{i}", [P, 1]) for i in range(XB)]

        psum = ctx.enter_context(nc.psum_tensor("psum", [P, 8, 512], F32))
        yacc = psum[:, 0:NCH, :]
        b_ps, c_ps = psum[:, 4, :], psum[:, 5, :]
        bank_a, bank_b = psum[:, 6, :], psum[:, 7, :]
        bank = [bank_a, bank_b]
        pg = [psum[:, 0, :], psum[:, 1, :]]
        pu = [psum[:, 2, :], psum[:, 3, :]]
        py = [psum[:, 4, 0:C], psum[:, 5, 0:C]]
        px, pt = psum[:, 6, :], psum[:, 7, :]

        s_emb = sem("s_emb")
        s_par = sem("s_par")
        s_wts = sem("s_wts")
        s_win = sem("s_win")
        s_band0 = sem("s_band0")
        s_const = sem("s_const")
        s_ctmp = sem("s_ctmp")
        s_zero = sem("s_zero")
        s_set = sem("s_set")
        s_aexp = sem("s_aexp")
        s_wpt = sem("s_wpt")
        s_wptc = sem("s_wptc")
        s_weff = sem("s_weff")
        s_weffc = sem("s_weffc")
        x_loaded = [sem(f"x_loaded{i}") for i in range(2)]
        tx_full = sem("tx_full")
        tx_free = sem("tx_free")
        emb_full = sem("emb_full")
        emb_free = sem("emb_free")
        h_moved = sem("h_moved")
        xnt_full = sem("xnt_full")
        xnt_free = sem("xnt_free")
        xi_full = sem("xi_full")
        xi_free = sem("xi_free")
        z_full = sem("z_full")
        z_free = sem("z_free")
        ssm_full = sem("ssm_full")
        draw_full = sem("draw_full")
        draw_free = sem("draw_free")
        stat_step = [sem(f"stat_step{i}") for i in range(2)]
        stat1 = sem("stat1")
        pow1 = sem("pow1")
        xn_ready = sem("xn_ready")
        conv_part = sem("conv_part")
        conv_ready = sem("conv_ready")
        xc_ready = sem("xc_ready")
        z_ready = sem("z_ready")
        hi_ready = sem("hi_ready")
        rest_ready = sem("rest_ready")
        mid_ready = sem("mid_ready")
        bc_ready = sem("bc_ready")
        sexp_ready = sem("sexp_ready")
        ln_ready = sem("ln_ready")
        delta_ready = sem("delta_ready")
        u_ready = sem("u_ready")
        b_full = sem("b_full")
        b_copied = sem("b_copied")
        c_full = sem("c_full")
        dA_ready = sem("dA_ready")
        dbx_dve = sem("dbx_dve")
        dbx_pool = sem("dbx_pool")
        scan_done = sem("scan_done")
        hc_ready = sem("hc_ready")
        skip_done = sem("skip_done")
        sum_done = sem("sum_done")
        yz_ready = sem("yz_ready")
        o_full = sem("o_full")
        h2_ready = sem("h2_ready")
        h2_stored = sem("h2_stored")
        stat2 = sem("stat2")
        pow2 = sem("pow2")
        row_ready = sem("row_ready")
        t_full = sem("t_full")
        xn2t_ready = sem("xn2t_ready")
        l_full = sem("l_full")
        lsub_ready = sem("lsub_ready")
        lexp_ready = sem("lexp_ready")
        mask_ready = sem("mask_ready")
        n_full = sem("n_full")
        slot_ready = sem("slot_ready")
        scattered = sem("scattered")
        row_copied = sem("row_copied")
        rows_left = sem("rows_left")
        dv = sem("dv")
        w_loaded = sem("w_loaded")
        tab_ready = sem("tab_ready")
        pad_ready = sem("pad_ready")
        padded = sem("padded")
        tile_loaded = [sem(f"tile_loaded{i}") for i in range(XB)]
        xg_turned = sem("xg_turned")
        xgt_ready = sem("xgt_ready")
        meta_ready = sem("meta_ready")
        gate_full = sem("gate_full")
        up_full = sem("up_full")
        silu_ready = sem("silu_ready")
        act_ready = sem("act_ready")
        at_full = sem("at_full")
        actt_ready = sem("actt_ready")
        y_full = sem("y_full")
        y_ready = sem("y_ready")
        added = sem("added")

        N_EMB = 2 + DS + SPC
        N_PAR = 6
        N_WTS = 5
        X_PER = 16 * 4 * GB
        ROUTER = 26
        ON_POOL = [1, 6, 7, 8, 9, 10, 11, 12, 13, 14, 15]
        Z_BANK = [1, 1, 0, 1]
        ON_DVE = [n for n in range(S) if n not in ON_POOL]
        NP_, ND_ = len(ON_POOL), len(ON_DVE)

        def gn(g, n):
            return (g + 1, n - S) if n >= S else (g, n)

        def ahead(eng, s, value):
            if not (isinstance(value, int) and value <= 0):
                eng.wait_ge(s, value)

        passed = {name: sem(f"passed_{name}") for name in ("pe", "dve", "pool", "sp")}

        def apart(eng, name):
            eng.sem_inc(passed[name], 1)

        def load_x(sp, g, par):
            ahead(sp, tx_full, 2 * (g - 1))
            apart(sp, "sp")

            for b in range(GB):
                def win(first_row, rows_, cut, width):
                    at0 = first_row * DS - PAD + cut
                    src = x[bass.ds(g * GB + b, 1), :, at0:at0 + width]
                    return bass.AP(tensor=src.tensor, offset=src.offset,
                                   ap=[[DS, rows_], [L, CI], [1, width]])

                def cell(k, p0, p1, cut, width):
                    return xw[par][p0:p1, b, k, 0:CI * WIN].rearrange("p (c w) -> p c w", c=CI)[:, :, cut:cut + width]

                sp.dma_start(cell(0, 1, P, 0, WIN), win(1, P - 1, 0, WIN)).then_inc(x_loaded[par], 16)
                sp.dma_start(cell(0, 0, 1, PAD, WIN - PAD), win(0, 1, PAD, WIN - PAD)).then_inc(x_loaded[par], 16)
                sp.dma_start(cell(1, 0, P - 1, 0, WIN), win(P, P - 1, 0, WIN)).then_inc(x_loaded[par], 16)
                sp.dma_start(cell(1, P - 1, P, 0, WIN - PAD), win(2 * P - 1, 1, 0, WIN - PAD))\
                    .then_inc(x_loaded[par], 16)

        def conv(eng, g, c):
            t = tap[c % 2]
            if c == 0:
                ahead(eng, skip_done, g)
                ahead(eng, u_ready, g)
            eng.wait_ge(xi_free, NCH * g + c + 1)
            dst = xc[:, c, :].rearrange("p (b t) -> p b t", b=GB)
            eng.tensor_tensor(dst, t[3][:, :, :], t[2][:, :, :], ALU.add).then_inc(conv_part, 1)
            eng.wait_ge(conv_part, 2 * (NCH * g + c) + 1)
            eng.tensor_tensor(dst, dst, t[1][:, :, :], ALU.add).then_inc(conv_part, 1)
            eng.wait_ge(conv_part, 2 * (NCH * g + c) + 2)
            eng.tensor_tensor(dst, dst, t[0][:, :, :], ALU.add).then_inc(conv_ready, 1)

        def add_delta(eng, g, par):
            eng.wait_ge(ln_ready, g + 1)
            eng.tensor_tensor(delta[par], delta[par], soft[:, :, :], ALU.add).then_inc(delta_ready, 1)

        block = ctx.enter_context(nc.Block())

        @block.sync
        def _(sp):
            sp.sem_inc(h2_stored, 16)
            sp.sem_inc(rows_left, 1)
            sp.dma_start(wp_sb, W_proj.rearrange("o c a -> o (c a)")).then_inc(s_emb, 16)
            sp.dma_start(bp_row, b_proj.rearrange("(a o) -> a o", a=1)).then_inc(s_emb, 16)
            sp.wait_ge(s_band0, 2)
            for s in range(DS):
                j, q = s // SPC, s % SPC
                dst = band[q * CM:(q + 1) * CM, j, 0:CI * WIN].rearrange("p (c w) -> p c w", c=CI)[:, :, s:s + KW]
                sp.dma_start(dst, W_embed).then_inc(s_emb, 16)
            for q in range(SPC):
                sp.dma_start(band[q * CM:(q + 1) * CM, :, KX - 1:KX],
                             b_embed.rearrange("(c a b) -> c a b", a=1, b=1).broadcast_to([CM, NJ, 1]),
                             allow_slow_non_contiguous=True)\
                    .then_inc(s_emb, 16)

            sp.wait_ge(s_set, 5)
            sp.dma_start(rows_dram[E * REG:E * REG + P, :], pad_row[:, :]).then_inc(padded, 16)

            def move_h(g, par):
                sp.wait_ge(emb_free, 2 * (g + 1))
                apart(sp, "sp")
                ahead(sp, h2_ready, 2 * (g - 1))
                sp.dma_start(hres[par][:, :, :], hnew[:, :, :]).then_inc(h_moved, 16)

            def store_h2(g):
                sp.wait_ge(h2_ready, 2 * g + 2)
                sp.dma_start(out[bass.ds(g * GB, GB), :, :].rearrange("b o l -> o b l"), h2[:, :, :])\
                    .then_inc(h2_stored, 16)

            sp.wait_ge(s_zero, 1)
            load_x(sp, 0, 0)
            sp.dma_start(w_in_sb[:, :, :], W_in.rearrange("(k p) n -> p k n", p=P)).then_inc(s_win, 16)
            load_x(sp, 1, 1)

            def step(g, par, first, load, last):
                if load:
                    load_x(sp, g + 2, par)
                if not last:
                    move_h(g + 1, 1 - par)
                if not first:
                    store_h2(g - 1)

            move_h(0, 0)
            step(0, 0, True, True, False)
            with sp.Fori(1, G - 3, 2) as g:
                step(g, 1, False, True, False)
                step(g + 1, 0, False, True, False)
            step(G - 3, 1, False, True, False)
            step(G - 2, 0, False, False, False)
            step(G - 1, 1, False, False, True)

            def load_expert(e):
                gate_w = w_moe[:, e, 0:NK * H].rearrange("p (k h) -> p k h", k=NK)
                up_w = w_moe[:, e, NK * H:2 * NK * H].rearrange("p (k h) -> p k h", k=NK)
                down_w = w_moe[:, e, 2 * NK * H:].rearrange("p (k c) -> p k c", k=NH)
                sp.dma_start(gate_w, wg[e].rearrange("(k p) h -> p k h", p=P)).then_inc(w_loaded, 16)
                sp.dma_start(up_w, wi[e].rearrange("(k p) h -> p k h", p=P)).then_inc(w_loaded, 16)
                sp.dma_start(down_w, wo[e].rearrange("(k p) c -> p k c", p=P)).then_inc(w_loaded, 16)

            def free_for(words, *counts_):
                for s, value in counts_:
                    sp.wait_ge(s, value)
                while loaded[0] < E and (loaded[0] + 1) * MW <= words:
                    load_expert(loaded[0])
                    loaded[0] += 1

            loaded = [0]
            free_for(3 * SCN, (skip_done, G), (scan_done, S * (G - 1)))
            free_for(5 * SCN, (dA_ready, S * G), (dbx_pool, NP_ * G), (dbx_dve, ND_ * G))
            free_for(9 * SCN, (scan_done, S * G))
            free_for(12 * SCN, (sum_done, S * G))
            store_h2(G - 1)

            sp.wait_ge(pad_ready, 1)
            for e in range(E):
                r = sp.value_load(pad_at[0:1, e:e + 1], min_val=0, max_val=E * REG)
                sp.dma_start(rows_dram[bass.ds(r, P), :], pad_row[:, :]).then_inc(padded, 16)

            sp.wait_ge(tab_ready, 1)
            sp.wait_ge(padded, 16 * (E + 1))
            sp.wait_ge(scattered, 16 * 2 * GB * G)

            def load_tile(i, k, first):
                if not first:
                    sp.wait_ge(xg_turned, i - XB + 1)
                    sp.wait_ge(meta_ready, i - XB + 1)
                r = sp.value_load(tab[0:1, 1, bass.ds(i, 1)], min_val=0, max_val=E * REG)
                sp.dma_start(xg[k], rows_dram[bass.ds(r, P), :]).then_inc(tile_loaded[k], 16)

            for k in range(XB):
                load_tile(k, k, True)
            with sp.Fori(XB, NT, XB) as i:
                for k in range(XB):
                    load_tile(i + k, k, False)
            sp.wait_ge(h2_stored, 16 * (G + 1))
            sp.wait_ge(added, 16 * NT)

        @block.gpsimd
        def _(pool):
            pool.memset(ident[:, :], 0.0).then_inc(s_ctmp, 1)
            pool.memset(select[:, :, :], 0.0).then_inc(s_ctmp, 1)
            pool.memset(below[:, :], 1.0).then_inc(s_ctmp, 1)
            pool.wait_ge(s_ctmp, 3)
            pool.affine_select(out=ident[:, :], in_=ident[:, :], compare_op=ALU.not_equal, fill=1.0, base=0,
                               pattern=[[-1, P]], channel_multiplier=1).then_inc(s_const, 1)
            pool.affine_select(out=below[:, :], in_=below[:, :], compare_op=ALU.is_gt, fill=0.0, base=0,
                               pattern=[[1, P]], channel_multiplier=-1).then_inc(s_const, 1)
            for q in range(3):
                pool.affine_select(out=select[:, :, :], in_=select[:, :, :], compare_op=ALU.not_equal, fill=1.0,
                                   base=-q * R, pattern=[[-1, R], [0, P]], channel_multiplier=1).then_inc(s_ctmp, 1)
                pool.wait_ge(s_ctmp, 4 + q)
            pool.dma_start(a_neg[:, :, :], A_log.rearrange("(c p) s -> p c s", p=P)).then_inc(s_par, 16)
            for dst, src in ((cb, conv_b), (wdt, w_dt), (bdt, b_dt), (dpar, D_param)):
                pool.dma_start(dst[:, :], src.rearrange("(c p) -> p c", p=P), allow_slow_non_contiguous=True)\
                    .then_inc(s_par, 16)
            pool.dma_start(cw[:, :, :], conv_w.rearrange("(c p) a k -> p c (a k)", p=P)).then_inc(s_par, 16)
            for q in range(3):
                pool.dma_start(w_x3[:, :, q * R:(q + 1) * R], W_xproj.rearrange("(c p) r -> p c r", p=P))\
                    .then_inc(s_wts, 16)
            pool.dma_start(w_out_sb[:, :, :], W_out.rearrange("(c p) n -> p c n", p=P)).then_inc(s_wts, 16)
            pool.dma_start(w_gate_sb[:, :, :], w_gate.rearrange("(k p) n -> p k n", p=P)).then_inc(s_wts, 16)
            pool.iota(key_w[:, :, :], pattern=[[0, GB], [-1, E]], base=E, channel_multiplier=0,
                      allow_small_or_imprecise_dtypes=True).then_inc(s_const, 1)
            pool.iota(ebase[:, :], pattern=[[REG, E]], base=0, channel_multiplier=0,
                      allow_small_or_imprecise_dtypes=True).then_inc(s_const, 1)
            pool.iota(jlim[:, :], pattern=[[P, TOKENS // P]], base=0, channel_multiplier=0,
                      allow_small_or_imprecise_dtypes=True).then_inc(s_const, 1)
            pool.iota(tile_no[:, :], pattern=[[1, NT]], base=0, channel_multiplier=0,
                      allow_small_or_imprecise_dtypes=True).then_inc(s_const, 1)
            pool.iota(iota_p[:, :], pattern=[[0, 1]], base=0, channel_multiplier=1,
                      allow_small_or_imprecise_dtypes=True).then_inc(s_const, 1)
            pool.iota(tokf[:, :], pattern=[[P, GB]], base=0, channel_multiplier=1,
                      allow_small_or_imprecise_dtypes=True).then_inc(s_const, 1)
            pool.memset(half[:, :], -0.5).then_inc(s_const, 1)
            pool.memset(ones_bf[:, :], 1.0).then_inc(s_const, 1)

            def rsqrt(g, which, ready, done):
                pool.wait_ge(ready, g + 1)
                pool.tensor_tensor(rstd[:, which, :], mv[:, which, :, 1], half[:, :], ALU.pow).then_inc(done, 1)

            def make_dbx(g, n, par):
                k = ON_POOL.index(n)
                if k == 0:
                    pool.wait_ge(u_ready, g + 1)
                ahead(pool, scan_done, S * g + n - 1)
                pool.wait_ge(b_copied, NP_ * g + k + 1)
                rep = b_rep[(NP_ * par + k) % 2][:, :].rearrange("p (a t) -> p a t", a=1)
                pool.tensor_tensor(dBx[n % 2], u[par], rep.broadcast_to([P, NCH, GT]), ALU.mult).then_inc(dbx_pool, 1)

            def scatter(g, part):
                todo = [(k, b) for k in range(2) for b in range(GB)][3 * part:3 * part + 3]
                if part == 0:
                    pool.wait_ge(slot_ready, g + 1)
                    pool.wait_ge(row_copied, g + 1)
                    apart(pool, "pool")
                for k, b in todo:
                    pool.indirect_dma_start(
                        out=rows_dram[:, :], out_offset=bass.IndirectOffsetOnAxis(ap=slot[:, k, b:b + 1], axis=0),
                        in_=row[k][:, b, :], in_offset=None).then_inc(scattered, 16)

            def rows_gone(g):
                pool.wait_ge(scattered, 16 * 2 * GB * (g + 1))
                pool.sem_inc(rows_left, 1)

            def front(g, par):
                rsqrt(g, 0, stat1, pow1)
                rsqrt(g + 1, 0, stat1, pow1)

            def step(g, par, first, more, last):
                for n in range(S):
                    if n + 1 in ON_POOL:
                        make_dbx(g, n + 1, par)
                    if n == 6 and not first:
                        rsqrt(g - 1, 1, stat2, pow2)
                    if n in (2, 3, 4, 5) and not last:
                        conv(pool, g + 1, n - 2)
                    if n == 12 and not last:
                        add_delta(pool, g + 1, 1 - par)
                    if n in (13, 14, 15) and not first:
                        scatter(g - 1, n - 13)
                    if n == 14 and more:
                        rsqrt(g + 2, 0, stat1, pow1)
                if not first:
                    rows_gone(g - 1)

            pool.wait_ge(s_const, 10)
            front(0, 0)
            step(0, 0, True, True, False)
            with pool.Fori(1, G - 3, 2) as g:
                step(g, 1, False, True, False)
                step(g + 1, 0, False, True, False)
            step(G - 3, 1, False, True, False)
            step(G - 2, 0, False, False, False)
            step(G - 1, 1, False, False, True)
            rsqrt(G - 1, 1, stat2, pow2)
            for part in range(3):
                scatter(G - 1, part)


            pool.wait_ge(h2_stored, 16 * (G + 1))

            def add_tile(i, k, first):
                pool.wait_ge(y_ready, i + 1)
                if not first:
                    pool.wait_ge(added, 16 * i)
                apart(pool, "pool")
                pool.indirect_dma_start(
                    out=out.rearrange("b o l -> (b o) l"),
                    out_offset=bass.IndirectOffsetOnAxis(ap=tok_id[k][:, 0:1], axis=0), in_=yt[k % 2],
                    in_offset=None, bounds_check=TOKENS - 1, oob_is_err=False, compute_op=ALU.add).then_inc(added, 16)

            for k in range(XB):
                add_tile(k, k, k == 0)
            with pool.Fori(XB, NT, XB) as i:
                for k in range(XB):
                    add_tile(i + k, k, False)

        @block.scalar
        def _(actq):
            actq.wait_ge(s_wpt, 1)
            actq.activation(wpt.rearrange("p j t -> p (j t)"), bank_a, ACT.Copy).then_inc(s_wptc, 1)
            actq.wait_ge(s_weff, 1)
            actq.activation(w_eff[:, :], bank_b[0:KX, 0:T], ACT.Copy).then_inc(s_weffc, 1)

            def evac_xt(g, m):
                actq.wait_ge(tx_full, 2 * g + m + 1)
                if not (isinstance(g, int) and g < 2):
                    actq.wait_ge(conv_ready, NCH * g)
                nc.scalar.activation(xt[m], bank_a[0:KX, :], ACT.Copy).then_inc(tx_free, 1)

            def evac_h(g, m):
                actq.wait_ge(emb_full, 2 * g + m + 1)
                if m == 0:
                    ahead(actq, h_moved, 16 * g)
                    ahead(actq, xn_ready, g)
                dst = hnew[:, 2 * m:2 * m + 2, :].rearrange("p b c -> p (b c)")
                nc.scalar.activation(dst, bank[m], ACT.Copy).then_inc(emb_free, 1)

            def evac_xnt(g, par, k):
                actq.wait_ge(xnt_full, NK * g + k + 1)
                nc.scalar.activation(xnt[par][:, k, :], bank[k], ACT.Copy).then_inc(xnt_free, 1)

            def taps(g, c, bank_x):
                actq.wait_ge(xi_full, NCH * g + c + 1)
                ahead(actq, conv_ready, NCH * g + c - 1)
                src = bank_x.rearrange("p (b t) -> p b t", b=GB)
                for k in range(TAPS):
                    d = TAPS - 1 - k
                    if d == 0:
                        nc.scalar.activation(tap[c % 2][k][:, :, :], src, ACT.Identity, scale=cw[:, c, k:k + 1],
                                             bias=cb[:, c:c + 1]).then_inc(xi_free, 1)
                    else:
                        nc.scalar.activation(tap[c % 2][k][:, :, d:T], src[:, :, 0:T - d], ACT.Copy,
                                             scale=cw[:, c, k:k + 1])

            def evac_z(g, c):
                actq.wait_ge(z_full, NCH * g + c + 1)
                if c == 0:
                    ahead(actq, yz_ready, g)
                nc.scalar.activation(z[:, c, :], bank[Z_BANK[c]], ACT.Copy).then_inc(z_free, 1)

            def silu_x(g):
                actq.wait_ge(conv_ready, NCH * (g + 1))
                nc.scalar.activation(xc, xc, ACT.Silu).then_inc(xc_ready, 1)

            def silu_z(g):
                actq.wait_ge(z_free, NCH * (g + 1))
                nc.scalar.activation(z[:, :, :], z[:, :, :], ACT.Silu).then_inc(z_ready, 1)

            def split_hi(g, par):
                actq.wait_ge(ssm_full, g + 1)
                ahead(actq, c_full, S * (g - 1))
                nc.scalar.activation(bc3[par][:, :], bank_a[0:3 * R, :], ACT.Copy).then_inc(hi_ready, 1)

            def split_mid(g, par):
                actq.wait_ge(rest_ready, g + 1)
                nc.scalar.activation(bc3[par][0:2 * R, :], split[:, :], ACT.Copy).then_inc(mid_ready, 1)

            def softplus_in(g, par, half_):
                if half_ == 0:
                    actq.wait_ge(draw_full, g + 1)
                    ahead(actq, o_full, 2 * (g - 1))
                    ahead(actq, delta_ready, g)
                for c in range(NCH // 2 * half_, NCH // 2 * (half_ + 1)):
                    nc.scalar.activation(soft[:, c, :], bank_a, ACT.Abs, scale=wdt[:, c:c + 1], bias=bdt[:, c:c + 1])
                    last = nc.scalar.activation(delta[par][:, c, :], bank_a, ACT.Relu, scale=wdt[:, c:c + 1],
                                                bias=bdt[:, c:c + 1])
                if half_ == 1:
                    last.then_inc(draw_free, 1)

            def softplus_exp(g):
                actq.wait_ge(draw_free, g + 1)
                nc.scalar.activation(soft[:, :, :], soft[:, :, :], ACT.Exp, scale=-1.0).then_inc(sexp_ready, 1)

            def softplus_ln(g):
                actq.wait_ge(sexp_ready, g + 1)
                nc.scalar.activation(soft[:, :, :], soft[:, :, :], ACT.Ln, bias=1.0).then_inc(ln_ready, 1)

            def copy_b(g, n, par):
                k = ON_POOL.index(n)
                actq.wait_ge(b_full, S * g + n + 1)
                ahead(actq, dbx_pool, NP_ * g + k - 1)
                nc.scalar.activation(b_rep[(NP_ * par + k) % 2][:, :], b_ps, ACT.Copy).then_inc(b_copied, 1)

            def exps(g, n, par):
                if n == 0:
                    actq.wait_ge(delta_ready, g + 1)
                ahead(actq, scan_done, S * g + n - 1)
                for c in range(NCH):
                    o = dA[n % 2][:, c, :].rearrange("p (b t) -> p b t", b=GB)[:, :, 1:T]
                    i = delta[par][:, c, :].rearrange("p (b t) -> p b t", b=GB)[:, :, 1:T]
                    last = nc.scalar.activation(o, i, ACT.Exp, scale=a_neg[:, c, n:n + 1])
                last.then_inc(dA_ready, 1)

            def copy_rows(g):
                actq.wait_ge(row_ready, g + 1)
                nc.scalar.activation(row[1][:, :, 0:C], row[0][:, :, 0:C], ACT.Copy).then_inc(row_copied, 1)

            def evac_xn2t(g, k):
                actq.wait_ge(t_full, NK * g + k + 1)
                nc.scalar.activation(xn2t[:, k, :], bank_b, ACT.Copy).then_inc(xn2t_ready, 1)

            def router_exp(g):
                actq.wait_ge(lsub_ready, g + 1)
                nc.scalar.activation(ex[:, :, :], ex[:, :, :], ACT.Exp).then_inc(lexp_ready, 1)

            def front(g, par):
                for m in range(2):
                    evac_xt(g, m)
                for m in range(2):
                    evac_h(g, m)
                for m in range(2):
                    evac_xt(g + 1, m)
                actq.wait_ge(s_par, 16 * N_PAR)
                actq.activation(a_neg[:, :, :], a_neg[:, :, :], ACT.Exp).then_inc(s_aexp, 1)
                for k in range(NK):
                    evac_xnt(g, par, k)
                for m in range(2):
                    evac_h(g + 1, m)
                for c in range(NCH):
                    taps(g, c, bank[c % 2])
                silu_x(g)
                split_hi(g, par)
                split_mid(g, par)
                for half_ in range(2):
                    softplus_in(g, par, half_)
                softplus_exp(g)
                softplus_ln(g)

            def step(g, par, first, more, last):
                for n in range(S):
                    g2, n2 = gn(g, n + 2)
                    if n == 9 and not last:
                        split_mid(g + 1, 1 - par)
                    if n == 11 and not first:
                        router_exp(g - 1)
                    if not (last and n2 < 2):
                        exps(g2, n2, par if n2 >= 2 else 1 - par)
                        if n2 in ON_POOL:
                            copy_b(g2, n2, par if n2 >= 2 else 1 - par)
                    if n == 0 and not last:
                        evac_xnt(g + 1, 1 - par, 0)
                        evac_xnt(g + 1, 1 - par, 1)
                    if n in (1, 2, 3, 4) and not last:
                        taps(g + 1, n - 1, bank_a)
                    if n == 6:
                        evac_z(g, 0)
                    if n == 6 and not last:
                        silu_x(g + 1)
                    if n == 7 and not last:
                        split_hi(g + 1, 1 - par)
                    if n in (8, 9) and not first:
                        evac_xn2t(g - 1, n - 8)
                    if n == 8 and not first:
                        copy_rows(g - 1)
                    if n == 9 and not last:
                        softplus_in(g + 1, 1 - par, 0)
                    if n == 10 and not last:
                        softplus_in(g + 1, 1 - par, 1)
                        softplus_exp(g + 1)
                    if n == 11:
                        if more:
                            evac_xt(g + 2, 0)
                        evac_z(g, 1)
                        if not last:
                            softplus_ln(g + 1)
                    if n == 12 and more:
                        evac_xt(g + 2, 1)
                    if n == 13:
                        if more:
                            evac_h(g + 2, 0)
                            evac_h(g + 2, 1)
                    if n == 14:
                        evac_z(g, 2)
                    if n == 15:
                        evac_z(g, 3)
                        silu_z(g)

            actq.wait_ge(s_zero, 2)
            front(0, 0)
            actq.wait_ge(s_set, 6 + NCH + 1)
            exps(0, 0, 0)
            exps(0, 1, 0)
            copy_b(0, 1, 0)
            step(0, 0, True, True, False)
            with actq.Fori(1, G - 3, 2) as g:
                step(g, 1, False, True, False)
                step(g + 1, 0, False, True, False)
            step(G - 3, 1, False, True, False)
            step(G - 2, 0, False, False, False)
            step(G - 1, 1, False, False, True)
            evac_xn2t(G - 1, 0)
            evac_xn2t(G - 1, 1)
            copy_rows(G - 1)
            router_exp(G - 1)

            def evac_x(i, k):
                actq.wait_ge(xg_turned, i + 1)
                if not (isinstance(i, int) and i < 2):
                    actq.wait_ge(up_full, i - 1)
                nc.scalar.activation(xgt[k % 2], px[:, 0:C], ACT.Copy).then_inc(xgt_ready, 1)

            def silu(i, k):
                actq.wait_ge(gate_full, i + 1)
                if not (isinstance(i, int) and i < 2):
                    actq.wait_ge(act_ready, i - 1)
                nc.scalar.activation(sg[k % 2], pg[k % 2], ACT.Silu).then_inc(silu_ready, 1)

            def weigh(i, k):
                actq.wait_ge(y_full, i + 1)
                actq.wait_ge(meta_ready, i + 1)
                if not (isinstance(i, int) and i < 2):
                    actq.wait_ge(added, 16 * (i - 1))
                nc.scalar.activation(yt[k % 2], py[k % 2], ACT.Copy, scale=tok_w[k][:, 0:1]).then_inc(y_ready, 1)

            def tiles(i, first, last):
                for k in range(XB):
                    if not (last and k == XB - 1):
                        evac_x(i + k + 1, (k + 1) % XB)
                    silu(i + k, k)
                    if not (first and k == 0):
                        weigh(i + k - 1, (k - 1) % XB)

            evac_x(0, 0)
            tiles(0, True, False)
            with actq.Fori(XB, NT - XB, XB) as i:
                tiles(i, False, False)
            tiles(NT - XB, False, True)
            weigh(NT - 1, XB - 1)

        @block.vector
        def _(dve):
            dve.memset(band, 0.0).then_inc(s_band0, 1)
            dve.memset(e_last, 0.0).then_inc(s_band0, 1)
            dve.wait_ge(s_band0, 2)
            dve.memset(e_last[:, KX - 1:KX], 1.0).then_inc(s_set, 1)
            for i in range(2):
                dve.memset(xw[i][:, :, :, :], 0.0).then_inc(s_set, 1)
            dve.wait_ge(s_set, 3)
            dve.memset(xw[0][:, :, :, KX - 1:KX], 1.0)
            dve.memset(xw[1][:, :, :, KX - 1:KX], 1.0).then_inc(s_zero, 1)
            for i in range(2):
                for k in range(TAPS - 1):
                    dve.memset(tap[i][k][:, :, 0:TAPS - 1 - k], 0.0)
                for c in range(NCH):
                    last = dve.memset(dA[i][:, c, :].rearrange("p (b t) -> p b t", b=GB)[:, :, 0:1], 0.0)
            last.then_inc(s_zero, 1)
            dve.memset(pad_row[:, :], 0.0).then_inc(s_set, 1)
            dve.memset(ones_e[:, :], 1.0)
            dve.wait_ge(s_set, 4)
            dve.memset(pad_row[:, C:C + 1].bitcast(I32), TOKENS).then_inc(s_set, 1)
            def stats(g, which, src, ready):
                for b in range(GB):
                    ins = nc.vector.bn_stats(stat[:, which, b, :], src[:, b, :])
                ins.then_inc(stat_step[which], 1)
                dve.wait_ge(stat_step[which], 2 * g + 1)
                apart(dve, "dve")
                for b in range(GB):
                    ins = nc.vector.bn_aggr(mv[:, which, b, :], stat[:, which, b, :])
                ins.then_inc(stat_step[which], 1)
                dve.wait_ge(stat_step[which], 2 * g + 2)
                nc.vector.tensor_scalar(mv[:, which, :, 1], mv[:, which, :, 1], EPS, None, ALU.add).then_inc(ready, 1)

            def norm1_stats(g):
                dve.wait_ge(emb_free, 2 * (g + 1))
                stats(g, 0, hnew, stat1)

            def norm1(g):
                dve.wait_ge(pow1, g + 1)
                ahead(dve, xnt_full, NK * g)
                for b in range(GB):
                    last = nc.vector.tensor_scalar(xn[:, b, :], hnew[:, b, :], mv[:, 0, b, 0:1],
                                                   rstd[:, 0, b:b + 1], ALU.subtract, ALU.mult)
                last.then_inc(xn_ready, 1)

            def split_rest(g, par):
                dve.wait_ge(hi_ready, g + 1)
                nc.vector.tensor_tensor(split[:, :], bank_a[0:2 * R, :], bc3[par][0:2 * R, :], ALU.subtract)\
                    .then_inc(rest_ready, 1)

            def split_lo(g, par):
                dve.wait_ge(mid_ready, g + 1)
                nc.vector.tensor_tensor(bc3[par][0:R, :], split[0:R, :], bc3[par][0:R, :], ALU.subtract)\
                    .then_inc(bc_ready, 1)

            def make_u(g, par):
                dve.wait_ge(delta_ready, g + 1)
                dve.wait_ge(xc_ready, g + 1)
                nc.vector.tensor_tensor(u[par], delta[par], xc, ALU.mult).then_inc(u_ready, 1)

            def make_dbx(g, n, par):
                k = ON_DVE.index(n)
                if k == 0:
                    dve.wait_ge(u_ready, g + 1)
                ahead(dve, scan_done, S * g + n - 1)
                dve.wait_ge(b_full, S * g + n + 1)
                rep = b_ps.rearrange("p (a t) -> p a t", a=1)
                nc.vector.tensor_tensor(dBx[n % 2], u[par], rep.broadcast_to([P, NCH, GT]), ALU.mult)\
                    .then_inc(dbx_dve, 1)

            def scan(g, n):
                dve.wait_ge(dA_ready, S * g + n + 1)
                if n in ON_POOL:
                    dve.wait_ge(dbx_pool, NP_ * g + ON_POOL.index(n) + 1)
                else:
                    dve.wait_ge(dbx_dve, ND_ * g + ON_DVE.index(n) + 1)
                ahead(dve, hc_ready, S * g + n)
                nc.vector.tensor_tensor_scan(flat(state), flat(dA[n % 2]), flat(dBx[n % 2]), 0.0,
                                             ALU.mult, ALU.add).then_inc(scan_done, 1)

            def times_c(g, n):
                dve.wait_ge(scan_done, S * g + n + 1)
                dve.wait_ge(c_full, S * g + n + 1)
                ahead(dve, sum_done, S * g + n - 1)
                rep = c_ps.rearrange("p (a t) -> p a t", a=1)
                nc.vector.tensor_tensor(hc[n % 2], state, rep.broadcast_to([P, NCH, GT]), ALU.mult)\
                    .then_inc(hc_ready, 1)

            def gate_y(g):
                dve.wait_ge(sum_done, S * (g + 1))
                dve.wait_ge(z_ready, g + 1)
                dve.wait_ge(delta_ready, min(g + 2, G) if isinstance(g, int) else g + 2)
                nc.vector.tensor_tensor(yz[:, :, :], yacc, z[:, :, :], ALU.mult).then_inc(yz_ready, 1)

            def residual(g, par, m):
                dve.wait_ge(o_full, 2 * g + m + 1)
                if m == 0:
                    dve.wait_ge(h_moved, 16 * (g + 1))
                    dve.wait_ge(h2_stored, 16 * (g + 1))
                dst = h2[:, 2 * m:2 * m + 2, :].rearrange("p b c -> p (b c)")
                src = hres[par][:, 2 * m:2 * m + 2, :].rearrange("p b c -> p (b c)")
                nc.vector.tensor_tensor(dst, bank_b, src, ALU.add).then_inc(h2_ready, 1)

            def norm2_stats(g):
                dve.wait_ge(h2_ready, 2 * g + 2)
                stats(g, 1, h2, stat2)

            def norm2(g):
                dve.wait_ge(pow2, g + 1)
                dve.wait_ge(rows_left, g + 1)
                for b in range(GB):
                    last = nc.vector.tensor_scalar(row[0][:, b, 0:C], h2[:, b, :], mv[:, 1, b, 0:1],
                                                   rstd[:, 1, b:b + 1], ALU.subtract, ALU.mult)
                last.then_inc(row_ready, 1)

            def after(g, k):
                dve.wait_ge(dv, ROUTER * g + k)

            def bc(ap):
                return ap.rearrange("p (b a) -> p b a", a=1).broadcast_to([P, GB, E])

            def router_a(g):
                dve.wait_ge(l_full, g + 1)
                logits = bank_b[:, 0:GB * E].rearrange("p (b e) -> p b e", b=GB)
                nc.vector.tensor_reduce(lmax[:, :], logits, AX_X, ALU.max).then_inc(dv, 1)
                after(g, 1)
                nc.vector.tensor_tensor(ex[:, :, :], logits, bc(lmax[:, :]), ALU.subtract).then_inc(lsub_ready, 1)

            def router_b(g):
                dve.wait_ge(lexp_ready, g + 1)
                nc.vector.tensor_reduce(esum[:, :], ex[:, :, :], AX_X, ALU.add).then_inc(dv, 1)
                after(g, 2)
                nc.vector.reciprocal(einv[:, :], esum[:, :]).then_inc(dv, 1)
                after(g, 3)
                nc.vector.tensor_tensor(gates[:, :, :], ex[:, :, :], bc(einv[:, :]), ALU.mult).then_inc(dv, 1)
                n = 4
                for k, src in ((0, gates), (1, g2)):
                    after(g, n)
                    nc.vector.tensor_reduce(m1[:, k, :], src[:, :, :], AX_X, ALU.max).then_inc(dv, 1)
                    after(g, n + 1)
                    nc.vector.tensor_tensor(eq[:, :, :], src[:, :, :], bc(m1[:, k, :]), ALU.is_equal).then_inc(dv, 1)
                    after(g, n + 2)
                    nc.vector.tensor_tensor(key[:, :, :], eq[:, :, :], key_w[:, :, :], ALU.mult).then_inc(dv, 1)
                    after(g, n + 3)
                    nc.vector.tensor_reduce(kmax[:, :], key[:, :, :], AX_X, ALU.max).then_inc(dv, 1)
                    after(g, n + 4)
                    nc.vector.tensor_tensor(oh[k][:, :, :], key[:, :, :], bc(kmax[:, :]), ALU.is_equal).then_inc(dv, 1)
                    n += 5
                    if k == 0:
                        after(g, n)
                        nc.vector.scalar_tensor_tensor(out=g2[:, :, :], in0=oh[0][:, :, :], scalar=-2.0,
                                                       in1=gates[:, :, :], op0=ALU.mult, op1=ALU.add).then_inc(dv, 1)
                        n += 1
                after(g, n)
                nc.vector.tensor_tensor(mask[:, :, :], oh[0][:, :, :], oh[1][:, :, :], ALU.add).then_inc(mask_ready, 1)
                for k in range(2):
                    nc.vector.tensor_copy(row[k][:, :, C:C + 1].bitcast(I32),
                                          tokf[:, :].rearrange("p (b a) -> p b a", a=1)).then_inc(dv, 1)
                    nc.vector.tensor_copy(row[k][:, :, C + 1:C + 2],
                                          m1[:, k, :].rearrange("p (b a) -> p b a", a=1)).then_inc(dv, 1)
                n += 4
                after(g, n)
                nc.vector.tensor_scalar(tokf[:, :], tokf[:, :], float(GT), None, ALU.add).then_inc(dv, 1)
                assert n + 1 == 20

            def router_c(g):
                dve.wait_ge(n_full, g + 1)
                earlier = bank_b[:, 0:GB * E].rearrange("p (b e) -> p b e", b=GB)
                cb_ = counts[:, :].rearrange("p (a e) -> p a e", a=1).broadcast_to([P, GB, E])
                nc.vector.tensor_tensor(pos[:, :, :], earlier, cb_, ALU.add).then_inc(dv, 1)
                after(g, 21)
                nc.vector.tensor_tensor(counts[:, :], counts[:, :], bank_b[:, GB * E:(GB + 1) * E], ALU.add)\
                    .then_inc(dv, 1)
                n = 22
                for k in range(2):
                    nc.vector.tensor_tensor(eq[:, :, :], oh[k][:, :, :], pos[:, :, :], ALU.mult).then_inc(dv, 1)
                    after(g, n + 1)
                    nc.vector.tensor_reduce(slot_f[:, k, :], eq[:, :, :], AX_X, ALU.add).then_inc(dv, 1)
                    n += 2
                    after(g, n)
                nc.vector.tensor_copy(slot[:, :, :], slot_f[:, :, :]).then_inc(slot_ready, 1)

            def front(g, par):
                for g0 in (g, g + 1):
                    norm1_stats(g0)
                    norm1(g0)
                dve.wait_ge(s_par, 16 * N_PAR)
                dve.wait_ge(s_aexp, 1)
                dve.tensor_scalar(a_neg[:, :, :], a_neg[:, :, :], -1.0, None, ALU.mult).then_inc(s_set, 1)
                dve.wait_ge(s_const, 10)
                for c in range(NCH):
                    dve.tensor_scalar(diag_d[:, c, :], ident[:, :], dpar[:, c:c + 1], None, ALU.mult).then_inc(s_set, 1)
                dve.tensor_copy(counts[:, :], ebase[:, :]).then_inc(s_set, 1)
                dve.wait_ge(s_set, 6 + NCH + 1)
                for c in range(NCH):
                    conv(dve, g, c)
                split_rest(g, par)
                split_lo(g, par)
                add_delta(dve, g, par)
                make_u(g, par)

            def step(g, par, first, more, last):
                for n in range(S):
                    scan(g, n)
                    if n == 6 and not first:
                        residual(g - 1, 1 - par, 1)
                        norm2_stats(g - 1)
                    if n == 9 and not last:
                        split_lo(g + 1, 1 - par)
                    if n + 1 in ON_DVE:
                        make_dbx(g, n + 1, par)
                    if n == 4 and not first:
                        residual(g - 1, 1 - par, 0)
                    if n == 0 and not first:
                        gate_y(g - 1)
                    if n == 14 and more:
                        norm1_stats(g + 2)
                    if n == 15 and not last:
                        make_dbx(g + 1, 0, 1 - par)
                    times_c(g, n)
                    if not first:
                        if n == 7:
                            norm2(g - 1)
                        if n == 10:
                            router_a(g - 1)
                        if n == 11:
                            router_b(g - 1)
                        if n == 12:
                            router_c(g - 1)
                    if n == 8 and not last:
                        split_rest(g + 1, 1 - par)
                    if n == 13 and not last:
                        make_u(g + 1, 1 - par)
                    if n == 15 and more:
                        norm1(g + 2)

            front(0, 0)
            make_dbx(0, 0, 0)
            step(0, 0, True, True, False)
            with dve.Fori(1, G - 3, 2) as g:
                step(g, 1, False, True, False)
                step(g + 1, 0, False, True, False)
            step(G - 3, 1, False, True, False)
            step(G - 2, 0, False, False, False)
            step(G - 1, 1, False, False, True)
            gate_y(G - 1)
            residual(G - 1, 1, 0)
            residual(G - 1, 1, 1)
            norm2_stats(G - 1)
            norm2(G - 1)
            router_a(G - 1)
            router_b(G - 1)
            router_c(G - 1)

            base = ROUTER * G
            dve.wait_ge(slot_ready, G)
            nc.vector.tensor_copy(pad_at[:, :], counts[0:1, :]).then_inc(pad_ready, 1)
            nc.vector.tensor_tensor(ne[:, :], counts[0:1, :], ebase[0:1, :], ALU.subtract).then_inc(dv, 1)
            dve.wait_ge(dv, base + 1)
            J = TOKENS // P
            ne_b = ne[:, :].rearrange("p (e a) -> p e a", a=1).broadcast_to([1, E, J])
            jl_b = jlim[:, :].rearrange("p (a j) -> p a j", a=1).broadcast_to([1, E, J])
            nc.vector.tensor_tensor(cmp1, ne_b, jl_b, ALU.is_gt).then_inc(dv, 1)
            dve.wait_ge(dv, base + 2)
            nc.vector.tensor_reduce(nt[:, :], cmp1, AX_X, ALU.add).then_inc(dv, 1)
            dve.wait_ge(dv, base + 3)
            nc.vector.tensor_tensor_scan(tend[:, :], ones_e[:, :], nt[:, :], 0.0, ALU.mult, ALU.add).then_inc(dv, 1)
            dve.wait_ge(dv, base + 4)
            te_b = tend[:, :].rearrange("p (a e) -> p a e", a=1).broadcast_to([1, NT, E])
            nt_b = nt[:, :].rearrange("p (a e) -> p a e", a=1).broadcast_to([1, NT, E])
            no_b = tile_no[:, :].rearrange("p (i a) -> p i a", a=1).broadcast_to([1, NT, E])
            nc.vector.tensor_tensor(cmp2, te_b, no_b, ALU.is_le).then_inc(dv, 1)
            dve.wait_ge(dv, base + 5)
            nc.vector.tensor_reduce(e_of, cmp2, AX_X, ALU.add).then_inc(dv, 1)
            nc.vector.tensor_tensor(cmp3, cmp2, nt_b, ALU.mult).then_inc(dv, 1)
            dve.wait_ge(dv, base + 7)
            nc.vector.tensor_reduce(t_of, cmp3, AX_X, ALU.add).then_inc(dv, 1)
            dve.wait_ge(dv, base + 8)
            nc.vector.tensor_tensor(r_of, tile_no[:, :], t_of, ALU.subtract).then_inc(dv, 1)
            nc.vector.tensor_scalar(b_of, e_of, float(REG), None, ALU.mult).then_inc(dv, 1)
            dve.wait_ge(dv, base + 10)
            nc.vector.scalar_tensor_tensor(out=r_of, in0=r_of, scalar=float(P), in1=b_of,
                                           op0=ALU.mult, op1=ALU.add).then_inc(dv, 1)
            dve.wait_ge(dv, base + 11)
            nc.vector.tensor_scalar(tab[:, 1, 0:NT], r_of, float(E * REG), None, ALU.min).then_inc(dv, 1)
            nc.vector.tensor_scalar(tab[:, 0, 0:NT], e_of, float(E - 1), None, ALU.min).then_inc(dv, 1)
            dve.wait_ge(dv, base + 13)
            dve.sem_inc(tab_ready, 1)

            def meta(i, k):
                dve.wait_ge(tile_loaded[k], (16 * (i // XB + 1)) if isinstance(i, int) else (i - k) * (16 // XB) + 16)
                if not (isinstance(i, int) and i < XB):
                    dve.wait_ge(added, 16 * (i - XB + 1))
                nc.vector.tensor_copy(tok_id[k][:, :], xg[k][:, C:C + 1].bitcast(U32))
                nc.vector.tensor_copy(tok_w[k][:, :], xg[k][:, C + 1:C + 2]).then_inc(meta_ready, 1)

            def gated(i, k):
                dve.wait_ge(silu_ready, i + 1)
                dve.wait_ge(up_full, i + 1)
                if not (isinstance(i, int) and i < 2):
                    dve.wait_ge(at_full, i - 1)
                nc.vector.tensor_tensor(act[k % 2], pu[k % 2], sg[k % 2], ALU.mult).then_inc(act_ready, 1)

            def evac_at(i, k):
                dve.wait_ge(at_full, i + 1)
                if not (isinstance(i, int) and i < 2):
                    dve.wait_ge(y_full, i - 1)
                nc.vector.tensor_copy(actt[k % 2], pt).then_inc(actt_ready, 1)

            def tiles(i, first, last):
                for k in range(XB):
                    if not (first and k == 0):
                        evac_at(i + k - 1, (k - 1) % XB)
                    meta(i + k, k)
                    gated(i + k, k)

            tiles(0, True, False)
            with dve.Fori(XB, NT - XB, XB) as i:
                tiles(i, False, False)
            tiles(NT - XB, False, True)
            evac_at(NT - 1, XB - 1)

        @block.tensor
        def _(pe):
            pe.wait_ge(s_emb, 16 * N_EMB)
            pe.wait_ge(s_const, 1)
            pe.wait_ge(s_set, 1)
            for j in range(NJ):
                last = nc.tensor.transpose(bank_a[:, j * T:(j + 1) * T], wp_sb[:, j * P:(j + 1) * P], ident[:, :])
            last.then_inc(s_wpt, 1)
            pe.wait_ge(s_wptc, 1)
            for j in range(NJ):
                nc.tensor.matmul(bank_b[0:KX, 0:T], band[:, j, :], wpt[:, j, :], start=(j == 0), stop=False)
            nc.tensor.matmul(bank_b[0:KX, 0:T], e_last, bp_row, start=False, stop=True).then_inc(s_weff, 1)
            pe.wait_ge(s_weffc, 1)

            def turn_x(g, par, m):
                pe.wait_ge(x_loaded[par], (g - par) * (X_PER // 2) + X_PER)
                apart(pe, "pe")
                if m:
                    pe.wait_ge(tx_free, 2 * g + 1)
                    apart(pe, "pe")
                for q in range(4):
                    b, k = 2 * m + q // 2, q % 2
                    last = nc.tensor.transpose(bank_a[0:KX, q * P:(q + 1) * P], xw[par][:, b, k, :], ident[:, :])
                last.then_inc(tx_full, 1)

            def embed(g, m):
                pe.wait_ge(tx_free, 2 * g + 2)
                nc.tensor.matmul(bank[m], w_eff[:, :], xt[m], start=True, stop=True).then_inc(emb_full, 1)

            def turn_xn(g, k):
                pe.wait_ge(xn_ready, g + 1)
                for b in range(GB):
                    last = nc.tensor.transpose(bank[k][:, b * T:(b + 1) * T], xn[:, b, k * P:(k + 1) * P], ident[:, :])
                last.then_inc(xnt_full, 1)

            def project(dst, par, c):
                for k in range(NK):
                    last = nc.tensor.matmul(dst, w_in_sb[:, k, c * P:(c + 1) * P], xnt[par][:, k, :],
                                            start=(k == 0), stop=(k == NK - 1))
                return last

            def project_x(g, par, c):
                if c == 0:
                    pe.wait_ge(xnt_free, NK * (g + 1))
                else:
                    pe.wait_ge(xi_free, NCH * g + c)
                project(bank_a, par, c).then_inc(xi_full, 1)

            def project_z(g, par, c):
                project(bank[Z_BANK[c]], par, NCH + c).then_inc(z_full, 1)

            def x_ssm(g):
                pe.wait_ge(xc_ready, g + 1)
                for c in range(NCH):
                    last = nc.tensor.matmul(bank_a[0:3 * R, :], w_x3[:, c, :], xc[:, c, :],
                                            start=(c == 0), stop=(c == NCH - 1))
                last.then_inc(ssm_full, 1)

            def replicate(dst, par, r):
                return nc.tensor.matmul(dst, select[:, r, :], bc3[par][:, :], start=True, stop=True)

            def delta_raw(g, par):
                pe.wait_ge(bc_ready, g + 1)
                replicate(bank_a, par, 0).then_inc(draw_full, 1)

            def b_all(g, n, par):
                g0, n0 = (g, n - 1) if n else (g - 1, S - 1)
                if n0 in ON_POOL:
                    ahead(pe, b_copied, NP_ * g0 + ON_POOL.index(n0) + 1)
                else:
                    ahead(pe, dbx_dve, ND_ * g0 + ON_DVE.index(n0) + 1)
                replicate(b_ps, par, 1 + n).then_inc(b_full, 1)

            def c_all(g, n, par):
                ahead(pe, hc_ready, S * g + n)
                replicate(c_ps, par, 1 + S + n).then_inc(c_full, 1)

            def skip(g, c0, c1):
                for c in range(c0, c1):
                    last = nc.tensor.matmul(yacc[:, c, :], diag_d[:, c, :], xc[:, c, :], start=False, stop=False)
                if c1 == NCH:
                    last.then_inc(skip_done, 1)

            def add_state(g, n):
                pe.wait_ge(hc_ready, S * g + n + 1)
                if n == 0:
                    ahead(pe, yz_ready, g)
                for c in range(NCH):
                    last = nc.tensor.matmul(yacc[:, c, :], ident[:, :], hc[n % 2][:, c, :], start=(n == 0),
                                            stop=(n == S - 1))
                last.then_inc(sum_done, 1)

            def project_out(g, m, b):
                if b == 0:
                    if m == 0:
                        pe.wait_ge(yz_ready, g + 1)
                    else:
                        pe.wait_ge(h2_ready, 2 * g + 1)
                for c in range(NCH):
                    t0 = (2 * m + b) * T
                    last = nc.tensor.matmul(bank_b[:, b * C:(b + 1) * C], yz[:, c, t0:t0 + T], w_out_sb[:, c, :],
                                            start=(c == 0), stop=(c == NCH - 1))
                if b == 1:
                    last.then_inc(o_full, 1)

            def turn_row(g, k):
                if k == 0:
                    pe.wait_ge(row_ready, g + 1)
                else:
                    pe.wait_ge(xn2t_ready, NK * g + k)
                for b in range(GB):
                    last = nc.tensor.transpose(bank_b[:, b * T:(b + 1) * T], row[0][:, b, k * P:(k + 1) * P],
                                               ident[:, :])
                last.then_inc(t_full, 1)

            def router(g):
                pe.wait_ge(xn2t_ready, NK * (g + 1))
                for b in range(GB):
                    for k in range(NK):
                        last = nc.tensor.matmul(bank_b[:, b * E:(b + 1) * E], xn2t[:, k, b * T:(b + 1) * T],
                                                w_gate_sb[:, k, :], start=(k == 0), stop=(k == NK - 1))
                last.then_inc(l_full, 1)

            def count(g):
                pe.wait_ge(mask_ready, g + 1)
                for b in range(GB + 1):
                    dst = bank_b[:, b * E:(b + 1) * E]
                    if b < GB:
                        last = nc.tensor.matmul(dst, below[:, :], mask[:, b, :], start=True, stop=(b == 0))
                    for b0 in range(b):
                        last = nc.tensor.matmul(dst, ones_bf[:, :], mask[:, b0, :], start=(b == GB and b0 == 0),
                                                stop=(b0 == b - 1))
                last.then_inc(n_full, 1)

            def front(g, par):
                for m in range(2):
                    turn_x(g, par, m)
                for m in range(2):
                    embed(g, m)
                pe.wait_ge(emb_free, 1)
                for m in range(2):
                    turn_x(g + 1, 1 - par, m)
                pe.wait_ge(tx_free, 4)
                for k in range(NK):
                    turn_xn(g, k)
                for m in range(2):
                    pe.wait_ge(xnt_free, m + 1)
                    embed(g + 1, m)
                pe.wait_ge(s_win, 16)
                for c in range(NCH):
                    if c < 2:
                        pe.wait_ge(emb_free, 3 + c)
                    else:
                        pe.wait_ge(xi_free, c - 1)
                    project(bank[c % 2], par, c).then_inc(xi_full, 1)
                pe.wait_ge(s_wts, 16 * N_WTS)
                x_ssm(g)
                pe.wait_ge(s_const, 10)
                delta_raw(g, par)

            def step(g, par, first, more, last):
                for n in range(S):
                    g2_, n2 = gn(g, n + 2)
                    g1, n1 = gn(g, n + 1)
                    b_due = not (last and n2 < 2)
                    b_first = n1 in ON_POOL
                    if b_due and b_first:
                        b_all(g2_, n2, par if n2 >= 2 else 1 - par)
                    if n == 0 and not last:
                        if first:
                            pe.wait_ge(draw_free, 1)
                        else:
                            pe.wait_ge(z_free, NCH * g)
                        turn_xn(g + 1, 0)
                    if n in (1, 2, 3, 4) and not last:
                        project_x(g + 1, 1 - par, n - 1)
                    if n == 7 and not last:
                        x_ssm(g + 1)
                    if n == 11 and more:
                        pe.wait_ge(draw_free, g + 2)
                        turn_x(g + 2, par, 0)
                    if n == 12 and more:
                        turn_x(g + 2, par, 1)
                    if n == 13 and more:
                        embed(g + 2, 0)
                    if n == 14:
                        if more:
                            pe.wait_ge(emb_free, 2 * g + 6)
                        elif not last:
                            pe.wait_ge(draw_free, g + 2)
                        project_z(g, par, 2)
                    if b_due and not b_first:
                        b_all(g2_, n2, par if n2 >= 2 else 1 - par)
                    if n == 0 and not last:
                        turn_xn(g + 1, 1)
                    if n in (2, 3, 4, 5) and not first:
                        project_out(g - 1, (n - 2) // 2, n % 2)
                    if n == 6:
                        ahead(pe, h2_ready, 2 * g)
                        project_z(g, par, 0)
                    if n == 8 and not first:
                        pe.wait_ge(z_free, NCH * g + 1)
                        turn_row(g - 1, 0)
                    if n == 9 and not first:
                        turn_row(g - 1, 1)
                    if n == 10 and not first:
                        router(g - 1)
                    if n == 11:
                        if first:
                            pe.wait_ge(z_free, NCH * g + 1)
                        else:
                            pe.wait_ge(lsub_ready, g)
                        project_z(g, par, 1)
                    if n == 12 and not first:
                        pe.wait_ge(z_free, NCH * g + 2)
                        count(g - 1)
                    if n == 13 and more:
                        if first:
                            pe.wait_ge(z_free, 2)
                        else:
                            pe.wait_ge(slot_ready, g)
                        embed(g + 2, 1)
                    if n == 15:
                        if more:
                            pe.wait_ge(emb_free, 2 * g + 6)
                        elif first:
                            pe.wait_ge(z_free, 2)
                        else:
                            pe.wait_ge(slot_ready, g)
                        project_z(g, par, 3)
                    if n == 1:
                        skip(g, NCH // 2, NCH)
                    if not (last and n1 == 0):
                        c_all(g1, n1, par if n1 else 1 - par)
                    if n == 9 and not last:
                        delta_raw(g + 1, 1 - par)
                    add_state(g, n)
                    if n == 0:
                        skip(g, 0, NCH // 2)

            front(0, 0)
            b_all(0, 0, 0)
            c_all(0, 0, 0)
            b_all(0, 1, 0)
            pe.wait_ge(s_set, 6 + NCH + 1)
            step(0, 0, True, True, False)
            with pe.Fori(1, G - 3, 2) as g:
                step(g, 1, False, True, False)
                step(g + 1, 0, False, True, False)
            step(G - 3, 1, False, True, False)
            step(G - 2, 0, False, False, False)
            step(G - 1, 1, False, False, True)
            for m in range(2):
                for b in range(2):
                    project_out(G - 1, m, b)
            turn_row(G - 1, 0)
            turn_row(G - 1, 1)
            router(G - 1)
            count(G - 1)

            pe.wait_ge(tab_ready, 1)
            pe.wait_ge(w_loaded, 16 * 3 * E)

            def turn_tile(i, k):
                pe.wait_ge(tile_loaded[k], (16 * (i // XB + 1)) if isinstance(i, int) else (i - k) * (16 // XB) + 16)
                if not (isinstance(i, int) and i < 1):
                    pe.wait_ge(xgt_ready, i)
                for q in range(NK):
                    last = nc.tensor.transpose(px[:, q * P:(q + 1) * P], xg[k][:, q * P:(q + 1) * P], ident[:, :])
                last.then_inc(xg_turned, 1)

            def hidden(i, k, e, base, dst, done):
                for q in range(NK):
                    w = w_moe[:, bass.ds(e, 1), base + q * H:base + (q + 1) * H].rearrange("p a h -> p (a h)")
                    last = nc.tensor.matmul(dst[k % 2], xgt[k % 2][:, q * P:(q + 1) * P], w,
                                            start=(q == 0), stop=(q == NK - 1))
                last.then_inc(done, 1)

            def turn_act(i, k):
                pe.wait_ge(act_ready, i + 1)
                if not (isinstance(i, int) and i < 1):
                    pe.wait_ge(actt_ready, i)
                for q in range(NH):
                    last = nc.tensor.transpose(pt[:, q * P:(q + 1) * P], act[k % 2][:, q * P:(q + 1) * P], ident[:, :])
                last.then_inc(at_full, 1)

            def down(i, k, e):
                pe.wait_ge(actt_ready, i + 1)
                if not (isinstance(i, int) and i < 2):
                    pe.wait_ge(y_ready, i - 1)
                for q in range(NH):
                    w = w_moe[:, bass.ds(e, 1), 2 * NK * H + q * C:2 * NK * H + (q + 1) * C]\
                        .rearrange("p a h -> p (a h)")
                    last = nc.tensor.matmul(py[k % 2], actt[k % 2][:, q * P:(q + 1) * P], w,
                                            start=(q == 0), stop=(q == NH - 1))
                last.then_inc(y_full, 1)

            def expert(i):
                return pe.value_load(tab[0:1, 0, bass.ds(i, 1)], min_val=0, max_val=E - 1)

            def tiles(i, first, last):
                e = None
                for k in range(XB):
                    t = i + k
                    e_before = expert(t - 1) if k == 0 and not first else e if k else None
                    e = expert(t)
                    if not (last and k == XB - 1):
                        turn_tile(t + 1, (k + 1) % XB)
                    pe.wait_ge(xgt_ready, t + 1)
                    if not (isinstance(t, int) and t < 2):
                        pe.wait_ge(silu_ready, t - 1)
                    hidden(t, k, e, 0, pg, gate_full)
                    if not (first and k == 0):
                        turn_act(t - 1, (k - 1) % XB)
                    hidden(t, k, e, NK * H, pu, up_full)
                    if not (first and k == 0):
                        down(t - 1, (k - 1) % XB, e_before)

            turn_tile(0, 0)
            tiles(0, True, False)
            with pe.Fori(XB, NT - XB, XB) as i:
                tiles(i, False, False)
            tiles(NT - XB, False, True)
            turn_act(NT - 1, XB - 1)
            down(NT - 1, XB - 1, expert(NT - 1))
    return nc


_INS = ['x', 'L0_tok_W_embed', 'L0_tok_b_embed', 'L0_tok_W_proj', 'L0_tok_b_proj', 'L0_attn_W_in', 'L0_attn_conv_w',
        'L0_attn_conv_b', 'L0_attn_W_xproj', 'L0_attn_w_dt', 'L0_attn_b_dt', 'L0_attn_A_log', 'L0_attn_D_param',
        'L0_attn_W_out', 'L0_ffn_w_gate', 'L0_ffn_wi', 'L0_ffn_wg', 'L0_ffn_wo']
_OUT = (64, 128, 256)


def kernel(**inputs):
    import numpy as _np
    import concourse.bacc as _bacc
    from concourse import mybir as _mybir
    from concourse.bass_utils import run_bass_kernel_spmd as _run

    nc = _bacc.Bacc("TRN2", target_bir_lowering=False, num_devices=1)
    arrays, args = {}, []
    for name in _INS:
        a = _np.ascontiguousarray(inputs[name])
        arrays[f"in_{name}_dram"] = a
        args.append(nc.dram_tensor(f"in_{name}_dram", a.shape, _mybir.dt.from_np(a.dtype), kind="ExternalInput").ap())
    args.append(nc.dram_tensor("out_0_dram", _OUT, _mybir.dt.from_np(_np.dtype("float32")), kind="ExternalOutput").ap())
    audio_tower(nc, *args)
    r = _run(nc, [arrays], core_ids=[0])
    return r.results[0]["out_0_dram"]
```
